# Optimizing a Trainium2 kernel written in Bass

```python
import numpy as np
import jax
import jax.numpy as jnp

def _softmax(x, axis=-1):
    return jax.nn.softmax(x, axis=axis)

def _gelu(x):
    return jax.nn.gelu(x, approximate=True)

def _silu(x):
    return jax.nn.silu(x)

def _sigmoid(x):
    return jax.nn.sigmoid(x)

def _layernorm(x, axis=-1, eps=1e-05):
    m = jnp.mean(x, axis=axis, keepdims=True)
    v = jnp.var(x, axis=axis, keepdims=True)
    return (x - m) / jnp.sqrt(v + eps)

def _scatter_add(tgt, idx, src, axis=0):
    return tgt.at[idx].add(src)

def _segment_sum(src, seg, n):
    return jax.ops.segment_sum(src, seg, n)
kernel_name = 'mk_flamingo_gated_d4_seqx_r4_e1ae16'

def setup_inputs(seed: int=0):
    np.random.seed(seed)
    _w = jnp.asarray

    def _rec_inputs():
        import jax
        import jax.numpy as jnp
        _rk = jax.random.key(seed)
        x = 0.0002417 + 0.9998 * jax.random.normal(jax.random.fold_in(_rk, 1), (8, 256, 256), jnp.float32)
        _lenS = 256 - jax.random.randint(jax.random.fold_in(_rk, 7), (8,), 0, max(1, 256 // 4) + 1, jnp.int32)
        _lenS2 = 77 - jax.random.randint(jax.random.fold_in(_rk, 8), (8,), 0, max(1, 77 // 4) + 1, jnp.int32)
        _ctx_1024P = jax.random.normal(jax.random.fold_in(_rk, 11), (8, 16, 256), jnp.float32)
        _ctx_1024c = jax.random.dirichlet(jax.random.fold_in(_rk, 511), 0.3 * jnp.ones((16,), jnp.float32), (8, 77))
        _ctx_1024t = jnp.einsum('bsk,bkd->bsd', _ctx_1024c, _ctx_1024P)
        _ctx_1024t = _ctx_1024t * jax.lax.rsqrt(jnp.mean(jnp.square(_ctx_1024t)) + 1e-12) * 0.953939
        ctx_1024 = 7.22013e-05 + 1.00017 * (_ctx_1024t + 0.3 * jax.random.normal(jax.random.fold_in(_rk, 611), (8, 77, 256), jnp.float32))
        _validS = jnp.arange(256)[None, :] < _lenS[:, None]
        _validS2 = jnp.arange(77)[None, :] < _lenS2[:, None]
        _causal = jnp.tril(jnp.ones((256, 256), dtype=bool))
        mask_BxS2_bf1 = jnp.ones((8, 77), dtype=bool)
        _g = jax.random.normal(jax.random.fold_in(_rk, 9001), (2, 4), jnp.float32)
        _g = jnp.sign(_g) * jnp.maximum(jnp.abs(_g), 1.0) + (_g == 0) * 1.0
        g_xattn = _g[0]
        g_ffn = _g[1]
        return (x, ctx_1024, mask_BxS2_bf1, g_xattn, g_ffn)
    x, ctx_1024, mask_BxS2_bf1, g_xattn, g_ffn = _rec_inputs()

    def _L0_xattn_setup():
        import jax, jax.numpy as jnp
        import numpy as np
        EMBED = 256
        HEADS = 16
        HEAD_DIM = EMBED // HEADS
        EXP_DIM = 2 * HEAD_DIM

        def _feature_map(x, fm_w, fm_b):
            z = jnp.einsum('nshd,ed->nshe', x, fm_w) + fm_b
            return jnp.concatenate([jnp.exp(z), jnp.exp(-z)], axis=-1)
        key = jax.random.key(seed)
        ks = jax.random.split(key, 7)
        N, S = (4, 512)
        values = jax.random.normal(ks[0], (N, S, EMBED), dtype=jnp.float32)
        keys_ = jax.random.normal(ks[1], (N, S, EMBED), dtype=jnp.float32)
        query = jax.random.normal(ks[2], (N, S, EMBED), dtype=jnp.float32)
        fm_w = jnp.eye(HEAD_DIM, dtype=jnp.float32) + 0.02 * jax.random.normal(ks[3], (HEAD_DIM, HEAD_DIM), dtype=jnp.float32)
        fm_b = 0.02 * jax.random.normal(ks[4], (HEAD_DIM,), dtype=jnp.float32)
        fc_w = jax.random.normal(ks[5], (EMBED, HEADS * EXP_DIM), dtype=jnp.float32) * (1.0 / np.sqrt(HEADS * EXP_DIM))
        fc_b = jnp.zeros((EMBED,), dtype=jnp.float32)
        return {'values': values, 'keys': keys_, 'query': query, 'fm_w': fm_w, 'fm_b': fm_b, 'fc_w': fc_w, 'fc_b': fc_b}
    _L0_xattn_all = _L0_xattn_setup()
    _L0_xattn_in = {k: v for k, v in _L0_xattn_all.items() if k in ('fm_w', 'fm_b', 'fc_w', 'fc_b')}
    del _L0_xattn_all

    def _L0_ffn_setup():
        import jax, jax.numpy as jnp
        import numpy as np
        key = jax.random.key(seed)
        kx, kw = jax.random.split(key)
        x = jax.random.normal(kx, (32, 1024, 256), dtype=jnp.float32)
        weight = jax.random.normal(kw, (256, 256), dtype=jnp.float32) * 0.01
        return {'x': x, 'weight': weight}
    _L0_ffn_all = _L0_ffn_setup()
    _L0_ffn_in = {k: v for k, v in _L0_ffn_all.items() if k in ('weight',)}
    del _L0_ffn_all

    def _L1_xattn_setup():
        import jax, jax.numpy as jnp
        import numpy as np
        B, LQ, LK = (4, 512, 512)
        DQ, DK, DO = (256, 256, 256)
        key = jax.random.key(seed)
        ks = jax.random.split(key, 9)
        s = 0.02
        return {'query_input': jax.random.normal(ks[0], (B, LQ, DQ), jnp.float32), 'key_input': jax.random.normal(ks[1], (B, LK, DK), jnp.float32), 'value_input': jax.random.normal(ks[2], (B, LK, DK), jnp.float32), 'Wq': jax.random.normal(ks[3], (DQ, DO), jnp.float32) * s, 'bq': jax.random.normal(ks[4], (DO,), jnp.float32) * s, 'Wk': jax.random.normal(ks[5], (DK, DO), jnp.float32) * s, 'bk': jax.random.normal(ks[6], (DO,), jnp.float32) * s, 'Wv': jax.random.normal(ks[7], (DK, DO), jnp.float32) * s, 'bv': jax.random.normal(ks[8], (DO,), jnp.float32) * s}
    _L1_xattn_all = _L1_xattn_setup()
    _L1_xattn_in = {k: v for k, v in _L1_xattn_all.items() if k in ('Wq', 'bq', 'Wk', 'bk', 'Wv', 'bv')}
    del _L1_xattn_all

    def _L1_ffn_setup():
        import jax, jax.numpy as jnp
        import numpy as np
        QB = 127.0
        EPS = 1e-05

        def _ste(x, q):
            return x + jax.lax.stop_gradient(q - x)

        def bitlinear(x, W, b):
            w_scale = jnp.clip(jnp.mean(jnp.abs(W)), EPS, None)
            Wq = _ste(W, jnp.clip(jnp.round(W / w_scale), -1.0, 1.0) * w_scale)
            x_scale = jnp.clip(jnp.max(jnp.abs(x), axis=-1, keepdims=True), EPS, None)
            xq = _ste(x, jnp.clip(jnp.round(x * (QB / x_scale)), -QB - 1.0, QB) * (x_scale / QB))
            return jnp.einsum('bnd,hd->bnh', xq, Wq) + b
        key = jax.random.key(seed)
        k0, k1, k2 = jax.random.split(key, 3)
        B, N, D = (8, 1024, 256)
        H = int(D * 4.0)
        x = jax.random.normal(k0, (B, N, D), dtype=jnp.float32)
        W1 = jax.random.normal(k1, (H, D), dtype=jnp.float32) * 0.02
        b1 = jnp.zeros((H,), dtype=jnp.float32)
        W2 = jax.random.normal(k2, (D, H), dtype=jnp.float32) * 0.02
        b2 = jnp.zeros((D,), dtype=jnp.float32)
        return {'x': x, 'W1': W1, 'b1': b1, 'W2': W2, 'b2': b2}
    _L1_ffn_all = _L1_ffn_setup()
    _L1_ffn_in = {k: v for k, v in _L1_ffn_all.items() if k in ('W1', 'b1', 'W2', 'b2')}
    del _L1_ffn_all

    def _L2_xattn_setup():
        import jax, jax.numpy as jnp
        import numpy as np
        B, N, HID, HEADS, TOPK = (2, 512, 256, 16, 64)
        DHEAD = HID // HEADS

        def _split_heads(x):
            b, n, _ = x.shape
            return x.reshape(b, n, HEADS, DHEAD).transpose(0, 2, 1, 3)
        key = jax.random.key(seed)
        ks = jax.random.split(key, 12)
        s = 1.0 / np.sqrt(HID)
        inp = {'q': jax.random.normal(ks[0], (B, N, HID), jnp.float32), 'k': jax.random.normal(ks[1], (B, N, HID), jnp.float32), 'v': jax.random.normal(ks[2], (B, N, HID), jnp.float32), 'mask': jnp.ones((B, N), jnp.bool_), 'topk': TOPK, 'wq_w': jax.random.normal(ks[3], (HID, HID), jnp.float32) * s, 'wq_b': jnp.zeros((HID,), jnp.float32), 'wk_w': jax.random.normal(ks[4], (HID, HID), jnp.float32) * s, 'wk_b': jnp.zeros((HID,), jnp.float32), 'wv_w': jax.random.normal(ks[5], (HID, HID), jnp.float32) * s, 'wv_b': jnp.zeros((HID,), jnp.float32), 'wo_w': jax.random.normal(ks[6], (HID, HID), jnp.float32) * s, 'wo_b': jnp.zeros((HID,), jnp.float32)}
        return inp
    _L2_xattn_all = _L2_xattn_setup()
    _L2_xattn_in = {k: v for k, v in _L2_xattn_all.items() if k in ('wq_w', 'wq_b', 'wk_w', 'wk_b', 'wv_w', 'wv_b', 'wo_w', 'wo_b')}
    del _L2_xattn_all

    def _L2_ffn_setup():
        import jax, jax.numpy as jnp
        import numpy as np
        HID, FFN, E, K = (256, 1024, 8, 2)
        CAP_FACTOR = 1.25
        key = jax.random.key(seed)
        k1, k2, k3, k4 = jax.random.split(key, 4)
        B, T = (4, 512)
        x = jax.random.normal(k1, (B, T, HID), dtype=jnp.float32)
        router_w = jax.random.normal(k2, (E, HID), dtype=jnp.float32) * 0.02
        w1 = jax.random.normal(k3, (E, HID, FFN), dtype=jnp.float32) * 0.02
        w2 = jax.random.normal(k4, (E, FFN, HID), dtype=jnp.float32) * 0.02
        return {'x': x, 'router_w': router_w, 'w1': w1, 'w2': w2}
    _L2_ffn_all = _L2_ffn_setup()
    _L2_ffn_in = {k: v for k, v in _L2_ffn_all.items() if k in ('router_w', 'w1', 'w2')}
    del _L2_ffn_all

    def _L3_xattn_setup():
        import jax, jax.numpy as jnp
        import numpy as np
        B, R, U, D = (16, 512, 512, 256)
        EPS_ATT = 1e-08
        EPS_LN = 1e-06
        key = jax.random.key(seed)
        ks = jax.random.split(key, 6)
        s = 1.0 / np.sqrt(D)
        return {'Q': jax.random.normal(ks[0], (B, R, D), dtype=jnp.float32), 'K': jax.random.normal(ks[1], (B, U, D), dtype=jnp.float32), 'V': jax.random.normal(ks[2], (B, U, D), dtype=jnp.float32), 'W1': jax.random.normal(ks[3], (D, D), dtype=jnp.float32) * s, 'b1': jnp.zeros((D,), dtype=jnp.float32), 'W2': jax.random.normal(ks[4], (D, D), dtype=jnp.float32) * s, 'b2': jnp.zeros((D,), dtype=jnp.float32), 'gamma': jnp.ones((D,), dtype=jnp.float32), 'beta': jnp.zeros((D,), dtype=jnp.float32)}
    _L3_xattn_all = _L3_xattn_setup()
    _L3_xattn_in = {k: v for k, v in _L3_xattn_all.items() if k in ('W1', 'b1', 'W2', 'b2', 'gamma', 'beta')}
    del _L3_xattn_all

    def _L3_ffn_setup():
        import jax, jax.numpy as jnp
        import numpy as np
        MAX_VAL = 100.0
        key = jax.random.key(seed)
        k1, k2, k3 = jax.random.split(key, 3)
        B, S, D_IN, D_OUT = (4, 2048, 256, 256)
        x = jax.random.normal(k1, (B, S, D_IN), dtype=jnp.float32)
        weights = jax.random.normal(k2, (D_OUT, D_IN), dtype=jnp.float32)
        scale = jnp.ones((D_OUT,), dtype=jnp.float32)
        bias = jax.random.normal(k3, (D_OUT,), dtype=jnp.float32)
        return {'x': x, 'weights': weights, 'scale': scale, 'bias': bias}
    _L3_ffn_all = _L3_ffn_setup()
    _L3_ffn_in = {k: v for k, v in _L3_ffn_all.items() if k in ('weights', 'scale', 'bias')}
    del _L3_ffn_all
    return {'x': x, 'ctx_1024': ctx_1024, 'mask_BxS2_bf1': mask_BxS2_bf1, 'g_xattn': g_xattn, 'g_ffn': g_ffn, 'L0_xattn_fm_w': _L0_xattn_in['fm_w'], 'L0_xattn_fm_b': _L0_xattn_in['fm_b'], 'L0_xattn_fc_w': _L0_xattn_in['fc_w'], 'L0_xattn_fc_b': _L0_xattn_in['fc_b'], 'L0_ffn_weight': _L0_ffn_in['weight'], 'L1_xattn_Wq': _L1_xattn_in['Wq'], 'L1_xattn_bq': _L1_xattn_in['bq'], 'L1_xattn_Wk': _L1_xattn_in['Wk'], 'L1_xattn_bk': _L1_xattn_in['bk'], 'L1_xattn_Wv': _L1_xattn_in['Wv'], 'L1_xattn_bv': _L1_xattn_in['bv'], 'L1_ffn_W1': _L1_ffn_in['W1'], 'L1_ffn_b1': _L1_ffn_in['b1'], 'L1_ffn_W2': _L1_ffn_in['W2'], 'L1_ffn_b2': _L1_ffn_in['b2'], 'L2_xattn_wq_w': _L2_xattn_in['wq_w'], 'L2_xattn_wq_b': _L2_xattn_in['wq_b'], 'L2_xattn_wk_w': _L2_xattn_in['wk_w'], 'L2_xattn_wk_b': _L2_xattn_in['wk_b'], 'L2_xattn_wv_w': _L2_xattn_in['wv_w'], 'L2_xattn_wv_b': _L2_xattn_in['wv_b'], 'L2_xattn_wo_w': _L2_xattn_in['wo_w'], 'L2_xattn_wo_b': _L2_xattn_in['wo_b'], 'L2_ffn_router_w': _L2_ffn_in['router_w'], 'L2_ffn_w1': _L2_ffn_in['w1'], 'L2_ffn_w2': _L2_ffn_in['w2'], 'L3_xattn_W1': _L3_xattn_in['W1'], 'L3_xattn_b1': _L3_xattn_in['b1'], 'L3_xattn_W2': _L3_xattn_in['W2'], 'L3_xattn_b2': _L3_xattn_in['b2'], 'L3_xattn_gamma': _L3_xattn_in['gamma'], 'L3_xattn_beta': _L3_xattn_in['beta'], 'L3_ffn_weights': _L3_ffn_in['weights'], 'L3_ffn_scale': _L3_ffn_in['scale'], 'L3_ffn_bias': _L3_ffn_in['bias']}

def reference(x, ctx_1024, mask_BxS2_bf1, g_xattn, g_ffn, L0_xattn_fm_w, L0_xattn_fm_b, L0_xattn_fc_w, L0_xattn_fc_b, L0_ffn_weight, L1_xattn_Wq, L1_xattn_bq, L1_xattn_Wk, L1_xattn_bk, L1_xattn_Wv, L1_xattn_bv, L1_ffn_W1, L1_ffn_b1, L1_ffn_W2, L1_ffn_b2, L2_xattn_wq_w, L2_xattn_wq_b, L2_xattn_wk_w, L2_xattn_wk_b, L2_xattn_wv_w, L2_xattn_wv_b, L2_xattn_wo_w, L2_xattn_wo_b, L2_ffn_router_w, L2_ffn_w1, L2_ffn_w2, L3_xattn_W1, L3_xattn_b1, L3_xattn_W2, L3_xattn_b2, L3_xattn_gamma, L3_xattn_beta, L3_ffn_weights, L3_ffn_scale, L3_ffn_bias):
    import jax
    import jax.numpy as jnp

    def _L0_xattn_ref(values, keys, query, fm_w, fm_b, fc_w, fc_b):
        import jax, jax.numpy as jnp
        import numpy as np
        EMBED = 256
        HEADS = 16
        HEAD_DIM = EMBED // HEADS
        EXP_DIM = 2 * HEAD_DIM

        def _feature_map(x, fm_w, fm_b):
            z = jnp.einsum('nshd,ed->nshe', x, fm_w) + fm_b
            return jnp.concatenate([jnp.exp(z), jnp.exp(-z)], axis=-1)
        N, S, _ = query.shape
        v = values.reshape(N, -1, HEADS, HEAD_DIM)
        k = keys.reshape(N, -1, HEADS, HEAD_DIM)
        q = query.reshape(N, -1, HEADS, HEAD_DIM)
        v, k, q = (_feature_map(x, fm_w, fm_b) for x in (v, k, q))
        scores = jnp.einsum('nqhd,nkhd->nhqk', q, k) / jnp.sqrt(jnp.float32(EMBED))
        attn = jax.nn.softmax(scores, axis=-1)
        out = jnp.einsum('nhql,nlhd->nqhd', attn, v)
        out = out.reshape(N, S, HEADS * EXP_DIM)
        return out @ fc_w.T + fc_b

    def _L0_ffn_ref(x, weight):
        import jax, jax.numpy as jnp
        import numpy as np
        b_weight = jnp.sign(weight)
        return jnp.einsum('bsi,oi->bso', x, b_weight)

    def _L1_xattn_ref(query_input, key_input, value_input, Wq, bq, Wk, bk, Wv, bv):
        import jax, jax.numpy as jnp
        import numpy as np
        B, LQ, LK = (4, 512, 512)
        DQ, DK, DO = (256, 256, 256)
        scale = jnp.asarray(DO, query_input.dtype) ** 0.5
        q = query_input @ Wq + bq
        k = key_input @ Wk + bk
        v = value_input @ Wv + bv
        attn = jnp.einsum('bqd,bkd->bqk', q, k) / scale
        attn = jax.nn.softmax(attn, axis=-1)
        return jnp.einsum('bqk,bkd->bqd', attn, v)

    def _L1_ffn_ref(x, W1, b1, W2, b2):
        import jax, jax.numpy as jnp
        import numpy as np
        QB = 127.0
        EPS = 1e-05

        def _ste(x, q):
            return x + jax.lax.stop_gradient(q - x)

        def bitlinear(x, W, b):
            w_scale = jnp.clip(jnp.mean(jnp.abs(W)), EPS, None)
            Wq = _ste(W, jnp.clip(jnp.round(W / w_scale), -1.0, 1.0) * w_scale)
            x_scale = jnp.clip(jnp.max(jnp.abs(x), axis=-1, keepdims=True), EPS, None)
            xq = _ste(x, jnp.clip(jnp.round(x * (QB / x_scale)), -QB - 1.0, QB) * (x_scale / QB))
            return jnp.einsum('bnd,hd->bnh', xq, Wq) + b
        h = bitlinear(x, W1, b1)
        h = jax.nn.gelu(h, approximate=False)
        return bitlinear(h, W2, b2)

    def _L2_xattn_ref(q, k, v, mask, topk, wq_w, wq_b, wk_w, wk_b, wv_w, wv_b, wo_w, wo_b):
        import jax, jax.numpy as jnp
        import numpy as np
        B, N, HID, HEADS, TOPK = (2, 512, 256, 16, 64)
        DHEAD = HID // HEADS

        def _split_heads(x):
            b, n, _ = x.shape
            return x.reshape(b, n, HEADS, DHEAD).transpose(0, 2, 1, 3)
        qh = _split_heads(q @ wq_w.T + wq_b)
        kh = _split_heads(k @ wk_w.T + wk_b)
        vh = _split_heads(v @ wv_w.T + wv_b)
        scores = jnp.einsum('bhqd,bhkd->bhqk', qh, kh) / np.sqrt(DHEAD)
        neg = jnp.finfo(scores.dtype).min
        scores = jnp.where(mask[:, None, None, :], scores, neg)
        if topk and 0 < topk < scores.shape[-1]:
            vals, idx = jax.lax.top_k(scores, topk)
            b, h, nq, _ = scores.shape
            bI = jnp.arange(b)[:, None, None, None]
            hI = jnp.arange(h)[None, :, None, None]
            qI = jnp.arange(nq)[None, None, :, None]
            scores = jnp.full_like(scores, neg).at[bI, hI, qI, idx].set(vals)
        probs = jax.nn.softmax(scores, axis=-1)
        ctx = jnp.einsum('bhqk,bhkd->bhqd', probs, vh)
        ctx = ctx.transpose(0, 2, 1, 3).reshape(q.shape[0], q.shape[1], HID)
        return ctx @ wo_w.T + wo_b

    def _L2_ffn_ref(x, router_w, w1, w2):
        import jax, jax.numpy as jnp
        import numpy as np
        HID, FFN, E, K = (256, 1024, 8, 2)
        CAP_FACTOR = 1.25
        B, T, H = x.shape
        N = B * T
        x_flat = x.reshape(N, H)
        C = max(1, int(CAP_FACTOR * N / E * K))
        logits = x_flat @ router_w.T
        probs = jax.nn.softmax(logits, axis=-1)
        top_v, top_i = jax.lax.top_k(probs, K)
        top_v = top_v / jnp.sum(top_v, axis=-1, keepdims=True)
        out = jnp.zeros_like(x_flat)
        for k in range(K):
            eid = top_i[:, k]
            gate = top_v[:, k]
            onehot = jax.nn.one_hot(eid, E, dtype=jnp.int32)
            pos = jnp.take_along_axis(jnp.cumsum(onehot, axis=0), eid[:, None], axis=1)[:, 0] - 1
            keep = pos < C
            slot = jnp.where(keep, eid * C + pos, E * C)
            buf = jnp.zeros((E * C + 1, H), dtype=x.dtype).at[slot].add(x_flat * keep[:, None].astype(x.dtype))
            expert_in = buf[:E * C].reshape(E, C, H)
            h = jax.nn.gelu(jnp.einsum('ech,ehf->ecf', expert_in, w1), approximate=False)
            y = jnp.einsum('ecf,efh->ech', h, w2)
            tok = y.reshape(E * C, H)[jnp.minimum(slot, E * C - 1)]
            out = out + tok * (gate * keep.astype(x.dtype))[:, None]
        return out.reshape(B, T, H)

    def _L3_xattn_ref(Q, K, V, W1, b1, W2, b2, gamma, beta):
        import jax, jax.numpy as jnp
        import numpy as np
        B, R, U, D = (16, 512, 512, 256)
        EPS_ATT = 1e-08
        EPS_LN = 1e-06
        d_model = Q.shape[-1]
        scale = jnp.sqrt(jnp.asarray(d_model, jnp.float32) + EPS_ATT)
        scores = jnp.einsum('brd,bud->bru', Q, K) / scale
        att = jax.nn.softmax(scores, axis=-1)
        V_att = jnp.einsum('bru,bud->brd', att, V)

        def layer_norm(x):
            mu = jnp.mean(x, axis=-1, keepdims=True)
            var = jnp.mean(jnp.square(x - mu), axis=-1, keepdims=True)
            return gamma * (x - mu) / jnp.sqrt(var + EPS_LN) + beta
        X = layer_norm(Q + V_att)
        ffn = jnp.maximum(X @ W1 + b1, 0.0) @ W2 + b2
        return layer_norm(ffn + X)

    def _L3_ffn_ref(x, weights, scale, bias):
        import jax, jax.numpy as jnp
        import numpy as np
        MAX_VAL = 100.0
        w = (weights >= 0.0).astype(x.dtype) * 2.0 - 1.0
        y = jnp.einsum('bsi,oi->bso', x, w)
        y = y * scale + bias
        y = jnp.clip(y, -MAX_VAL, MAX_VAL)
        return y
    x = x + jnp.tanh(g_xattn[0]) * _L0_xattn_ref(ctx_1024, ctx_1024, _layernorm(x, axis=-1), L0_xattn_fm_w, L0_xattn_fm_b, L0_xattn_fc_w, L0_xattn_fc_b)
    x = x + jnp.tanh(g_ffn[0]) * _L0_ffn_ref(_layernorm(x, axis=-1), L0_ffn_weight)
    x = x + jnp.tanh(g_xattn[1]) * _L1_xattn_ref(_layernorm(x, axis=-1), ctx_1024, ctx_1024, L1_xattn_Wq, L1_xattn_bq, L1_xattn_Wk, L1_xattn_bk, L1_xattn_Wv, L1_xattn_bv)
    x = x + jnp.tanh(g_ffn[1]) * _L1_ffn_ref(_layernorm(x, axis=-1), L1_ffn_W1, L1_ffn_b1, L1_ffn_W2, L1_ffn_b2)
    x = x + jnp.tanh(g_xattn[2]) * _L2_xattn_ref(_layernorm(x, axis=-1), ctx_1024, ctx_1024, mask_BxS2_bf1, 64, L2_xattn_wq_w, L2_xattn_wq_b, L2_xattn_wk_w, L2_xattn_wk_b, L2_xattn_wv_w, L2_xattn_wv_b, L2_xattn_wo_w, L2_xattn_wo_b)
    x = x + jnp.tanh(g_ffn[2]) * _L2_ffn_ref(_layernorm(x, axis=-1), L2_ffn_router_w, L2_ffn_w1, L2_ffn_w2)
    x = x + jnp.tanh(g_xattn[3]) * _L3_xattn_ref(_layernorm(x, axis=-1), ctx_1024, ctx_1024, L3_xattn_W1, L3_xattn_b1, L3_xattn_W2, L3_xattn_b2, L3_xattn_gamma, L3_xattn_beta)
    x = x + jnp.tanh(g_ffn[3]) * _L3_ffn_ref(_layernorm(x, axis=-1), L3_ffn_weights, L3_ffn_scale, L3_ffn_bias)
    return x

_drawn_inputs = setup_inputs


def setup_inputs(seed=0):
    import zlib

    import numpy as np

    out = dict(_drawn_inputs(seed))
    spreads = {'L0_xattn_fc_b': (0.0, 0.491),
     'L1_ffn_b1': (0.0, 0.8),
     'L1_ffn_b2': (0.0, 0.8),
     'L2_xattn_wq_b': (0.0, 0.8),
     'L2_xattn_wk_b': (0.0, 2.0),
     'L2_xattn_wv_b': (0.0, 0.8),
     'L2_xattn_wo_b': (0.0, 0.8),
     'L3_xattn_b1': (0.0, 2.0),
     'L3_xattn_b2': (0.0, 2.0),
     'L3_xattn_gamma': (1.0, 0.558),
     'L3_xattn_beta': (0.0, 0.598),
     'L3_ffn_scale': (1.0, 0.2)}
    factors = {'L1_xattn_Wq': 8.0,
     'L1_xattn_bq': 8.0,
     'L1_xattn_Wk': 8.0,
     'L1_xattn_bk': 200.0,
     'L1_xattn_Wv': 4.034,
     'L1_xattn_bv': 8.0,
     'L1_ffn_W1': 8.0,
     'L1_ffn_W2': 8.0,
     'L2_xattn_wq_w': 3.452,
     'L2_xattn_wk_w': 3.411,
     'L2_ffn_router_w': 8.0,
     'L2_ffn_w1': 8.0,
     'L2_ffn_w2': 8.0}
    for name, (base, spread) in spreads.items():
        noise = np.random.default_rng([zlib.crc32(name.encode()), seed]).standard_normal(out[name].shape)
        drawn = base * np.exp(spread * noise) if base else spread * noise
        out[name] = jnp.asarray(drawn.astype(out[name].dtype))
    for name, factor in factors.items():
        out[name] = (out[name] * factor).astype(out[name].dtype)
    return out
```

```python
B, S, D = 8, 256, 256
P = 128
CH = D // P
TT = B * S // P
TB = S // P
KEYS = 77
NK = B * KEYS
HALF = NK // 2
HEADS = 16
HG = 4
GR = HEADS // HG
GK = HG * KEYS
FF = 4 * D
E = 8
CAP = int(1.25 * B * S / E * 2)
DROP = KEYS - 64
MT = B * S * 2 // P + E - 1
PAIRS = B // 2
ITEMS = 2 * GR
BIG = 1e38
MAGIC = 12582912.0
QB = 127.0
EPS_Q = 1e-5


def build(nc, a, out, phases=8):
    from concourse import mybir
    import concourse.bass as bass
    from contextlib import ExitStack

    f32, bf16, i32, u32, u8 = (mybir.dt.float32, mybir.dt.bfloat16, mybir.dt.int32,
                               mybir.dt.uint32, mybir.dt.uint8)
    ALU = mybir.AluOpType
    ACT = mybir.ActivationFunctionType
    AX = mybir.AxisListType
    ctx = ExitStack()
    with ctx:
        def sb(name, shape, dt=f32):
            return ctx.enter_context(nc.sbuf_tensor(name, shape, dt))

        def sem(name):
            return ctx.enter_context(nc.semaphore(name))

        seeds = []

        def counted(name):
            s = sem(name)
            seeds.append(s)
            return Share(s, 0)

        class Share:

            def __init__(self, s, base):
                self.sem, self.base = s, base

            def past(self, n):
                return n + (self.base + 1)

        def shared(name, per_phase):
            s, base, out = counted(name).sem, 0, {}
            for n, k in per_phase.items():
                out[n] = Share(s, base)
                base += k
            return out

        class Chain:

            def __init__(self, eng, s, base=0):
                self.eng, self.s, self.base, self.n = eng, s, base, 0

            def step(self, ins):
                self.n += 1
                ins.then_inc(self.s.sem, 1)

            def settle(self):
                self.eng.wait_ge(self.s.sem, self.s.past(self.base + self.n))

            def link(self, ins):
                self.step(ins)
                self.settle()

        def apart(eng):
            eng.sem_inc(s_apart, 1)

        x = sb("x", [P, TT, D])
        xkeep = sb("xkeep", [P, TT, D])
        experts = sb("experts", [P, 2 * E * CH * FF])
        EW = CH * FF
        EARLY = 5
        arena_at = [EARLY * EW]

        def arena(n, parts=P):
            at = arena_at[0]
            arena_at[0] += n
            assert arena_at[0] <= 2 * E * EW
            return experts[0:parts, at:at + n]

        fcw = arena(4 * D).rearrange("p (c n) -> p c n", c=4)
        sgw = arena(CH * D).rearrange("p (c n) -> p c n", c=CH)
        w1q = arena(CH * D).rearrange("p (c n) -> p c n", c=CH)
        w1k = arena(CH * D).rearrange("p (c n) -> p c n", c=CH)
        w1v = arena(CH * D).rearrange("p (c n) -> p c n", c=CH)
        w2q = arena(CH * D).rearrange("p (c n) -> p c n", c=CH)
        w2k = arena(CH * D).rearrange("p (c n) -> p c n", c=CH)
        w2v = arena(CH * D).rearrange("p (c n) -> p c n", c=CH)
        w2o = arena(GR * D, 64).rearrange("p (c n) -> p c n", c=GR)
        tern1 = arena(EW // 2).bitcast(bf16).rearrange("p (c n) -> p c n", c=CH)
        tern2 = arena(EW // 2).bitcast(bf16).rearrange("p (c n) -> p c n", c=FF // P)
        kall = arena(GR * NK).rearrange("p (g n) -> p g n", g=GR)
        vall = arena(B * HEADS * 33, KEYS)
        kb = [arena(GR * GK).rearrange("p (g n) -> p g n", g=GR) for _ in range(2)]
        pr = [arena(TB * GK).rearrange("p (t n) -> p t n", t=TB) for _ in range(2)]
        dd = [arena(TB * GK).rearrange("p (t n) -> p t n", t=TB) for _ in range(2)]
        fmw = arena(2 * P).rearrange("p (g n) -> p g n", g=2)
        b1bc = arena(FF)
        b2bc = arena(D)
        osb = [arena(TB * P).rearrange("p (t n) -> p t n", t=TB) for _ in range(2)]
        xkeep_tmp = vall_tmp = kall[:, :, :].rearrange("p g n -> p (g n)")
        vtmp = xkeep_tmp[:, 0:EW]
        kb0, kb1 = (k[:, :, :].rearrange("p g n -> p (g n)") for k in kb)
        xq = [k[:, 0:S].bitcast(bf16).rearrange("p (t d) -> p t d", t=TB) for k in (kb0, kb1)]
        hq = [k[:, S:S + FF // 2].bitcast(bf16) for k in (kb0, kb1)]
        stage1 = xkeep[:, 0:8, :].rearrange("p t d -> p (t d)")
        stage2 = xkeep[:, 8:16, :].rearrange("p t d -> p (t d)")

        ident = sb("ident", [P, P])
        identb = sb("identb", [P, P], bf16)
        ones = sb("ones", [P, P])
        ctxT = sb("ctxT", [P, CH, NK])
        ctxn = sb("ctxn", [KEYS, B, D])
        xn = [sb(f"xn{i}", [P, TB, D]) for i in range(2)]
        xnT = [sb(f"xnT{i}", [P, CH, S]) for i in range(2)]
        wk = [sb(f"wk{i}", [P, 4, S]) for i in range(2)]
        pt = [sb(f"pt{i}", [KEYS, HG * S]) for i in range(2)]
        oT = wk
        rows = sb("rows", [1, 5, D])
        cols = sb("cols", [P, 16])
        gates = sb("gates", [P, 2 * 4])
        graw = sb("graw", [P, 2 * 4])
        st = [sb(f"st{i}", [P, TB, 6]) for i in range(2)]
        mv = [sb(f"mv{i}", [P, TB, 2]) for i in range(2)]
        rs = [sb(f"rs{i}", [P, TB]) for i in range(2)]
        mhalf = sb("mhalf", [P, TB])
        sm = sb("sm", [P, 2, 4, 8])
        m8 = [sb(f"m8{i}", [P, 8, 8]) for i in range(2)]
        m8b = [sb(f"m8b{i}", [P, 8, 8]) for i in range(2)]
        rden = [sb(f"rden{i}", [P, 8]) for i in range(2)]
        mx = [sb(f"mx{i}", [P, 8]) for i in range(2)]
        hsel = sb("hsel", [P, 4 + 8])
        mrow8 = sb("mrow8", [P, NK], u8)
        mrow = arena(NK)
        mcol = sb("mcol", [P, B])
        wstat = sb("wstat", [P, 8])
        w3a, w3b, w3f = (xkeep[:, 2 * k:2 * k + 2, :] for k in range(3))
        bc3 = xkeep[:, 6:10, :]
        rwT = sb("rwT", [P, CH, E])
        lg = [sb(f"lg{i}", [P, TB, E]) for i in range(2)]
        ix = [sb(f"ix{i}", [P, TB, 8], u32) for i in range(2)]
        topv = sb("topv", [P, TT, 2])
        topi = sb("topi", [P, TT, 2])
        lower = sb("lower", [P, P])
        iota = sb("iota", [P, 64])
        gate2 = sb("gate2", [P, TT, 2])
        slot = sb("slot", [P, 2, TT], i32)
        eid = sb("eid", [P, 64], i32)
        zeros = arena(D)
        xsb = [xn[0][:, 0, :], xn[0][:, 1, :], xn[1][:, 0, :]]
        xTb = [v.rearrange("p (c s) -> p c s", c=CH) for v in (xnT[0][:, 0, :], xnT[0][:, 1, :], xnT[1][:, 0, :])]
        hid = wk[0]
        hidT = wk[1][:, :, :].rearrange("p c s -> p (c s)")
        ysb = [xkeep[:, 10 + u, :] for u in range(3)]
        got = experts[:, 0:2 * TT * D].rearrange("p (k t d) -> p k t d", k=2, t=TT)
        rt = experts[:, E * EW:E * EW + 4096]
        ps = [ctx.enter_context(nc.psum_tensor(f"ps{i}", [P, 2, 512], f32)) for i in range(4)]

        def bank(i):
            return ps[i // 2][:, i % 2, :]

        xs_d = nc.dram_tensor("expert_in", [MT * P, D], f32).ap()
        ys_d = nc.dram_tensor("expert_out", [MT * P, D], f32).ap()

        L = (0, 1, 2, 3, 4, 5, 6, 7, 8)
        SC = B * GR
        NORMS = (0, 1, 2, 3, 4, 5, 7, 8)
        s_x = sem("s_x")
        s_ctx = sem("s_ctx")
        s_cst = sem("s_cst")
        s_w = {n: sem(f"s_w{n}") for n in (0, 1, 2, 3, 4, 5, 7)}
        s_we = sem("s_we")
        s_wl = [sem(f"s_wl{e}") for e in range(E)]
        s_out = sem("s_out")
        s_seeded = sem("s_seeded")
        s_apart = sem("s_apart")
        s_set = counted("s_set")
        s_setp = counted("s_setp")
        s_ctp = counted("s_ctp")
        s_cta = counted("s_cta")
        s_gate = counted("s_gate")
        stat = shared("stat", {n: TT for n in NORMS})
        rstd = shared("rstd", {n: B for n in NORMS})
        nrm = shared("nrm", {n: B for n in NORMS})
        xtp = shared("xtp", {n: B for n in NORMS})
        xts = shared("xts", {n: B for n in NORMS})
        done = shared("done", {n: 0 if n == 5 else TT for n in L})
        pool = shared("pool", {n: B for n in NORMS})
        dve = shared("dve", {n: TT for n in NORMS})
        act = shared("act", {0: SC, 2: B, 4: SC, 7: B})
        prep_p = {n: counted(f"prep_p{n}") for n in (0, 2, 3, 4)}
        prep_a = {n: counted(f"prep_a{n}") for n in (0, 2, 4)}
        prep_v = {n: counted(f"prep_v{n}") for n in (0, 1, 2, 3, 4)}
        q_p = shared("q_p", {0: B, 2: B, 4: B, 7: B})
        q_s = shared("q_s", {0: B, 2: 2 * B, 3: B, 4: 2 * B, 7: B})
        kb_s = shared("kb_s", {0: B, 4: B})
        sc_p = shared("sc_p", {0: SC, 2: B, 4: SC, 7: B})
        sc_r = shared("sc_r", {0: SC, 2: B, 4: SC, 7: B})
        sc_d = counted("sc_d")
        tk_s = counted("tk_s")
        ex_s = shared("ex_s", {0: SC, 2: B, 4: SC, 7: B})
        pt_p = shared("pt_p", {0: SC, 2: B, 4: SC, 7: B})
        pt_s = shared("pt_s", {0: SC, 2: B, 4: SC, 7: B})
        pv_p = shared("pv_p", {0: SC, 2: B, 4: SC, 7: B})
        o_s = shared("o_s", {0: SC, 4: SC})
        ot_p = shared("ot_p", {0: SC, 4: SC})
        ot_s = shared("ot_s", {0: SC, 4: SC})
        f_p = shared("f_p", {n: TT for n in (0, 1, 3, 4, 8)})
        g_s = counted("g_s")
        hq_s = counted("hq_s")
        ht_p = counted("ht_p")
        ht_s = counted("ht_s")
        h_p = counted("h_p")
        h_b = counted("h_b")
        h_r = counted("h_r")
        s_ab = counted("s_ab")
        tk_r = counted("tk_r")
        h_z = counted("h_z")
        s_rd = shared("s_rd", {0: SC, 2: 2 * B, 4: SC, 7: 2 * B})
        keep_s = counted("keep_s")
        lg_p = counted("lg_p")
        rt_v = counted("rt_v")
        rt_a = counted("rt_a")
        rt_p = counted("rt_p")
        routed = counted("routed")
        s_zero = sem("s_zero")
        s_sc = sem("s_sc")
        s_ld = [sem(f"s_ld{u}") for u in range(3)]
        s_st = [counted(f"s_st{u}") for u in range(3)]
        s_ga = [sem(f"s_ga{u}") for u in range(PAIRS)]
        m_xp = counted("m_xp")
        m_xs = counted("m_xs")
        m_h = counted("m_h")
        m_g = counted("m_g")
        m_tp = counted("m_tp")
        m_ts = counted("m_ts")
        m_y = counted("m_y")
        m_ys = counted("m_ys")
        v2_s = counted("v2_s")
        r2_a = counted("r2_a")
        r2_s = counted("r2_s")
        x7_s = counted("x7_s")
        x7_p = counted("x7_p")
        x7_t = counted("x7_t")
        h7_p = counted("h7_p")
        h7_s = counted("h7_s")
        f7_p = counted("f7_p")
        prep_8 = counted("prep_8")
        rt_l = counted("rt_l")
        rt_m = counted("rt_m")
        rt_i = counted("rt_i")
        rt_c = counted("rt_c")
        cmb = counted("cmb")
        dvx = {n: counted(f"dvx{n}") for n in (2, 3, 7, 8)}

        block = ctx.enter_context(nc.Block())

        def pairs(eng):
            return eng.Fori(0, PAIRS)

        def late(n):
            return E * EW + n * EW

        @block.sync
        def _(sp):
            for s in seeds:
                sp.sem_inc(s, 1)
            sp.sem_inc(s_seeded, 1)
            xv = a["x"].rearrange("b (t p) d -> p (b t) d", p=P)
            sp.dma_start(ctxn[:, :, :], a["ctx"].rearrange("b k d -> k b d")).then_inc(s_ctx, 16)
            for dst, key in ((ident, "ident"), (lower, "lower"), (iota, "iota"), (hsel, "hsel"), (cols, "cols")):
                sp.dma_start(dst[:, :], a[key]).then_inc(s_cst, 16)
            sp.dma_start(graw[:, :], a["g"].partition_broadcast(P)).then_inc(s_cst, 16)
            sp.dma_start(rows[:, :, :], a["rows"].rearrange("(o r) d -> o r d", o=1)).then_inc(s_cst, 16)
            sp.dma_start(fmw[:, :, :], a["fmw"]).then_inc(s_w[0], 16)
            sp.dma_start(x[:, :, :], xv).then_inc(s_x, 16)
            sp.dma_start(fcw[:, :, :], a["fcw"].rearrange("(c p) n -> p c n", p=P)).then_inc(s_w[0], 16)
            sp.dma_start(sgw[:, :, :], a["sgw"].rearrange("(c p) n -> p c n", p=P)).then_inc(s_w[1], 16)
            for w, key in ((w1q, "w1q"), (w1k, "w1k"), (w1v, "w1v")):
                sp.dma_start(w[:, :, :], a[key].rearrange("(c p) n -> p c n", p=P)).then_inc(s_w[2], 16)
            sp.dma_start(stage1.rearrange("p (c n) -> p c n", c=CH), a["bw1"].rearrange("(c p) n -> p c n", p=P)).then_inc(s_w[3], 16)
            sp.dma_start(stage2.rearrange("p (c n) -> p c n", c=FF // P), a["bw2"].rearrange("(c p) n -> p c n", p=P)).then_inc(s_w[3], 16)
            sp.dma_start(b1bc, a["bb1"].partition_broadcast(P)).then_inc(s_w[3], 16)
            sp.dma_start(b2bc, a["bb2"].partition_broadcast(P)).then_inc(s_w[3], 16)
            for w, key in ((w2q, "w2q"), (w2k, "w2k"), (w2v, "w2v")):
                sp.dma_start(w[:, :, :], a[key].rearrange("(c p) n -> p c n", p=P)).then_inc(s_w[4], 16)
            sp.dma_start(w2o[:, :, :], a["w2o"].rearrange("(c p) n -> p c n", p=64)).then_inc(s_w[4], 16)
            sp.dma_start(mrow8[:, :], a["mask"].partition_broadcast(P)).then_inc(s_w[4], 16)
            sp.dma_start(rwT[:, :, :], a["rw"].rearrange("(c p) n -> p c n", p=P)).then_inc(s_w[5], 16)
            sp.wait_ge(s_setp.sem, s_setp.past(3))
            if phases >= 5:
                sp.dma_start(xs_d.rearrange("(j p) d -> p j d", p=P),
                             zeros.unsqueeze(1).broadcast_to([P, MT, D])).then_inc(s_zero, 16)
            if phases >= 6:
                def first(e):
                    sp.dma_start(experts[:, e * EW:(e + 1) * EW].rearrange("p (c n) -> p c n", c=CH),
                                 a["ew1"][e].rearrange("(c p) n -> p c n", p=P)).then_inc(s_we, 16)

                def second(e):
                    sp.dma_start(experts[:, late(e):late(e) + EW].rearrange("p (c n) -> p c n", c=FF // P),
                                 a["ew2"][e].rearrange("(c p) n -> p c n", p=P)).then_inc(s_we, 16)

                for e in range(EARLY):
                    first(e)
                sp.wait_ge(done[4].sem, done[4].past(TT))
                sp.wait_ge(s_zero, 16)
                for e in range(EARLY, E):
                    first(e)
                for e in range(2, E):
                    second(e)
                sp.wait_ge(routed.sem, routed.past(1))
                for e in range(2):
                    second(e)
                sp.wait_ge(s_sc, 2 * TT * 16)
                for w, key in ((w3a, "w3a"), (w3b, "w3b"), (w3f, "w3f")):
                    sp.dma_start(w, a[key].rearrange("(c p) n -> p c n", p=P)).then_inc(s_w[7], 16)
                sp.dma_start(bc3, a["bc3"].partition_broadcast(P)).then_inc(s_w[7], 16)

                def load(j, u, k):
                    sp.dma_start(xsb[u], xs_d[bass.ds(j * P, P), :]).then_inc(s_ld[u], 16)

                def store(j, u):
                    sp.wait_ge(m_ys.sem, m_ys.past(j + 1))
                    sp.dma_start(ys_d[bass.ds(j * P, P), :], ysb[u]).then_inc(s_st[u].sem, 16)

                for j in range(3):
                    load(j, j, 0)
                with sp.Fori(0, MT // 3 - 1) as r:
                    for u in range(3):
                        j = r * 3 + u
                        sp.wait_ge(m_xp.sem, m_xp.past(j + 1))
                        load(j + 3, u, r)
                        store(j, u)
                for j in range(MT - 3, MT):
                    store(j, j % 3)
            last = min(phases, 8)
            if last == 8:
                for b in range(B):
                    sp.wait_ge(done[8].sem, done[8].past(TB * (b + 1)))
                    sp.dma_start(out[b].rearrange("(t p) d -> p t d", p=P), x[:, TB * b:TB * b + TB, :]).then_inc(s_out, 16)
                sp.wait_ge(s_out, 16 * B)
            else:
                sp.wait_ge(done[last].sem, done[last].past(TT))
                sp.dma_start(out.rearrange("b (t p) d -> p (b t) d", p=P), x[:, :, :]).then_inc(s_out, 16)
                sp.wait_ge(s_out, 16)

        @block.gpsimd
        def _(gp):
            gp.wait_ge(s_seeded, 1)

            def ln_rstd(n, bb, eps, per=2, src=None, at=0):
                for p in range(2):
                    gp.wait_ge(stat[n].sem, stat[n].past(4 * bb + 2 * p + 2))
                    gp.wait_ge(nrm[n].sem, nrm[n].past(2 * bb))
                    apart(gp)
                    nc.gpsimd.tensor_scalar(rs[p][:, :], mv[p][:, :, 1], eps, None, ALU.add).then_inc(pool[n].sem, 1)
                    gp.wait_ge(pool[n].sem, pool[n].past(2 * bb + p + 1))
                    nc.gpsimd.tensor_tensor(rs[p][:, :], rs[p][:, :], mhalf[:, :], ALU.pow).then_inc(rstd[n].sem, 1)

            nc.gpsimd.memset(ones[:, :], 1.0).then_inc(s_setp.sem, 1)
            nc.gpsimd.memset(mhalf[:, :], -0.5).then_inc(s_setp.sem, 1)
            nc.gpsimd.memset(zeros, 0.0).then_inc(s_setp.sem, 1)

            def heads_keys(n, bb):
                for p in range(2):
                    b = 2 * bb + p
                    gp.wait_ge(sc_p[n].sem, sc_p[n].past(ITEMS * bb))
                    dst = kb[p].rearrange("p g (h k) -> p g h k", h=HG)
                    if n == 0:
                        src = kall[:, :, bass.ds(b * KEYS, KEYS)].unsqueeze(2).broadcast_to([P, GR, HG, KEYS])
                        sel = hsel[:, 0:4].unsqueeze(1).unsqueeze(3).broadcast_to([P, GR, HG, KEYS])
                        nc.gpsimd.tensor_tensor(dst, src, sel, ALU.mult).then_inc(kb_s[n].sem, 1)
                    else:
                        for c in range(CH):
                            d2 = kb[p][:, 2 * c:2 * c + 2, :].rearrange("p g (h k) -> p (g h) k", h=HG)
                            src = kall[:, c, bass.ds(b * KEYS, KEYS)].unsqueeze(1).broadcast_to([P, 8, KEYS])
                            sel = hsel[:, 4:12].unsqueeze(2).broadcast_to([P, 8, KEYS])
                            ins = nc.gpsimd.tensor_tensor(d2, src, sel, ALU.mult)
                        ins.then_inc(kb_s[n].sem, 1)

            gp.wait_ge(prep_a[0].sem, prep_a[0].past(8))
            gp.wait_ge(s_cst, 7 * 16)
            gp.wait_ge(s_setp.sem, s_setp.past(2))
            with pairs(gp) as bb:
                heads_keys(0, bb)
                ln_rstd(0, bb, 1e-5)
            if phases >= 1:
                with pairs(gp) as bb:
                    ln_rstd(1, bb, 1e-5)
            if phases >= 2:
                with pairs(gp) as bb:
                    ln_rstd(2, bb, 1e-5)
            if phases >= 3:
                with pairs(gp) as bb:
                    ln_rstd(3, bb, 1e-5)
            if phases >= 4:
                gp.wait_ge(prep_a[4].sem, prep_a[4].past(4))
                with pairs(gp) as bb:
                    heads_keys(4, bb)
                    ln_rstd(4, bb, 1e-5)
            if phases >= 5:
                with pairs(gp) as bb:
                    ln_rstd(5, bb, 1e-5)
                gp.wait_ge(routed.sem, routed.past(1))
                gp.wait_ge(keep_s.sem, keep_s.past(B))
                gp.wait_ge(s_zero, 16)
                for t in range(TT):
                    for k in range(2):
                        gp.indirect_dma_start(xs_d, bass.IndirectOffsetOnAxis(ap=slot[:, k, t:t + 1], axis=0),
                                              xkeep[:, t, :], None).then_inc(s_sc, 16)
            if phases >= 6:
                gp.wait_ge(m_y.sem, m_y.past(MT))
                for u in range(3):
                    gp.wait_ge(s_st[u].sem, s_st[u].past(MT // 3 * 16))
                for t in range(TT):
                    for k in range(2):
                        gp.indirect_dma_start(got[:, k, t, :], None, ys_d,
                                              bass.IndirectOffsetOnAxis(ap=slot[:, k, t:t + 1], axis=0)
                                              ).then_inc(s_ga[t // 4], 16)
            if phases >= 7:
                with pairs(gp) as bb:
                    ln_rstd(7, bb, 1e-5)
                    for k in range(2):
                        for p in range(2):
                            gp.wait_ge(v2_s.sem, v2_s.past(4 * bb + 2 * k + p + 1))
                            apart(gp)
                            nc.gpsimd.tensor_scalar(rs[p][:, :], mv[p][:, :, 1], 1e-6, None, ALU.add
                                                    ).then_inc(r2_a.sem, 1)
                            gp.wait_ge(r2_a.sem, r2_a.past(4 * bb + 2 * k + p + 1))
                            nc.gpsimd.tensor_tensor(rs[p][:, :], rs[p][:, :], mhalf[:, :], ALU.pow).then_inc(r2_s.sem, 1)
            if phases >= 8:
                with pairs(gp) as bb:
                    ln_rstd(8, bb, 1e-5)

        @block.scalar
        def _(ac):
            ac.wait_ge(s_seeded, 1)

            def copy(dst, src):
                return nc.scalar.activation(dst, src, ACT.Copy)

            def turned(n, bb, used, per):
                for p in range(2):
                    ac.wait_ge(xtp[n].sem, xtp[n].past(2 * bb + p + 1))
                    ac.wait_ge(used.sem, used.past(per * bb))
                    copy(xnT[p][:, :, :].rearrange("p c s -> p (c s)"), bank(p)).then_inc(xts[n].sem, 1)

            ac.wait_ge(s_cst, 7 * 16)
            nc.scalar.activation(gates[:, :], graw[:, :], ACT.Tanh).then_inc(s_gate.sem, 1)
            for c in range(CH):
                for h in range(2):
                    ac.wait_ge(s_ctp.sem, s_ctp.past(2 * c + h + 1))
                    copy(ctxT[:, c, h * HALF:(h + 1) * HALF], bank(2 * c + h)[:, 0:HALF]).then_inc(s_cta.sem, 1)

            ac.wait_ge(s_set.sem, s_set.past(3))
            for j in range(2 * GR):
                ac.wait_ge(prep_p[0].sem, prep_p[0].past(j + 1))
                nc.scalar.activation(kall[:, j // 2, (j % 2) * HALF:(j % 2 + 1) * HALF], bank(j)[:, 0:HALF], ACT.Exp,
                                     bias=cols[:, 0:1]).then_inc(prep_a[0].sem, 1)

            def heads(n, bb):
                top = n == 4
                lag = 1 if top else 0
                nq = 2 if top else 1
                turned(n, bb, q_p[n], 2)
                for p in range(2):
                    ac.wait_ge(q_p[n].sem, q_p[n].past(2 * bb + p + 1))
                    ac.wait_ge(f_p[n].sem, f_p[n].past(4 * bb))
                    if n == 0:
                        nc.scalar.activation(wk[p][:, :, :].rearrange("p (u g) s -> p u (g s)", u=2),
                                             ps[1 + p][:, :, :], ACT.Exp, bias=cols[:, 0:1]).then_inc(q_s[n].sem, 1)
                    else:
                        for m in range(CH):
                            nc.scalar.activation(wk[p][:, m, :], bank(2 + p)[:, m * S:(m + 1) * S], ACT.Identity,
                                                 bias=cols[:, 12 + m:13 + m], scale=-0.25).then_inc(q_s[n].sem, 1)
                for s in range(ITEMS + 3 + lag):
                    i = s - lag
                    if 0 <= i < ITEMS:
                        u = i % 2
                        row = pr[u]
                        if top:
                            ac.wait_ge(tk_s.sem, tk_s.past(ITEMS * bb + i + 1))
                            ac.wait_ge(pt_p[n].sem, pt_p[n].past(ITEMS * bb + max(i - 1, 0)))
                            nc.scalar.activation(row[:, :, :], dd[u][:, :, :], ACT.Abs).then_inc(s_ab.sem, 1)
                            ac.wait_ge(s_ab.sem, s_ab.past(ITEMS * bb + i + 1))
                            apart(ac)
                            nc.scalar.activation(row[:, :, :], row[:, :, :], ACT.Exp,
                                                 scale=mcol[:, bass.ds(2 * bb + u, 1)]).then_inc(ex_s[n].sem, 1)
                        else:
                            ac.wait_ge(sc_r[n].sem, sc_r[n].past(ITEMS * bb + i + 1))
                            nc.scalar.activation(row[:, :, :], row[:, :, :], ACT.Exp, scale=1.0 / 16).then_inc(ex_s[n].sem, 1)
                    i = s - 1 - lag
                    if 0 <= i < ITEMS:
                        ac.wait_ge(pt_p[n].sem, pt_p[n].past(ITEMS * bb + i + 1))
                        ac.wait_ge(pv_p[n].sem, pv_p[n].past(ITEMS * bb + max(i - 1, 0)))
                        nc.scalar.activation(pt[i % 2][:, :].rearrange("p (u n) -> p u n", u=2), ps[2][0:KEYS, :, :],
                                             ACT.Copy).then_inc(pt_s[n].sem, 1)
                    i = s - 3 - lag
                    if 0 <= i < ITEMS:
                        w = 64 if top else P
                        ac.wait_ge(ot_p[n].sem, ot_p[n].past(ITEMS * bb + i + 1))
                        copy(oT[i % 2][0:w, i // 2, :], bank(7)[0:w, 0:S]).then_inc(ot_s[n].sem, 1)

            with pairs(ac) as bb:
                heads(0, bb)

            def single(n, bb, vscale):
                for p in range(2):
                    ac.wait_ge(sc_r[n].sem, sc_r[n].past(2 * bb + p + 1))
                    nc.scalar.activation(pr[p][:, :, 0:KEYS], pr[p][:, :, 0:KEYS], ACT.Exp,
                                         scale=1.0 / 16).then_inc(ex_s[n].sem, 1)
                for p in range(2):
                    ac.wait_ge(pt_p[n].sem, pt_p[n].past(2 * bb + p + 1))
                    ac.wait_ge(pv_p[n].sem, pv_p[n].past(2 * bb))
                    copy(pt[p][:, 0:S], bank(6 + p)[0:KEYS, 0:S]).then_inc(pt_s[n].sem, 1)

            if phases >= 1:
                ac.wait_ge(done[0].sem, done[0].past(TT))
                with pairs(ac) as bb:
                    turned(1, bb, f_p[1], 4)
            if phases >= 2:
                ac.wait_ge(done[1].sem, done[1].past(TT))
                for j in range(4):
                    ac.wait_ge(prep_p[2].sem, prep_p[2].past(j + 1))
                    nc.scalar.activation(kall[:, j // 2, (j % 2) * HALF:(j % 2 + 1) * HALF], bank(j)[:, 0:HALF],
                                         ACT.Identity, bias=cols[:, 3 + j // 2:4 + j // 2]).then_inc(prep_a[2].sem, 1)
                with pairs(ac) as bb:
                    turned(2, bb, q_p[2], 2)
                    for p in range(2):
                        ac.wait_ge(q_p[2].sem, q_p[2].past(2 * bb + p + 1))
                        ac.wait_ge(sc_p[2].sem, sc_p[2].past(2 * bb))
                        for m in range(CH):
                            nc.scalar.activation(wk[p][:, m, :], bank(2 + p)[:, m * S:(m + 1) * S], ACT.Identity,
                                                 bias=cols[:, 1 + m:2 + m]).then_inc(q_s[2].sem, 1)
                    single(2, bb, 1)
            if phases >= 3:
                ac.wait_ge(done[2].sem, done[2].past(TT))
                with pairs(ac) as bb:
                    for p in range(2):
                        ac.wait_ge(xtp[3].sem, xtp[3].past(2 * bb + p + 1))
                        ac.wait_ge(h_p.sem, h_p.past(4 * bb))
                        copy(xnT[p][:, 0, :].bitcast(bf16), bank(4 + 3 * p)[:, 0:S].bitcast(bf16)).then_inc(xts[3].sem, 1)
                    for s in range(4 + 2):
                        if s < 4:
                            ac.wait_ge(h_b.sem, h_b.past(4 * bb + s + 1))
                            hrow = wk[s % 2][:, :, :].rearrange("p c s -> p (c s)")
                            nc.scalar.activation(hrow, hrow, ACT.Gelu).then_inc(g_s.sem, 1)
                        if 1 <= s < 5:
                            u = s - 1
                            ac.wait_ge(h_r.sem, h_r.past(4 * bb + u + 1))
                            hrow = wk[u % 2][:, :, :].rearrange("p c s -> p (c s)")
                            nc.scalar.activation(hrow, hrow, ACT.Copy, scale=sm[:, u % 2, 3, u // 2:u // 2 + 1],
                                                 bias=MAGIC).then_inc(hq_s.sem, 1)
                        if s >= 2:
                            u = s - 2
                            ac.wait_ge(ht_p.sem, ht_p.past(4 * bb + u + 1))
                            ac.wait_ge(f_p[3].sem, f_p[3].past(4 * bb + max(u - 1, 0)))
                            copy(pr[u % 2].rearrange("p t n -> p (t n)")[:, 0:512].bitcast(bf16),
                                 bank(5).bitcast(bf16)).then_inc(ht_s.sem, 1)
            if phases >= 4:
                ac.wait_ge(done[3].sem, done[3].past(TT))
                ac.wait_ge(s_w[4], 5 * 16)
                ac.wait_ge(s_set.sem, s_set.past(3))
                for j in range(4):
                    ac.wait_ge(prep_p[4].sem, prep_p[4].past(j + 1))
                    nc.scalar.activation(kall[:, j // 2, (j % 2) * HALF:(j % 2 + 1) * HALF], bank(j)[:, 0:HALF],
                                         ACT.Identity, bias=cols[:, 7 + j // 2:8 + j // 2]).then_inc(prep_a[4].sem, 1)
                ac.wait_ge(prep_v[4].sem, prep_v[4].past(7))
                with pairs(ac) as bb:
                    heads(4, bb)
            if phases >= 5:
                ac.wait_ge(done[4].sem, done[4].past(TT))
                with pairs(ac) as bb:
                    for p in range(2):
                        ac.wait_ge(nrm[5].sem, nrm[5].past(2 * bb + p + 1))
                        copy(xkeep[:, bass.ds(4 * bb + 2 * p, 2), :], xn[p][:, :, :]).then_inc(keep_s.sem, 1)
                    turned(5, bb, lg_p, 2)
                ac.wait_ge(rt_v.sem, rt_v.past(1))
                nc.scalar.activation(gate2[:, :, 1], gate2[:, :, 0], ACT.Exp).then_inc(rt_a.sem, 1)
            if phases >= 6:
                ac.wait_ge(routed.sem, routed.past(1))

                def gelu(j):
                    ac.wait_ge(m_h.sem, m_h.past(j + 1))
                    ac.wait_ge(m_tp.sem, m_tp.past(j))
                    nc.scalar.activation(hid[:, :, :].rearrange("p (v c) s -> p v (c s)", v=2), ps[0][:, :, :],
                                         ACT.Gelu).then_inc(m_g.sem, 1)

                def result(j, u, k):
                    ac.wait_ge(m_y.sem, m_y.past(j + 1))
                    ac.wait_ge(s_st[u].sem, s_st[u].past(16 * k))
                    copy(ysb[u], bank(4)[:, 0:D]).then_inc(m_ys.sem, 1)

                gelu(0)
                with ac.Fori(0, (MT - 3) // 3) as r:
                    for u in range(3):
                        j = r * 3 + u + 1
                        gelu(j)
                        result(j - 1, u, r)
                for j in range(MT - 2, MT):
                    gelu(j)
                    result(j - 1, (j - 1) % 3, (j - 1) // 3)
                result(MT - 1, (MT - 1) % 3, (MT - 1) // 3)
            if phases >= 7:
                ac.wait_ge(done[6].sem, done[6].past(TT))
                with pairs(ac) as bb:
                    turned(7, bb, h7_p, 2)
                    single(7, bb, 1)
                    for p in range(2):
                        ac.wait_ge(x7_p.sem, x7_p.past(2 * bb + p + 1))
                        copy(xnT[p][:, :, :].rearrange("p c s -> p (c s)"), bank(p)).then_inc(x7_t.sem, 1)
                    for p in range(2):
                        ac.wait_ge(h7_p.sem, h7_p.past(2 * bb + p + 1))
                        ac.wait_ge(f7_p.sem, f7_p.past(2 * bb))
                        for m in range(CH):
                            ins = nc.scalar.activation(wk[p][:, m, :], bank(2 + p)[:, m * S:(m + 1) * S], ACT.Relu,
                                                       bias=cols[:, 9 + m:10 + m])
                        ins.then_inc(h7_s.sem, 1)
            if phases >= 8:
                ac.wait_ge(done[7].sem, done[7].past(TT))
                with pairs(ac) as bb:
                    turned(8, bb, f_p[8], 4)

        @block.vector
        def _(ve):
            ve.wait_ge(s_seeded, 1)

            def ln(n, bb, keep=False, used=None, per=2):
                for p in range(2):
                    for t in range(TB):
                        if p == 0 and t == 0:
                            ve.wait_ge(dve[n].sem, dve[n].past(4 * bb))
                        nc.vector.bn_stats(st[p][:, t, :], x[:, 4 * bb + 2 * p + t, :]).then_inc(dve[n].sem, 1)
                for p in range(2):
                    for t in range(TB):
                        ve.wait_ge(dve[n].sem, dve[n].past(4 * bb + 2 * p + t + 1))
                        ve.wait_ge(rstd[n].sem, rstd[n].past(2 * bb))
                        apart(ve)
                        nc.vector.bn_aggr(mv[p][:, t, :], st[p][:, t, :]).then_inc(stat[n].sem, 1)
                for p in range(2):
                    ve.wait_ge(rstd[n].sem, rstd[n].past(2 * bb + p + 1))
                    ve.wait_ge(used.sem, used.past(per * bb))
                    for t in range(TB):
                        ins = nc.vector.tensor_scalar(xn[p][:, t, :], x[:, 4 * bb + 2 * p + t, :], mv[p][:, t, 0:1],
                                                      rs[p][:, t:t + 1], ALU.subtract, ALU.mult)
                    ins.then_inc(nrm[n].sem, 1)

            def residual(n, bb, p, t, src, factor):
                row = x[:, 4 * bb + 2 * p + t, :]
                nc.vector.scalar_tensor_tensor(row, src, factor, row, ALU.mult, ALU.add).then_inc(done[n].sem, 1)

            ve.wait_ge(s_cst, 7 * 16)
            ve.wait_ge(s_w[0], 2 * 16)
            nc.vector.tensor_copy(identb[:, :], ident[:, :]).then_inc(s_set.sem, 1)
            neg = fmw[:, :, :].rearrange("p g (h s e) -> p (g h) s e", h=HG, s=2)[:, :, 1, :]
            nc.vector.tensor_scalar(neg, neg, -1.0, None, ALU.mult).then_inc(s_set.sem, 1)
            nc.vector.tensor_tensor(cols[:, 0:1], cols[:, 0:1], cols[:, 15:16], ALU.mult).then_inc(s_set.sem, 1)
            v0 = vall[:, 0:B * HEADS * 33].rearrange("p (b h e) -> p b h e", b=B, h=HEADS)
            nc.vector.memset(vall[:, 0:B * HEADS * 33].rearrange("p (q e) -> p q e", e=33)[:, :, 32:33], 1.0)
            for b in range(B):
                ve.wait_ge(prep_p[0].sem, prep_p[0].past(8 + b + 1))
                nc.vector.tensor_copy(v0[:, b, :, 0:32], bank(b)[0:KEYS, :].rearrange("p (h e) -> p h e", h=HEADS)
                                      ).then_inc(prep_v[0].sem, 1)
            ve.wait_ge(s_x, 16)
            ve.wait_ge(s_gate.sem, s_gate.past(1))

            def heads(n, bb):
                top = n == 4
                vd = 16 if top else 32
                lag = 1 if top else 0
                ln(n, bb, used=xtp[n])
                per = 1 if not top else 2 + 1
                for s in range(ITEMS + 2 + lag):
                    if s < ITEMS:
                        i, u = s, s % 2
                        ve.wait_ge(sc_p[n].sem, sc_p[n].past(ITEMS * bb + i + 1))
                        sv = ps[u][:, :, 0:GK].rearrange("p t (h k) -> p (t h) k", h=HG) if False else \
                            ps[u][:, :, 0:GK].rearrange("p t (h k) -> p t h k", h=HG)
                        if not top:
                            nc.vector.tensor_reduce(mx[u][:, :].rearrange("p (t h) -> p t h", t=TB), sv, AX.X, ALU.max
                                                    ).then_inc(act[n].sem, 1)
                            ve.wait_ge(act[n].sem, act[n].past(ITEMS * bb + i + 1))
                            ve.wait_ge(pt_p[n].sem, pt_p[n].past(ITEMS * bb + max(i - 1, 0)))
                            nc.vector.tensor_tensor(pr[u].rearrange("p t (h k) -> p t h k", h=HG), sv,
                                                    mx[u][:, :].rearrange("p (t h) -> p t h", t=TB).unsqueeze(3)
                                                    .broadcast_to([P, TB, HG, KEYS]), ALU.subtract).then_inc(sc_r[n].sem, 1)
                        else:
                            dv = dd[u].rearrange("p t (h k) -> p t h k", h=HG)
                            ve.wait_ge(ex_s[n].sem, ex_s[n].past(ITEMS * bb + max(i - 1, 0)))
                            mb = mrow[:, bass.ds((2 * bb + u) * KEYS, KEYS)].unsqueeze(1).unsqueeze(1) \
                                .broadcast_to([P, TB, HG, KEYS])
                            nc.vector.tensor_tensor(dv, sv, mb, ALU.max).then_inc(sc_r[n].sem, 1)
                            ve.wait_ge(sc_r[n].sem, sc_r[n].past(ITEMS * bb + i + 1))
                            mn = mx[u][:, :].rearrange("p (t h) -> p t h", t=TB)
                            nc.vector.tensor_reduce(mn, dv, AX.X, ALU.min).then_inc(act[n].sem, 1)
                            ve.wait_ge(act[n].sem, act[n].past(ITEMS * bb + i + 1))
                            nc.vector.tensor_tensor(dv, dv, mn.unsqueeze(3).broadcast_to([P, TB, HG, KEYS]),
                                                    ALU.subtract).then_inc(sc_d.sem, 1)
                    if top and 1 <= s <= ITEMS:
                        i = s - 1
                        u = i % 2
                        ve.wait_ge(sc_d.sem, sc_d.past(ITEMS * bb + i + 1))
                        rounds = Chain(ve, tk_r, (ITEMS * bb + i) * 33)
                        d = [dd[u][:, j // HG, (j % HG) * KEYS:(j % HG + 1) * KEYS] for j in range(8)]
                        apart(ve)
                        for j in range(8):
                            rounds.step(nc.vector.max(m8[u][:, j, :], d[j]))
                        for j in range(8):
                            ve.wait_ge(tk_r.sem, tk_r.past((ITEMS * bb + i) * 33 + j + 1))
                            apart(ve)
                            rounds.step(nc.vector.match_replace(d[j], m8[u][:, j, :], d[j], -BIG))
                        for j in range(8):
                            ve.wait_ge(tk_r.sem, tk_r.past((ITEMS * bb + i) * 33 + 8 + j + 1))
                            apart(ve)
                            rounds.step(nc.vector.max(m8b[u][:, j, :], d[j]))
                        rounds.settle()
                        rounds.link(nc.vector.memset(m8b[u][:, :, DROP - 8:8], -BIG))
                        apart(ve)
                        for j in range(8):
                            ins = nc.vector.match_replace(d[j], m8b[u][:, j, :], d[j], -BIG)
                            if j < 7:
                                rounds.step(ins)
                        rounds.n += 1
                        ins.then_inc(tk_r.sem, 1)
                        ve.wait_ge(tk_r.sem, tk_r.past((ITEMS * bb + i + 1) * 33))
                        ve.sem_inc(tk_s.sem, 1)
                    i = s - 2 - lag
                    if 0 <= i < ITEMS:
                        u = i % 2
                        ve.wait_ge(pv_p[n].sem, pv_p[n].past(ITEMS * bb + i + 1))
                        ov = bank(6)[:, 0:8 * (vd + 1)].rearrange("p (j e) -> p j e", j=8)
                        nc.vector.reciprocal(rden[u][:, :], ov[:, :, vd]).then_inc(s_rd[n].sem, 1)
                        ve.wait_ge(s_rd[n].sem, s_rd[n].past(ITEMS * bb + i + 1))
                        ve.wait_ge(ot_p[n].sem, ot_p[n].past(ITEMS * bb + max(i - 1, 0)))
                        nc.vector.tensor_tensor(osb[u][:, :, 0:HG * vd].rearrange("p t (h e) -> p t h e", h=HG),
                                                ov[:, :, 0:vd].rearrange("p (t h) e -> p t h e", t=TB),
                                                rden[u][:, :].rearrange("p (t h) -> p t h", t=TB).unsqueeze(3)
                                                .broadcast_to([P, TB, HG, vd]), ALU.mult).then_inc(o_s[n].sem, 1)
                for p in range(2):
                    for t in range(TB):
                        ve.wait_ge(f_p[n].sem, f_p[n].past(4 * bb + 2 * p + t + 1))
                        residual(n, bb, p, t, bank(2 * p + t)[:, 0:D], gates[:, n // 2:n // 2 + 1])

            with pairs(ve) as bb:
                heads(0, bb)

            if phases >= 1:
                ve.wait_ge(s_w[1], 16)
                ve.wait_ge(done[0].sem, done[0].past(TT))
                c1 = Chain(ve, prep_v[1])
                wv = sgw[:, :, :].rearrange("p c n -> p (c n)")
                tmp = xkeep_tmp[:, 0:CH * D]
                c1.link(nc.vector.tensor_scalar(tmp, wv, 0.0, None, ALU.is_lt))
                c1.link(nc.vector.scalar_tensor_tensor(wv, wv, 0.0, tmp, ALU.is_gt, ALU.subtract))
                with pairs(ve) as bb:
                    ln(1, bb, used=xtp[1])
                    for p in range(2):
                        for t in range(TB):
                            ve.wait_ge(f_p[1].sem, f_p[1].past(4 * bb + 2 * p + t + 1))
                            residual(1, bb, p, t, bank(4 + 2 * p + t)[:, 0:D], gates[:, 4:5])

            def single_soft(n, bb, p):
                ve.wait_ge(sc_p[n].sem, sc_p[n].past(2 * bb + p + 1))
                sv = bank(4 + p)[:, 0:TB * KEYS].rearrange("p (t k) -> p t k", t=TB)
                nc.vector.tensor_reduce(mx[p][:, 0:TB], sv, AX.X, ALU.max).then_inc(act[n].sem, 1)
                ve.wait_ge(act[n].sem, act[n].past(3 * (2 * bb + p) + 1 if False else 2 * bb + p + 1))
                ve.wait_ge(pt_p[n].sem, pt_p[n].past(2 * bb))
                nc.vector.tensor_tensor(pr[p][:, :, 0:KEYS], sv, mx[p][:, 0:TB].unsqueeze(2)
                                        .broadcast_to([P, TB, KEYS]), ALU.subtract).then_inc(sc_r[n].sem, 1)

            def single_sum(n, bb, p):
                ve.wait_ge(ex_s[n].sem, ex_s[n].past(2 * bb + p + 1))
                nc.vector.tensor_reduce(rden[p][:, 0:TB], pr[p][:, :, 0:KEYS], AX.X, ALU.add).then_inc(s_rd[n].sem, 1)
                ve.wait_ge(s_rd[n].sem, s_rd[n].past(2 * (2 * bb + p) + 1))
                nc.vector.reciprocal(rden[p][:, TB:2 * TB], rden[p][:, 0:TB]).then_inc(s_rd[n].sem, 1)
                ve.wait_ge(s_rd[n].sem, s_rd[n].past(2 * (2 * bb + p) + 2))

            if phases >= 2:
                ve.wait_ge(done[1].sem, done[1].past(TT))
                for j in range(4):
                    ve.wait_ge(prep_p[2].sem, prep_p[2].past(4 + j + 1))
                    nc.vector.tensor_copy(vall[:, j * 512:(j + 1) * 512], bank(4 + j)[0:KEYS, :]).then_inc(prep_v[2].sem, 1)
                with pairs(ve) as bb:
                    ln(2, bb, used=xtp[2])
                    for p in range(2):
                        single_soft(2, bb, p)
                    for p in range(2):
                        single_sum(2, bb, p)
                        nc.vector.tensor_scalar(rden[p][:, 4:4 + TB], rden[p][:, TB:2 * TB], gates[:, 1:2], None,
                                                ALU.mult).then_inc(dvx[2].sem, 1)
                    ve.wait_ge(dvx[2].sem, dvx[2].past(2 * bb + 2))
                    for p in range(2):
                        ve.wait_ge(pv_p[2].sem, pv_p[2].past(2 * bb + p + 1))
                        for t in range(TB):
                            residual(2, bb, p, t, bank(p)[:, t * D:(t + 1) * D], rden[p][:, 4 + t:5 + t])

            if phases >= 3:
                ve.wait_ge(done[2].sem, done[2].past(TT))
                ve.wait_ge(s_w[3], 4 * 16)
                c3 = Chain(ve, prep_v[3])
                for k, (stg, tern) in enumerate(((stage1, tern1), (stage2, tern2))):
                    tv = tern[:, :, :].rearrange("p c n -> p (c n)")
                    tmp = vtmp
                    c3.link(nc.vector.tensor_reduce(wstat[:, k:k + 1], stg, AX.X, ALU.add, apply_absolute_value=True))
                    ve.wait_ge(prep_p[3].sem, prep_p[3].past(k + 1))
                    c3.link(nc.vector.tensor_scalar(wstat[:, 2 + k:3 + k], bank(k)[:, 0:1], 1.0 / (D * FF), EPS_Q,
                                                    ALU.mult, ALU.max))
                    c3.link(nc.vector.tensor_scalar(wstat[:, 4 + k:5 + k], wstat[:, 2 + k:3 + k], 0.5, None, ALU.mult))
                    c3.link(nc.vector.tensor_scalar(wstat[:, 6 + k:7 + k], wstat[:, 2 + k:3 + k], -0.5, None, ALU.mult))
                    c3.link(nc.vector.tensor_scalar(tmp, stg, wstat[:, 4 + k:5 + k], None, ALU.is_gt))
                    c3.link(nc.vector.scalar_tensor_tensor(tv, stg, wstat[:, 6 + k:7 + k], tmp, ALU.is_lt, ALU.subtract))
                    c3.link(nc.vector.tensor_scalar(wstat[:, 4 + k:5 + k], wstat[:, 2 + k:3 + k], -1.0 / QB, None,
                                                    ALU.mult))
                c3.link(nc.vector.tensor_tensor(wstat[:, 5:6], wstat[:, 5:6], gates[:, 5:6], ALU.mult))
                c3.link(nc.vector.tensor_scalar(b2bc, b2bc, gates[:, 5:6], None, ALU.mult))
                N3 = 2 * (6) + 4 * 6
                with pairs(ve) as bb:
                    ln(3, bb, used=xtp[3])
                    ch = Chain(ve, dvx[3], N3 * bb)
                    for p in range(2):
                        ve.wait_ge(nrm[3].sem, nrm[3].past(2 * bb + p + 1))
                        ch.link(nc.vector.tensor_reduce(sm[:, p, 0, 0:TB], xn[p][:, :, :], AX.X, ALU.max,
                                                        apply_absolute_value=True))
                        ch.link(nc.vector.tensor_scalar(sm[:, p, 0, 0:TB], sm[:, p, 0, 0:TB], EPS_Q, None, ALU.max))
                        ch.link(nc.vector.reciprocal(sm[:, p, 1, 0:TB], sm[:, p, 0, 0:TB]))
                        ch.link(nc.vector.tensor_scalar(sm[:, p, 1, 0:TB], sm[:, p, 1, 0:TB], QB, None, ALU.mult))
                        ch.step(nc.vector.tensor_scalar(sm[:, p, 0, 0:TB], sm[:, p, 0, 0:TB], wstat[:, 4:5], None,
                                                        ALU.mult))
                        for t in range(TB):
                            ins = nc.vector.tensor_scalar(xn[p][:, t, :], xn[p][:, t, :], sm[:, p, 1, t:t + 1], MAGIC,
                                                          ALU.mult, ALU.add)
                        ch.link(ins)
                        nc.vector.tensor_scalar(xq[p][:, :, :], xn[p][:, :, :], MAGIC, QB, ALU.subtract, ALU.min
                                                ).then_inc(q_s[3].sem, 1)
                    for s in range(4 + 2):
                        if s < 4:
                            u = s
                            ve.wait_ge(h_p.sem, h_p.past(4 * bb + u + 1))
                            if u >= 2:
                                pass
                            ve.wait_ge(h_z.sem, h_z.past(4 * bb + max(u - 1, 0)))
                            hrow = wk[u % 2][:, :, :].rearrange("p (v c) s -> p v (c s)", v=2)
                            nc.vector.scalar_tensor_tensor(hrow, ps[u % 2][:, :, :], sm[:, u // 2, 0, u % 2:u % 2 + 1],
                                                           b1bc.rearrange("p (v n) -> p v n", v=2),
                                                           ALU.mult, ALU.add).then_inc(h_b.sem, 1)
                        if 1 <= s < 5:
                            u = s - 1
                            k = slice(u // 2, u // 2 + 1)
                            ve.wait_ge(g_s.sem, g_s.past(4 * bb + u + 1))
                            hrow = wk[u % 2][:, :, :].rearrange("p c s -> p (c s)")
                            ch.link(nc.vector.tensor_reduce(sm[:, u % 2, 2, k], hrow, AX.X, ALU.max,
                                                            apply_absolute_value=True))
                            ch.link(nc.vector.tensor_scalar(sm[:, u % 2, 2, k], sm[:, u % 2, 2, k], EPS_Q, None, ALU.max))
                            ch.link(nc.vector.reciprocal(sm[:, u % 2, 3, k], sm[:, u % 2, 2, k]))
                            ch.link(nc.vector.tensor_scalar(sm[:, u % 2, 3, k], sm[:, u % 2, 3, k], QB, None, ALU.mult))
                            ch.link(nc.vector.tensor_scalar(sm[:, u % 2, 2, k], sm[:, u % 2, 2, k], wstat[:, 5:6], None,
                                                            ALU.mult))
                            ve.sem_inc(h_r.sem, 1)
                            ve.wait_ge(hq_s.sem, hq_s.past(4 * bb + u + 1))
                            ve.wait_ge(ht_p.sem, ht_p.past(4 * bb + max(u - 1, 0)))
                            nc.vector.tensor_scalar(hq[u % 2], hrow, MAGIC, QB, ALU.subtract, ALU.min).then_inc(h_z.sem, 1)
                        if s >= 2:
                            u = s - 2
                            k = slice(u // 2, u // 2 + 1)
                            ve.wait_ge(f_p[3].sem, f_p[3].past(4 * bb + u + 1))
                            row = x[:, 4 * bb + u, :]
                            ch.link(nc.vector.scalar_tensor_tensor(row, bank(6 + u % 2)[:, 0:D], sm[:, u % 2, 2, k], row,
                                                                   ALU.mult, ALU.add))
                            nc.vector.tensor_tensor(row, row, b2bc, ALU.add).then_inc(done[3].sem, 1)
                    assert ch.n == N3, ch.n

            if phases >= 4:
                ve.wait_ge(done[3].sem, done[3].past(TT))
                ve.wait_ge(s_w[4], 5 * 16)
                c4 = Chain(ve, prep_v[4])
                v2 = vall[:, 0:B * HEADS * 17].rearrange("p (b h e) -> p b h e", b=B, h=HEADS)
                c4.link(nc.vector.tensor_copy(mrow, mrow8[:, :]))
                c4.link(nc.vector.tensor_reduce(mcol[:, :], mrow.rearrange("p (b k) -> p b k", b=B), AX.X, ALU.max))
                c4.link(nc.vector.tensor_scalar(mcol[:, :], mcol[:, :], -1.0, None, ALU.mult))
                c4.link(nc.vector.tensor_scalar(mrow, mrow, -2.0 * BIG, BIG, ALU.mult, ALU.add))
                c4.link(nc.vector.tensor_scalar(cols[:, 12:14], cols[:, 5:7], -0.25, None, ALU.mult))
                c4.link(nc.vector.memset(vall[:, 0:B * HEADS * 17].rearrange("p (q e) -> p q e", e=17)[:, :, 16:17], 1.0))
                for j in range(4):
                    ve.wait_ge(prep_p[4].sem, prep_p[4].past(4 + j + 1))
                    for h in range(2):
                        ins = nc.vector.tensor_copy(v2[:, 2 * j + h, :, 0:16],
                                                    bank(4 + j)[0:KEYS, h * D:(h + 1) * D]
                                                    .rearrange("p (h e) -> p h e", h=HEADS))
                    c4.step(ins)
                with pairs(ve) as bb:
                    heads(4, bb)

            if phases >= 5:
                ve.wait_ge(done[4].sem, done[4].past(TT))
                with pairs(ve) as bb:
                    ve.wait_ge(keep_s.sem, keep_s.past(2 * bb))
                    ln(5, bb, used=xtp[5])
                    for p in range(2):
                        ve.wait_ge(lg_p.sem, lg_p.past(2 * bb + p + 1))
                        nc.vector.tensor_copy(lg[p][:, :, :], bank(2 + p)[:, 0:TB * E].rearrange(
                            "p (t e) -> p t e", t=TB)).then_inc(rt_l.sem, 1)
                    for p in range(2):
                        ve.wait_ge(rt_l.sem, rt_l.past(2 * bb + p + 1))
                        apart(ve)
                        for t in range(TB):
                            nc.vector.max(m8[p][:, t, :], lg[p][:, t, :]).then_inc(rt_m.sem, 1)
                    for p in range(2):
                        for t in range(TB):
                            ve.wait_ge(rt_m.sem, rt_m.past(4 * bb + 2 * p + t + 1))
                            apart(ve)
                            nc.vector.max_index(ix[p][:, t, :], m8[p][:, t, :], lg[p][:, t, :]).then_inc(rt_i.sem, 1)
                    for p in range(2):
                        ve.wait_ge(rt_i.sem, rt_i.past(4 * bb + 2 * p + 2))
                        nc.vector.tensor_copy(topv[:, bass.ds(4 * bb + 2 * p, 2), :], m8[p][:, 0:2, 0:2]).then_inc(rt_c.sem, 1)
                        nc.vector.tensor_copy(topi[:, bass.ds(4 * bb + 2 * p, 2), :], ix[p][:, :, 0:2]).then_inc(rt_c.sem, 1)
                ve.wait_ge(rt_c.sem, rt_c.past(16))
                c5 = Chain(ve, rt_v)
                c5.link(nc.vector.tensor_tensor(gate2[:, :, 0], topv[:, :, 1], topv[:, :, 0], ALU.subtract))
                oh = rt[:, 0:256]
                cum = rt[:, 256:512]
                tot = rt[:, 512:768]
                base = rt[:, 768:1024]
                cnt = rt[:, 1024:1040]
                off = rt[:, 1040:1056]
                til = rt[:, 1056:1064]
                end = rt[:, 1064:1072]
                tmp = rt[:, 1280:1536]
                pos = rt[:, 1536:1568]
                where = rt[:, 1568:1600]
                one = rt[:, 1600:1632]
                ef = rt[:, 1632:1632 + 64]
                oh3 = oh.rearrange("p (q e) -> p q e", e=E)
                c5.link(nc.vector.tensor_tensor(oh3, iota[:, 0:E].unsqueeze(1).broadcast_to([P, 2 * TT, E]),
                                                topi[:, :, :].rearrange("p t k -> p (t k)").unsqueeze(2)
                                                .broadcast_to([P, 2 * TT, E]), ALU.is_equal))
                ve.wait_ge(rt_p.sem, rt_p.past(2))
                c5.step(nc.vector.tensor_copy(cum, bank(0)[:, 0:256]))
                c5.link(nc.vector.tensor_copy(tot, bank(1)[:, 0:256]))
                c5.link(nc.vector.memset(base[:, 0:16], 0.0))
                for t in range(1, TT):
                    c5.link(nc.vector.tensor_tensor(base[:, 16 * t:16 * t + 16], base[:, 16 * t - 16:16 * t],
                                                    tot[:, 16 * t - 16:16 * t], ALU.add))
                c5.link(nc.vector.tensor_tensor(cnt, base[:, 240:256], tot[:, 240:256], ALU.add))
                c5.link(nc.vector.tensor_tensor(til, cnt[:, 0:8], cnt[:, 8:16], ALU.add))
                c5.link(nc.vector.tensor_scalar(til, til, 1.0 / P, 127.0 / 256, ALU.mult, ALU.add))
                c5.link(nc.vector.tensor_scalar(til, til, MAGIC, None, ALU.add))
                c5.link(nc.vector.tensor_scalar(til, til, MAGIC, None, ALU.subtract))
                c5.link(nc.vector.tensor_copy(end[:, 0:1], til[:, 0:1]))
                for e in range(1, E):
                    c5.link(nc.vector.tensor_tensor(end[:, e:e + 1], end[:, e - 1:e], til[:, e:e + 1], ALU.add))
                c5.link(nc.vector.tensor_tensor(off[:, 0:8], end, til, ALU.subtract))
                c5.link(nc.vector.tensor_scalar(off[:, 0:8], off[:, 0:8], float(P), -1.0, ALU.mult, ALU.add))
                c5.link(nc.vector.tensor_tensor(off[:, 8:16], off[:, 0:8], cnt[:, 0:8], ALU.add))
                c5.link(nc.vector.tensor_tensor(cum, cum, base, ALU.add))
                c5.link(nc.vector.tensor_tensor(tmp, cum, oh, ALU.mult))
                c5.link(nc.vector.tensor_reduce(pos, tmp.rearrange("p (q e) -> p q e", e=E), AX.X, ALU.add))
                c5.link(nc.vector.tensor_tensor(cum.rearrange("p (t n) -> p t n", t=TT),
                                                cum.rearrange("p (t n) -> p t n", t=TT),
                                                off.unsqueeze(1).broadcast_to([P, TT, 16]), ALU.add))
                c5.link(nc.vector.tensor_tensor(tmp, cum, oh, ALU.mult))
                c5.link(nc.vector.tensor_reduce(where, tmp.rearrange("p (q e) -> p q e", e=E), AX.X, ALU.add))
                c5.link(nc.vector.tensor_copy(slot[:, :, :].rearrange("p k t -> p t k"),
                                              where.rearrange("p (t k) -> p t k", k=2)))
                ve.wait_ge(rt_a.sem, rt_a.past(1))
                c5.link(nc.vector.tensor_scalar(one[:, 0:16], gate2[:, :, 1], 1.0, None, ALU.add))
                c5.link(nc.vector.reciprocal(gate2[:, :, 0], one[:, 0:16]))
                c5.link(nc.vector.tensor_tensor(gate2[:, :, 1], gate2[:, :, 1], gate2[:, :, 0], ALU.mult))
                c5.link(nc.vector.tensor_scalar(pos, pos, float(CAP), gates[:, 6:7], ALU.is_le, ALU.mult))
                g2 = gate2[:, :, :].rearrange("p t k -> p (t k)")
                c5.link(nc.vector.tensor_tensor(g2, g2, pos, ALU.mult))
                c5.link(nc.vector.tensor_scalar(ef, iota[:, 0:64], end[:, 0:1], None, ALU.is_ge))
                for e in range(1, E - 1):
                    c5.link(nc.vector.scalar_tensor_tensor(ef, iota[:, 0:64], end[:, e:e + 1], ef, ALU.is_ge, ALU.add))
                c5.link(nc.vector.tensor_copy(eid[:, :], ef))
                ve.sem_inc(routed.sem, 1)
            if phases >= 6:
                def rows_in(j, u):
                    ve.wait_ge(m_xp.sem, m_xp.past(j + 1))
                    nc.vector.tensor_copy(xTb[u], bank(5)[:, 0:D].rearrange("p (c s) -> p c s", c=CH)).then_inc(m_xs.sem, 1)

                def hidden(j):
                    ve.wait_ge(m_tp.sem, m_tp.past(j + 1))
                    ve.wait_ge(m_y.sem, m_y.past(j))
                    nc.vector.tensor_copy(hidT.rearrange("p (v n) -> p v n", v=2), ps[1][:, :, :]).then_inc(m_ts.sem, 1)

                rows_in(0, 0)
                with ve.Fori(0, (MT - 3) // 3) as r:
                    for u in range(3):
                        j = r * 3 + u + 1
                        rows_in(j, (u + 1) % 3)
                        hidden(j - 1)
                for j in range(MT - 2, MT):
                    rows_in(j, j % 3)
                    hidden(j - 1)
                hidden(MT - 1)
                for t in range(TT):
                    if t % 4 == 0:
                        ve.wait_ge(s_ga[t // 4], 8 * 16)
                    nc.vector.scalar_tensor_tensor(x[:, t, :], got[:, 0, t, :], gate2[:, t, 0:1], x[:, t, :], ALU.mult,
                                                   ALU.add).then_inc(cmb.sem, 1)
                for t in range(TT):
                    ve.wait_ge(cmb.sem, cmb.past(t + 1))
                    nc.vector.scalar_tensor_tensor(x[:, t, :], got[:, 1, t, :], gate2[:, t, 1:2], x[:, t, :], ALU.mult,
                                                   ALU.add).then_inc(done[6].sem, 1)
            if phases >= 7:
                ve.wait_ge(s_w[7], 4 * 16)
                ve.wait_ge(done[6].sem, done[6].past(TT))
                gam = bc3[:, 0:1, :].broadcast_to([P, TB, D])
                bet = bc3[:, 1:2, :].broadcast_to([P, TB, D])
                N7 = 2 * 2 + 2 * 2 + 2 * 2 + 2 * 3
                with pairs(ve) as bb:
                    ln(7, bb, used=xtp[7])
                    ch = Chain(ve, dvx[7], N7 * bb)

                    def spread(p):
                        for t in range(TB):
                            ins = nc.vector.bn_stats(st[p][:, t, :], xn[p][:, t, :])
                        ch.link(ins)
                        apart(ve)
                        for t in range(TB):
                            ins = nc.vector.bn_aggr(mv[p][:, t, :], st[p][:, t, :])
                        ins.then_inc(v2_s.sem, 1)

                    def normed(p, count):
                        ve.wait_ge(r2_s.sem, r2_s.past(count))
                        for t in range(TB):
                            ins = nc.vector.tensor_scalar(xn[p][:, t, :], xn[p][:, t, :], mv[p][:, t, 0:1],
                                                          rs[p][:, t:t + 1], ALU.subtract, ALU.mult)
                        ch.link(ins)
                        ch.link(nc.vector.tensor_tensor(xn[p][:, :, :], xn[p][:, :, :], gam, ALU.mult))
                        return nc.vector.tensor_tensor(xn[p][:, :, :], xn[p][:, :, :], bet, ALU.add)

                    for p in range(2):
                        single_soft(7, bb, p)
                    for p in range(2):
                        single_sum(7, bb, p)
                    for p in range(2):
                        ve.wait_ge(pv_p[7].sem, pv_p[7].past(2 * bb + p + 1))
                        for t in range(TB):
                            ins = nc.vector.scalar_tensor_tensor(xn[p][:, t, :], bank(p)[:, t * D:(t + 1) * D],
                                                                 rden[p][:, TB + t:TB + t + 1], xn[p][:, t, :],
                                                                 ALU.mult, ALU.add)
                        ch.link(ins)
                        spread(p)
                    for p in range(2):
                        normed(p, 4 * bb + p + 1).then_inc(x7_s.sem, 1)
                    for p in range(2):
                        ve.wait_ge(f7_p.sem, f7_p.past(2 * bb + p + 1))
                        ve.wait_ge(x7_s.sem, x7_s.past(2 * bb + p + 1))
                        ch.link(nc.vector.tensor_tensor(xn[p][:, :, :], xn[p][:, :, :],
                                                        bank(4 + p).rearrange("p (t d) -> p t d", t=TB), ALU.add))
                        spread(p)
                    for p in range(2):
                        ch.link(normed(p, 4 * bb + 2 + p + 1))
                        for t in range(TB):
                            residual(7, bb, p, t, xn[p][:, t, :], gates[:, 3:4])

                    assert ch.n == N7, ch.n
            if phases >= 8:
                c8 = Chain(ve, prep_8)
                ve.wait_ge(done[7].sem, done[7].past(TT))
                c8.link(nc.vector.tensor_scalar(w3f, w3f, 0.0, 2.0, ALU.is_ge, ALU.mult))
                c8.link(nc.vector.tensor_scalar(w3f, w3f, -1.0, None, ALU.add))
                with pairs(ve) as bb:
                    ln(8, bb, used=xtp[8])
                    ch = Chain(ve, dvx[8], 12 * bb)
                    for p in range(2):
                        for t in range(TB):
                            y = xkeep[:, 12 + 2 * p + t, :]
                            ve.wait_ge(f_p[8].sem, f_p[8].past(4 * bb + 2 * p + t + 1))
                            ch.link(nc.vector.tensor_tensor(y, bank(4 + 2 * p + t)[:, 0:D], bc3[:, 2, :], ALU.mult))
                            ch.link(nc.vector.tensor_tensor(y, y, bc3[:, 3, :], ALU.add))
                            ch.link(nc.vector.tensor_scalar(y, y, -100.0, 100.0, ALU.max, ALU.min))
                            residual(8, bb, p, t, y, gates[:, 7:8])

        @block.tensor
        def _(pe):
            pe.wait_ge(s_seeded, 1)

            def turn(n, bb):
                for p in range(2):
                    pe.wait_ge(nrm[n].sem, nrm[n].past(2 * bb + p + 1))
                    pe.wait_ge(done[n].sem, done[n].past(4 * bb))
                    for c in range(CH):
                        for t in range(TB):
                            ins = nc.tensor.transpose(bank(p)[:, c * S + t * P:c * S + (t + 1) * P],
                                                      xn[p][:, t, c * P:(c + 1) * P], ident[:, :])
                    ins.then_inc(xtp[n].sem, 1)

            pe.wait_ge(s_cst, 7 * 16)
            pe.wait_ge(s_ctx, 16)
            for c in range(CH):
                for h in range(2):
                    for b in range(4):
                        ins = nc.tensor.transpose(bank(2 * c + h)[:, b * KEYS:(b + 1) * KEYS],
                                                  ctxn[:, 4 * h + b, c * P:(c + 1) * P], ident[0:KEYS, 0:KEYS])
                    ins.then_inc(s_ctp.sem, 1)
            pe.wait_ge(s_cta.sem, s_cta.past(4))
            pe.wait_ge(s_set.sem, s_set.past(3))
            for j in range(2 * GR):
                nc.tensor.matmul(bank(j)[:, 0:HALF], fmw[:, j // 2 % 2, :],
                                 ctxT[:, j // 4, (j % 2) * HALF:(j % 2 + 1) * HALF],
                                 start=True, stop=True).then_inc(prep_p[0].sem, 1)
            pe.wait_ge(prep_a[0].sem, prep_a[0].past(8))
            for b in range(B):
                for g in range(GR):
                    ins = nc.tensor.transpose(bank(b)[0:KEYS, g * P:(g + 1) * P], kall[:, g, b * KEYS:(b + 1) * KEYS],
                                              ident[:, :])
                ins.then_inc(prep_p[0].sem, 1)
            pe.wait_ge(prep_v[0].sem, prep_v[0].past(8))
            pe.wait_ge(s_setp.sem, s_setp.past(2))

            def heads(n, bb):
                top = n == 4
                vd = 16 if top else 32
                w = HG * vd
                lag = 1 if top else 0
                turn(n, bb)
                for p in range(2):
                    pe.wait_ge(xts[n].sem, xts[n].past(2 * bb + p + 1))
                    if n == 0:
                        for g in range(GR):
                            ins = nc.tensor.matmul(ps[1 + p][:, g // 2, (g % 2) * S:(g % 2 + 1) * S], fmw[:, g % 2, :],
                                                   xnT[p][:, g // 2, :], start=True, stop=True)
                    else:
                        for m in range(CH):
                            for c in range(CH):
                                ins = nc.tensor.matmul(bank(2 + p)[:, m * S:(m + 1) * S], w2q[:, c, m * P:(m + 1) * P],
                                                       xnT[p][:, c, :], start=c == 0, stop=c == CH - 1)
                    ins.then_inc(q_p[n].sem, 1)
                vv = vall[:, 0:B * HEADS * (vd + 1)].rearrange("p (b h e) -> p b h e", b=B, h=HEADS)
                for s in range(ITEMS + 3 + lag):
                    if s < ITEMS:
                        i, g, u = s, s // 2, s % 2
                        if s == 0:
                            pe.wait_ge(q_s[n].sem, q_s[n].past((4 if top else 2) * (bb + 1) - (0 if True else 0)))
                            pe.wait_ge(kb_s[n].sem, kb_s[n].past(2 * bb + 2))
                        if s >= 2:
                            read = act[n] if top else sc_r[n]
                            pe.wait_ge(read.sem, read.past(ITEMS * bb + i - 1))
                        for t in range(TB):
                            ins = nc.tensor.matmul(ps[u][:, t, 0:GK], wk[u][:, g // 2 if top else g, t * P:(t + 1) * P],
                                                   kb[u][:, g, :], start=True, stop=True)
                        ins.then_inc(sc_p[n].sem, 1)
                    i = s - 1 - lag
                    if 0 <= i < ITEMS:
                        pe.wait_ge(ex_s[n].sem, ex_s[n].past(ITEMS * bb + i + 1))
                        pe.wait_ge(pt_s[n].sem, pt_s[n].past(ITEMS * bb + i))
                        for h in range(HG):
                            for t in range(TB):
                                at = (h % 2) * S + t * P
                                ins = nc.tensor.transpose(ps[2][0:KEYS, h // 2, at:at + P],
                                                          pr[i % 2][:, t, h * KEYS:(h + 1) * KEYS], ident[:, :])
                        ins.then_inc(pt_p[n].sem, 1)
                    i = s - 2 - lag
                    if 0 <= i < ITEMS:
                        pe.wait_ge(pt_s[n].sem, pt_s[n].past(ITEMS * bb + i + 1))
                        pe.wait_ge(o_s[n].sem, o_s[n].past(ITEMS * bb + i))
                        for t in range(TB):
                            for h in range(HG):
                                j = t * HG + h
                                ins = nc.tensor.matmul(bank(6)[:, j * (vd + 1):(j + 1) * (vd + 1)],
                                                       pt[i % 2][:, h * S + t * P:h * S + (t + 1) * P],
                                                       vv[:, 2 * bb + i % 2, i // 2 * HG + h, :], start=True, stop=True)
                        ins.then_inc(pv_p[n].sem, 1)
                    i = s - 3 - lag
                    if 0 <= i < ITEMS:
                        pe.wait_ge(o_s[n].sem, o_s[n].past(ITEMS * bb + i + 1))
                        pe.wait_ge(ot_s[n].sem, ot_s[n].past(ITEMS * bb + i))
                        apart(pe)
                        for t in range(TB):
                            ins = nc.tensor.transpose(bank(7)[0:w, t * P:(t + 1) * P], osb[i % 2][:, t, 0:w],
                                                      ident[:, :])
                        ins.then_inc(ot_p[n].sem, 1)
                pe.wait_ge(ot_s[n].sem, ot_s[n].past(ITEMS * bb + ITEMS))
                wo = w2o if top else fcw
                for p in range(2):
                    for t in range(TB):
                        for g in range(GR):
                            nc.tensor.matmul(bank(2 * p + t)[:, 0:D], oT[p][0:w, g, t * P:(t + 1) * P], wo[:, g, :],
                                             start=g == 0, stop=False)
                        nc.tensor.matmul(bank(2 * p + t)[:, 0:D], ones[0:1, :], rows[0:1, 2 if top else 0, :],
                                         start=False, stop=True).then_inc(f_p[n].sem, 1)

            pe.wait_ge(s_w[0], 2 * 16)
            with pairs(pe) as bb:
                heads(0, bb)

            def plain(n, bb, w):
                turn(n, bb)
                for p in range(2):
                    pe.wait_ge(xts[n].sem, xts[n].past(2 * bb + p + 1))
                    for t in range(TB):
                        for c in range(CH):
                            ins = nc.tensor.matmul(bank(4 + 2 * p + t)[:, 0:D], xnT[p][:, c, t * P:(t + 1) * P],
                                                   w[:, c, :], start=c == 0, stop=c == CH - 1)
                        ins.then_inc(f_p[n].sem, 1)

            if phases >= 1:
                pe.wait_ge(done[0].sem, done[0].past(TT))
                pe.wait_ge(prep_v[1].sem, prep_v[1].past(2))
                with pairs(pe) as bb:
                    plain(1, bb, sgw)

            def keys(n, wkey):
                for j in range(4):
                    m, h = j // 2, j % 2
                    for c in range(CH):
                        ins = nc.tensor.matmul(bank(j)[:, 0:HALF], wkey[:, c, m * P:(m + 1) * P],
                                               ctxT[:, c, h * HALF:(h + 1) * HALF], start=c == 0, stop=c == CH - 1)
                    ins.then_inc(prep_p[n].sem, 1)

            def values(n, wval, bias):
                for b in range(B):
                    dst = bank(4 + b // 2)[0:KEYS, (b % 2) * D:(b % 2 + 1) * D]
                    for c in range(CH):
                        nc.tensor.matmul(dst, ctxT[:, c, b * KEYS:(b + 1) * KEYS], wval[:, c, :], start=c == 0,
                                         stop=False)
                    ins = nc.tensor.matmul(dst, ones[0:1, 0:KEYS], rows[0:1, bias, :], start=False, stop=True)
                    if b % 2:
                        ins.then_inc(prep_p[n].sem, 1)

            def single(n, bb, keyT, val):
                nk = 4 if n == 2 else 2
                for p in range(2):
                    q = wk[p] if n == 2 else xnT[p]
                    if n == 2:
                        pe.wait_ge(q_s[2].sem, q_s[2].past(4 * bb + 2 * p + 2))
                    for t in range(TB):
                        for m in range(CH):
                            ins = nc.tensor.matmul(bank(4 + p)[:, t * KEYS:(t + 1) * KEYS], q[:, m, t * P:(t + 1) * P],
                                                   keyT[:, m, bass.ds((2 * bb + p) * KEYS, KEYS)],
                                                   start=m == 0, stop=m == CH - 1)
                    ins.then_inc(sc_p[n].sem, 1)
                for p in range(2):
                    pe.wait_ge(ex_s[n].sem, ex_s[n].past(2 * bb + p + 1))
                    pe.wait_ge(pt_s[n].sem, pt_s[n].past(2 * bb))
                    for t in range(TB):
                        ins = nc.tensor.transpose(bank(6 + p)[0:KEYS, t * P:(t + 1) * P],
                                                  pr[p][:, t, 0:KEYS], ident[:, :])
                    ins.then_inc(pt_p[n].sem, 1)
                for p in range(2):
                    pe.wait_ge(pt_s[n].sem, pt_s[n].past(2 * bb + p + 1))
                    for t in range(TB):
                        ins = nc.tensor.matmul(bank(p)[:, t * D:(t + 1) * D], pt[p][:, t * P:(t + 1) * P],
                                               val(2 * bb + p), start=True, stop=True)
                    ins.then_inc(pv_p[n].sem, 1)

            if phases >= 2:
                pe.wait_ge(done[1].sem, done[1].past(TT))
                pe.wait_ge(s_w[2], 3 * 16)
                keys(2, w1k)
                values(2, w1v, 1)
                pe.wait_ge(prep_a[2].sem, prep_a[2].past(4))
                pe.wait_ge(prep_v[2].sem, prep_v[2].past(4))
                with pairs(pe) as bb:
                    turn(2, bb)
                    for p in range(2):
                        pe.wait_ge(xts[2].sem, xts[2].past(2 * bb + p + 1))
                        for m in range(CH):
                            for c in range(CH):
                                ins = nc.tensor.matmul(bank(2 + p)[:, m * S:(m + 1) * S], w1q[:, c, m * P:(m + 1) * P],
                                                       xnT[p][:, c, :], start=c == 0, stop=c == CH - 1)
                        ins.then_inc(q_p[2].sem, 1)
                    single(2, bb, kall, lambda b: vall[:, bass.ds(b * D, D)])
            if phases >= 3:
                pe.wait_ge(done[2].sem, done[2].past(TT))
                for k in range(2):
                    pe.wait_ge(prep_v[3].sem, prep_v[3].past(1 + 7 * k))
                    nc.tensor.matmul(bank(k)[:, 0:1], ones[:, :], wstat[:, k:k + 1], start=True,
                                     stop=True).then_inc(prep_p[3].sem, 1)
                pe.wait_ge(prep_v[3].sem, prep_v[3].past(16))
                with pairs(pe) as bb:
                    for p in range(2):
                        pe.wait_ge(q_s[3].sem, q_s[3].past(2 * bb + p + 1))
                        pe.wait_ge(done[3].sem, done[3].past(4 * bb))
                        tb = bank(4 + 3 * p).bitcast(bf16)
                        for c in range(CH):
                            for t in range(TB):
                                ins = nc.tensor.transpose(tb[:, c * S + t * P:c * S + (t + 1) * P],
                                                          xq[p][:, t, c * P:(c + 1) * P], identb[:, :])
                        ins.then_inc(xtp[3].sem, 1)
                    for s in range(4 + 2):
                        if s < 4:
                            u = s
                            pe.wait_ge(xts[3].sem, xts[3].past(2 * bb + u // 2 + 1))
                            pe.wait_ge(h_b.sem, h_b.past(4 * bb + max(u - 1, 0)))
                            xT = xnT[u // 2][:, 0, :].bitcast(bf16).rearrange("p (c s) -> p c s", c=CH)
                            for v in range(2):
                                for c in range(CH):
                                    ins = nc.tensor.matmul(ps[u % 2][:, v, :], xT[:, c, (u % 2) * P:(u % 2 + 1) * P],
                                                           tern1[:, c, v * 512:(v + 1) * 512], start=c == 0,
                                                           stop=c == CH - 1)
                            ins.then_inc(h_p.sem, 1)
                        if 1 <= s < 5:
                            u = s - 1
                            pe.wait_ge(h_z.sem, h_z.past(4 * bb + u + 1))
                            pe.wait_ge(ht_s.sem, ht_s.past(4 * bb + u))
                            tb = bank(5).bitcast(bf16)
                            for k in range(FF // P):
                                ins = nc.tensor.transpose(tb[:, k * P:(k + 1) * P], hq[u % 2][:, k * P:(k + 1) * P],
                                                          identb[:, :])
                            ins.then_inc(ht_p.sem, 1)
                        if s >= 2:
                            u = s - 2
                            pe.wait_ge(ht_s.sem, ht_s.past(4 * bb + u + 1))
                            pe.wait_ge(done[3].sem, done[3].past(4 * bb + max(u - 1, 0)))
                            hT = pr[u % 2].rearrange("p t n -> p (t n)")[:, 0:512].bitcast(bf16)
                            for k in range(FF // P):
                                ins = nc.tensor.matmul(bank(6 + u % 2)[:, 0:D], hT[:, k * P:(k + 1) * P],
                                                       tern2[:, k, :], start=k == 0, stop=k == FF // P - 1)
                            ins.then_inc(f_p[3].sem, 1)
            if phases >= 4:
                pe.wait_ge(done[3].sem, done[3].past(TT))
                pe.wait_ge(s_w[4], 5 * 16)
                keys(4, w2k)
                values(4, w2v, 3)
                pe.wait_ge(prep_a[4].sem, prep_a[4].past(4))
                pe.wait_ge(prep_v[4].sem, prep_v[4].past(10))
                with pairs(pe) as bb:
                    heads(4, bb)

            if phases >= 5:
                pe.wait_ge(done[4].sem, done[4].past(TT))
                pe.wait_ge(s_w[5], 16)
                with pairs(pe) as bb:
                    for p in range(2):
                        pe.wait_ge(nrm[5].sem, nrm[5].past(2 * bb + p + 1))
                        pe.wait_ge(xts[5].sem, xts[5].past(2 * bb))
                        for c in range(CH):
                            for t in range(TB):
                                ins = nc.tensor.transpose(bank(p)[:, c * S + t * P:c * S + (t + 1) * P],
                                                          xn[p][:, t, c * P:(c + 1) * P], ident[:, :])
                        ins.then_inc(xtp[5].sem, 1)
                    for p in range(2):
                        pe.wait_ge(xts[5].sem, xts[5].past(2 * bb + p + 1))
                        pe.wait_ge(rt_l.sem, rt_l.past(2 * bb))
                        for t in range(TB):
                            for c in range(CH):
                                ins = nc.tensor.matmul(bank(2 + p)[:, t * E:(t + 1) * E],
                                                       xnT[p][:, c, t * P:(t + 1) * P], rwT[:, c, :], start=c == 0,
                                                       stop=c == CH - 1)
                        ins.then_inc(lg_p.sem, 1)
                pe.wait_ge(rt_v.sem, rt_v.past(2))
                nc.tensor.matmul(bank(0)[:, 0:256], lower[:, :], rt[:, 0:256], start=True, stop=True).then_inc(rt_p.sem, 1)
                nc.tensor.matmul(bank(1)[:, 0:256], ones[:, :], rt[:, 0:256], start=True, stop=True).then_inc(rt_p.sem, 1)
            if phases >= 6:
                pe.wait_ge(routed.sem, routed.past(1))
                pe.wait_ge(s_we, 2 * E * 16)

                def rows_t(j, u, k):
                    pe.wait_ge(s_ld[u], 16 * k + 16)
                    pe.wait_ge(m_xs.sem, m_xs.past(j))
                    for c in range(CH):
                        ins = nc.tensor.transpose(bank(5)[:, c * P:(c + 1) * P], xsb[u][:, c * P:(c + 1) * P],
                                                  ident[:, :])
                    ins.then_inc(m_xp.sem, 1)

                def first(j, u):
                    pe.wait_ge(m_xs.sem, m_xs.past(j + 1))
                    pe.wait_ge(m_g.sem, m_g.past(j))
                    apart(pe)
                    e = pe.value_load(eid[0:1, bass.ds(j, 1)], min_val=0, max_val=E - 1)
                    for v in range(2):
                        for c in range(CH):
                            ins = nc.tensor.matmul(ps[0][:, v, :], xTb[u][:, c, :],
                                                   experts[:, bass.ds(e * EW + (c * FF + v * 512), 512)],
                                                   start=c == 0, stop=c == CH - 1)
                    ins.then_inc(m_h.sem, 1)

                def hidden_t(j):
                    pe.wait_ge(m_g.sem, m_g.past(j + 1))
                    pe.wait_ge(m_ts.sem, m_ts.past(j))
                    hv = hid[:, :, :].rearrange("p c s -> p (c s)")
                    for k in range(FF // P):
                        ins = nc.tensor.transpose(ps[1][:, k // 4, (k % 4) * P:(k % 4 + 1) * P],
                                                  hv[:, k * P:(k + 1) * P], ident[:, :])
                    ins.then_inc(m_tp.sem, 1)

                def second(j):
                    pe.wait_ge(m_ts.sem, m_ts.past(j + 1))
                    pe.wait_ge(m_ys.sem, m_ys.past(j))
                    apart(pe)
                    e = pe.value_load(eid[0:1, bass.ds(j, 1)], min_val=0, max_val=E - 1)
                    for k in range(FF // P):
                        ins = nc.tensor.matmul(bank(4)[:, 0:D], hidT[:, k * P:(k + 1) * P],
                                               experts[:, bass.ds(e * EW + (E * EW + k * D), D)], start=k == 0,
                                               stop=k == FF // P - 1)
                    ins.then_inc(m_y.sem, 1)

                rows_t(0, 0, 0)
                rows_t(1, 1, 0)
                first(0, 0)
                with pe.Fori(0, (MT - 3) // 3) as r:
                    for u in range(3):
                        j = r * 3 + u + 1
                        rows_t(j + 1, (u + 2) % 3, r if u == 0 else r + 1)
                        hidden_t(j - 1)
                        first(j, (u + 1) % 3)
                        second(j - 1)
                for j in range(MT - 2, MT):
                    if j + 1 < MT:
                        rows_t(j + 1, (j + 1) % 3, (j + 1) // 3)
                    hidden_t(j - 1)
                    first(j, j % 3)
                    second(j - 1)
                hidden_t(MT - 1)
                second(MT - 1)
            if phases >= 7:
                pe.wait_ge(done[6].sem, done[6].past(TT))
                pe.wait_ge(s_w[7], 4 * 16)
                with pairs(pe) as bb:
                    turn(7, bb)
                    for p in range(2):
                        pe.wait_ge(xts[7].sem, xts[7].past(2 * bb + p + 1))
                    single(7, bb, ctxT, lambda b: ctxn[:, b, :])
                    for p in range(2):
                        pe.wait_ge(x7_s.sem, x7_s.past(2 * bb + p + 1))
                        for c in range(CH):
                            for t in range(TB):
                                ins = nc.tensor.transpose(bank(p)[:, c * S + t * P:c * S + (t + 1) * P],
                                                          xn[p][:, t, c * P:(c + 1) * P], ident[:, :])
                        ins.then_inc(x7_p.sem, 1)
                    for p in range(2):
                        pe.wait_ge(x7_t.sem, x7_t.past(2 * bb + p + 1))
                        for m in range(CH):
                            for c in range(CH):
                                ins = nc.tensor.matmul(bank(2 + p)[:, m * S:(m + 1) * S], w3a[:, c, m * P:(m + 1) * P],
                                                       xnT[p][:, c, :], start=c == 0, stop=c == CH - 1)
                        ins.then_inc(h7_p.sem, 1)
                    for p in range(2):
                        pe.wait_ge(h7_s.sem, h7_s.past(2 * bb + p + 1))
                        for t in range(TB):
                            dst = bank(4 + p)[:, t * D:(t + 1) * D]
                            for c in range(CH):
                                nc.tensor.matmul(dst, wk[p][:, c, t * P:(t + 1) * P], w3b[:, c, :], start=c == 0,
                                                 stop=False)
                            ins = nc.tensor.matmul(dst, ones[0:1, :], rows[0:1, 4, :], start=False, stop=True)
                        ins.then_inc(f7_p.sem, 1)
            if phases >= 8:
                pe.wait_ge(done[7].sem, done[7].past(TT))
                pe.wait_ge(prep_8.sem, prep_8.past(2))
                with pairs(pe) as bb:
                    plain(8, bb, w3f)


def kernel(**inputs):
    import numpy as np
    import concourse.bacc as bacc
    from concourse import mybir
    from concourse.bass_utils import run_bass_kernel_spmd

    i = {k: np.asarray(v) for k, v in inputs.items()}
    p = np.arange(128)
    fm = i["L0_xattn_fm_w"].T
    fmw = np.zeros((128, 2, 4, 2, 16), fm.dtype)
    for g in range(2):
        for h in range(4):
            for s in range(2):
                fmw[g * 64 + h * 16:g * 64 + h * 16 + 16, g, h, s, :] = fm
    cols = np.zeros((128, 16), np.float32)
    cols[:, 0] = np.tile(i["L0_xattn_fm_b"], 8)
    cols[:, 15] = np.where(p // 16 % 2 == 0, 1.0, -1.0)
    for n, key in ((1, "L1_xattn_bq"), (3, "L1_xattn_bk"), (5, "L2_xattn_wq_b"), (7, "L2_xattn_wk_b"), (9, "L3_xattn_b1")):
        cols[:, n:n + 2] = i[key].reshape(2, 128).T
    hsel = np.zeros((128, 12), np.float32)
    hsel[p, p // 32] = 1.0
    hsel[p, 4 + p // 16] = 1.0
    iota = np.tile(np.arange(64, dtype=np.float32), (128, 1))
    given = {
        "x": i["x"],
        "ctx": i["ctx_1024"][:, ::-1],
        "mask": i["mask_BxS2_bf1"][:, ::-1].reshape(-1).view(np.uint8),
        "g": np.concatenate([i["g_xattn"], i["g_ffn"]]),
        "ident": np.eye(128, dtype=np.float32),
        "lower": np.triu(np.ones((128, 128), np.float32)),
        "iota": iota, "hsel": hsel, "cols": cols,
        "rows": np.stack([i["L0_xattn_fc_b"], i["L1_xattn_bv"], i["L2_xattn_wo_b"], i["L2_xattn_wv_b"],
                          i["L3_xattn_b2"]]),
        "fmw": fmw.reshape(128, 2, 128),
        "fcw": i["L0_xattn_fc_w"].T, "sgw": i["L0_ffn_weight"].T,
        "w1q": i["L1_xattn_Wq"], "w1k": i["L1_xattn_Wk"], "w1v": i["L1_xattn_Wv"],
        "bw1": i["L1_ffn_W1"].T, "bw2": i["L1_ffn_W2"].T, "bb1": i["L1_ffn_b1"], "bb2": i["L1_ffn_b2"],
        "w2q": i["L2_xattn_wq_w"].T, "w2k": i["L2_xattn_wk_w"].T, "w2v": i["L2_xattn_wv_w"].T,
        "w2o": i["L2_xattn_wo_w"].T, "rw": i["L2_ffn_router_w"].T,
        "ew1": i["L2_ffn_w1"], "ew2": i["L2_ffn_w2"],
        "w3a": i["L3_xattn_W1"], "w3b": i["L3_xattn_W2"],
        "bc3": np.stack([i["L3_xattn_gamma"], i["L3_xattn_beta"], i["L3_ffn_scale"], i["L3_ffn_bias"]]),
        "w3f": i["L3_ffn_weights"].T,
    }
    nc = bacc.Bacc("TRN2", target_bir_lowering=False, num_devices=1)
    arrays, aps = {}, {}
    for key, v in given.items():
        v = np.ascontiguousarray(v)
        arrays["in_" + key] = v
        aps[key] = nc.dram_tensor("in_" + key, v.shape, mybir.dt.from_np(v.dtype), kind="ExternalInput").ap()
    res = nc.dram_tensor("out_0", (B, S, D), mybir.dt.float32, kind="ExternalOutput").ap()
    build(nc, aps, res, PHASES)
    r = run_bass_kernel_spmd(nc, [arrays], core_ids=[0])
    return r.results[0]["out_0"]


PHASES = 8
```

```python
B, S, D = 8, 256, 256
P = 128
CH = D // P
TT = B * S // P
TB = S // P
KEYS = 77
NK = B * KEYS
HALF = NK // 2
HEADS = 16
HG = 4
GR = HEADS // HG
GK = HG * KEYS
FF = 4 * D
E = 8
CAP = int(1.25 * B * S / E * 2)
DROP = KEYS - 64
MT = B * S * 2 // P + E - 1
PAIRS = B // 2
ITEMS = 2 * GR
BIG = 1e38
MAGIC = 12582912.0
QB = 127.0
EPS_Q = 1e-5


def build(nc, a, out, phases=8):
    from concourse import mybir
    import concourse.bass as bass
    from contextlib import ExitStack

    f32, bf16, i32, u32, u8 = (mybir.dt.float32, mybir.dt.bfloat16, mybir.dt.int32,
                               mybir.dt.uint32, mybir.dt.uint8)
    ALU = mybir.AluOpType
    ACT = mybir.ActivationFunctionType
    AX = mybir.AxisListType
    ctx = ExitStack()
    with ctx:
        def sb(name, shape, dt=f32):
            return ctx.enter_context(nc.sbuf_tensor(name, shape, dt))

        def sem(name):
            return ctx.enter_context(nc.semaphore(name))

        seeds = []

        def counted(name):
            s = sem(name)
            seeds.append(s)
            return Share(s, 0)

        class Share:

            def __init__(self, s, base):
                self.sem, self.base = s, base

            def past(self, n):
                return n + (self.base + 1)

        def shared(name, per_phase):
            s, base, out = counted(name).sem, 0, {}
            for n, k in per_phase.items():
                out[n] = Share(s, base)
                base += k
            return out

        class Chain:

            def __init__(self, eng, s, base=0):
                self.eng, self.s, self.base, self.n = eng, s, base, 0

            def step(self, ins):
                self.n += 1
                ins.then_inc(self.s.sem, 1)

            def settle(self):
                self.eng.wait_ge(self.s.sem, self.s.past(self.base + self.n))

            def link(self, ins):
                self.step(ins)
                self.settle()

        def apart(eng):
            eng.sem_inc(s_apart, 1)

        x = sb("x", [P, TT, D])
        xkeep = sb("xkeep", [P, TT, D])
        experts = sb("experts", [P, 2 * E * CH * FF])
        EW = CH * FF
        EARLY = 5
        arena_at = [EARLY * EW]

        def arena(n, parts=P):
            at = arena_at[0]
            arena_at[0] += n
            assert arena_at[0] <= 2 * E * EW
            return experts[0:parts, at:at + n]

        fcw = arena(4 * D).rearrange("p (c n) -> p c n", c=4)
        sgw = arena(CH * D).rearrange("p (c n) -> p c n", c=CH)
        w1q = arena(CH * D).rearrange("p (c n) -> p c n", c=CH)
        w1k = arena(CH * D).rearrange("p (c n) -> p c n", c=CH)
        w1v = arena(CH * D).rearrange("p (c n) -> p c n", c=CH)
        w2q = arena(CH * D).rearrange("p (c n) -> p c n", c=CH)
        w2k = arena(CH * D).rearrange("p (c n) -> p c n", c=CH)
        w2v = arena(CH * D).rearrange("p (c n) -> p c n", c=CH)
        w2o = arena(CH * D).rearrange("p (c n) -> p c n", c=CH)
        gb = arena(2 * D).rearrange("p (c n) -> p c n", c=2)
        tern1 = arena(EW // 2).bitcast(bf16).rearrange("p (c n) -> p c n", c=CH)
        tern2 = arena(EW // 2).bitcast(bf16).rearrange("p (c n) -> p c n", c=FF // P)
        kall = arena(GR * NK).rearrange("p (g n) -> p g n", g=GR)
        vall = arena(B * HEADS * 33, KEYS)
        kb = [arena(GR * GK).rearrange("p (g n) -> p g n", g=GR) for _ in range(2)]
        pr = [arena(TB * GK).rearrange("p (t n) -> p t n", t=TB) for _ in range(2)]
        dd = [arena(TB * GK).rearrange("p (t n) -> p t n", t=TB) for _ in range(2)]
        fmw = arena(2 * P).rearrange("p (g n) -> p g n", g=2)
        b1bc = arena(FF)
        b2bc = arena(D)
        osb = [arena(TB * P).rearrange("p (t n) -> p t n", t=TB) for _ in range(2)]
        xkeep_tmp = kall[:, :, :].rearrange("p g n -> p (g n)")
        vtmp = xkeep_tmp[:, 0:EW]
        hmag = [xkeep[:, 4 * u:4 * u + 4, :].rearrange("p t d -> p (t d)") for u in range(2)]
        kb0, kb1 = (k[:, :, :].rearrange("p g n -> p (g n)") for k in kb)
        xq = [k[:, 0:S].bitcast(bf16).rearrange("p (t d) -> p t d", t=TB) for k in (kb0, kb1)]
        hq = [k[:, S:S + FF // 2].bitcast(bf16) for k in (kb0, kb1)]
        stage1 = xkeep[:, 0:8, :].rearrange("p t d -> p (t d)")
        stage2 = xkeep[:, 8:16, :].rearrange("p t d -> p (t d)")

        ident = sb("ident", [P, P])
        identb = sb("identb", [P, P], bf16)
        ones = sb("ones", [P, P])
        ctxT = sb("ctxT", [P, CH, NK])
        ctxn = sb("ctxn", [KEYS, B, D])
        xn = [sb(f"xn{i}", [P, TB, D]) for i in range(2)]
        xnT = [sb(f"xnT{i}", [P, CH, S]) for i in range(2)]
        wk = [sb(f"wk{i}", [P, 4, S]) for i in range(2)]
        pt = [sb(f"pt{i}", [KEYS, HG * S]) for i in range(2)]
        oT = [xkeep[:, 8 + 4 * i:12 + 4 * i, :] for i in range(2)]
        row0 = sb("row0", [P, P])
        rows = sb("rows", [1, 3, D])
        cols = sb("cols", [P, 16])
        gates = sb("gates", [P, 2 * 4])
        graw = sb("graw", [P, 2 * 4])
        st = [sb(f"st{i}", [P, TB, 6]) for i in range(2)]
        mv = [sb(f"mv{i}", [P, TB, 2]) for i in range(2)]
        rs = [sb(f"rs{i}", [P, TB]) for i in range(2)]
        mhalf = sb("mhalf", [P, TB])
        mone = sb("mone", [P, TB])
        sm = sb("sm", [P, 2, 4, 8])
        m8 = [sb(f"m8{i}", [P, 8, 8]) for i in range(2)]
        m8b = [sb(f"m8b{i}", [P, 8, 8]) for i in range(2)]
        rden = [sb(f"rden{i}", [P, 8]) for i in range(2)]
        mx = [sb(f"mx{i}", [P, 8]) for i in range(2)]
        hsel = sb("hsel", [P, 4 + 8])
        mrow8 = sb("mrow8", [P, NK], u8)
        mrow = arena(NK)
        mcol = sb("mcol", [P, B])
        wstat = sb("wstat", [P, 8])
        w3a, w3b, w3f = (xkeep[:, 2 * k:2 * k + 2, :] for k in range(3))
        bc3 = xkeep[:, 6:10, :]
        rwT = sb("rwT", [P, CH, E])
        lg = [sb(f"lg{i}", [P, TB, E]) for i in range(2)]
        ix = [sb(f"ix{i}", [P, TB, 8], u32) for i in range(2)]
        topv = sb("topv", [P, TT, 2])
        topi = sb("topi", [P, TT, 2])
        lower = sb("lower", [P, P])
        iota = sb("iota", [P, 64])
        gate2 = sb("gate2", [P, TT, 2])
        slot = sb("slot", [P, 2, TT], i32)
        eid = sb("eid", [P, 64], i32)
        zeros = arena(D)
        xsb = [xn[0][:, 0, :], xn[0][:, 1, :], xn[1][:, 0, :]]
        xTb = [v.rearrange("p (c s) -> p c s", c=CH) for v in (xnT[0][:, 0, :], xnT[0][:, 1, :], xnT[1][:, 0, :])]
        hid = wk[0]
        hidT = wk[1][:, :, :].rearrange("p c s -> p (c s)")
        ysb = [xkeep[:, 10 + u, :] for u in range(3)]
        got = experts[:, 0:2 * TT * D].rearrange("p (k t d) -> p k t d", k=2, t=TT)
        rt = experts[:, E * EW:E * EW + 4096]
        ps = [ctx.enter_context(nc.psum_tensor(f"ps{i}", [P, 2, 512], f32)) for i in range(4)]

        def bank(i):
            return ps[i // 2][:, i % 2, :]

        xs_d = nc.dram_tensor("expert_in", [MT * P, D], f32).ap()
        ys_d = nc.dram_tensor("expert_out", [MT * P, D], f32).ap()

        L = (0, 1, 2, 3, 4, 5, 6, 7, 8)
        SC = B * GR
        NORMS = (0, 1, 2, 3, 4, 5, 7, 8)
        s_x = sem("s_x")
        s_ctx = sem("s_ctx")
        s_cst = sem("s_cst")
        s_w = {n: sem(f"s_w{n}") for n in (0, 1, 2, 3, 4, 5, 7)}
        s_we = sem("s_we")
        s_out = sem("s_out")
        s_seeded = sem("s_seeded")
        s_apart = sem("s_apart")
        s_set = counted("s_set")
        s_setp = counted("s_setp")
        s_ctp = counted("s_ctp")
        s_cta = counted("s_cta")
        s_gate = counted("s_gate")
        stat = shared("stat", {n: TT for n in NORMS})
        rstd = shared("rstd", {n: B for n in NORMS})
        nrm = shared("nrm", {n: B for n in NORMS})
        xtp = shared("xtp", {n: B for n in NORMS})
        xts = shared("xts", {n: B for n in NORMS})
        done = shared("done", {n: 0 if n == 5 else TT for n in L})
        pool = shared("pool", {n: B for n in NORMS})
        dve = shared("dve", {n: TT for n in NORMS})
        act = shared("act", {0: SC, 2: B, 4: SC, 7: B})
        prep_p = {n: counted(f"prep_p{n}") for n in (0, 2, 3, 4)}
        prep_a = {n: counted(f"prep_a{n}") for n in (0, 2, 4)}
        prep_v = {n: counted(f"prep_v{n}") for n in (0, 1, 2, 3, 4)}
        q_p = shared("q_p", {0: B, 2: B, 4: B, 7: B})
        q_s = shared("q_s", {0: B, 2: 2 * B, 3: B, 4: 2 * B, 7: B})
        xb_s = shared("xb_s", {0: PAIRS, 3: B, 4: PAIRS})
        kb_s = shared("kb_s", {0: B, 4: B})
        sc_p = shared("sc_p", {0: SC, 2: B, 4: SC, 7: B})
        sc_r = shared("sc_r", {0: SC, 2: B, 4: SC, 7: B})
        sc_d = counted("sc_d")
        tk_s = counted("tk_s")
        ex_s = shared("ex_s", {0: SC, 2: B, 4: SC, 7: B})
        pt_p = shared("pt_p", {0: SC, 2: B, 4: SC, 7: B})
        pt_s = shared("pt_s", {0: SC, 2: B, 4: SC, 7: B})
        pv_p = shared("pv_p", {0: SC, 2: B, 4: SC, 7: B})
        o_s = shared("o_s", {0: SC, 4: SC})
        ot_p = shared("ot_p", {0: SC, 4: SC // 2})
        ot_s = shared("ot_s", {0: SC, 4: SC // 2})
        f_p = shared("f_p", {n: TT for n in (0, 1, 3, 4, 8)})
        g_s = counted("g_s")
        hq_s = counted("hq_s")
        ht_p = counted("ht_p")
        ht_s = counted("ht_s")
        h_p = counted("h_p")
        h_b = counted("h_b")
        h_r = counted("h_r")
        s_ab = counted("s_ab")
        tk_r = counted("tk_r")
        h_z = counted("h_z")
        q_m = counted("q_m")
        q_c = counted("q_c")
        q_r = counted("q_r")
        h_m = counted("h_m")
        h_c = counted("h_c")
        h_w = counted("h_w")
        s_rd = shared("s_rd", {0: SC, 2: 2 * B, 4: SC, 7: 2 * B})
        keep_s = counted("keep_s")
        lg_p = counted("lg_p")
        rt_v = counted("rt_v")
        rt_a = counted("rt_a")
        rt_p = counted("rt_p")
        routed = counted("routed")
        s_zero = sem("s_zero")
        s_sc = sem("s_sc")
        s_ld = [sem(f"s_ld{u}") for u in range(3)]
        s_st = [counted(f"s_st{u}") for u in range(3)]
        s_ga = [sem(f"s_ga{u}") for u in range(PAIRS)]
        m_xp = counted("m_xp")
        m_xs = counted("m_xs")
        m_h = counted("m_h")
        m_g = counted("m_g")
        m_tp = counted("m_tp")
        m_ts = counted("m_ts")
        m_y = counted("m_y")
        m_ys = counted("m_ys")
        v2_s = counted("v2_s")
        r2_a = counted("r2_a")
        r2_s = counted("r2_s")
        x7_s = counted("x7_s")
        x7_p = counted("x7_p")
        x7_t = counted("x7_t")
        h7_p = counted("h7_p")
        h7_s = counted("h7_s")
        f7_p = counted("f7_p")
        prep_8 = counted("prep_8")
        rt_l = counted("rt_l")
        rt_m = counted("rt_m")
        rt_i = counted("rt_i")
        rt_c = counted("rt_c")
        cmb = counted("cmb")
        dvx = {n: counted(f"dvx{n}") for n in (2, 3, 7, 8)}

        block = ctx.enter_context(nc.Block())

        def pairs(eng):
            return eng.Fori(0, PAIRS)

        def least(n):
            return max(n, 0) if isinstance(n, int) else n

        def bit_steps(eng, step):
            for k in range(-4, 3):
                step(0, k)
            with eng.Fori(0, 2) as r:
                for k in range(3, 7):
                    step(r, k)
            for k in range(11, TT + 3):
                step(0, k)

        def late(n):
            return E * EW + n * EW

        @block.sync
        def _(sp):
            for s in seeds:
                sp.sem_inc(s, 1)
            sp.sem_inc(s_seeded, 1)
            xv = a["x"].rearrange("b (t p) d -> p (b t) d", p=P)
            sp.dma_start(ctxn[:, :, :], a["ctx"].rearrange("b k d -> k b d")).then_inc(s_ctx, 16)
            for dst, key in ((ident, "ident"), (lower, "lower"), (iota, "iota"), (hsel, "hsel"), (cols, "cols")):
                sp.dma_start(dst[:, :], a[key]).then_inc(s_cst, 16)
            sp.dma_start(graw[:, :], a["g"].partition_broadcast(P)).then_inc(s_cst, 16)
            sp.dma_start(rows[:, :, :], a["rows"].rearrange("(o r) d -> o r d", o=1)).then_inc(s_cst, 16)
            sp.dma_start(row0[:, :], a["row0"]).then_inc(s_cst, 16)
            sp.dma_start(fmw[:, :, :], a["fmw"]).then_inc(s_w[0], 16)
            sp.dma_start(gb[:, :, :], a["outb"].partition_broadcast(P)).then_inc(s_w[0], 16)
            sp.dma_start(x[:, :, :], xv).then_inc(s_x, 16)
            sp.dma_start(fcw[:, :, :], a["fcw"].rearrange("(c p) n -> p c n", p=P)).then_inc(s_w[0], 16)
            sp.dma_start(sgw[:, :, :], a["sgw"].rearrange("(c p) n -> p c n", p=P)).then_inc(s_w[1], 16)
            for w, key in ((w1q, "w1q"), (w1k, "w1k"), (w1v, "w1v")):
                sp.dma_start(w[:, :, :], a[key].rearrange("(c p) n -> p c n", p=P)).then_inc(s_w[2], 16)
            sp.dma_start(stage1.rearrange("p (c n) -> p c n", c=CH), a["bw1"].rearrange("(c p) n -> p c n", p=P)).then_inc(s_w[3], 16)
            sp.dma_start(b1bc, a["bb1"].partition_broadcast(P)).then_inc(s_w[3], 16)
            sp.dma_start(b2bc, a["bb2"].partition_broadcast(P)).then_inc(s_w[3], 16)
            for w, key in ((w2q, "w2q"), (w2k, "w2k"), (w2v, "w2v")):
                sp.dma_start(w[:, :, :], a[key].rearrange("(c p) n -> p c n", p=P)).then_inc(s_w[4], 16)
            sp.dma_start(w2o[:, :, :], a["w2o"].rearrange("(c p) n -> p c n", p=P)).then_inc(s_w[4], 16)
            sp.dma_start(mrow8[:, :], a["mask"].partition_broadcast(P)).then_inc(s_w[4], 16)
            sp.dma_start(rwT[:, :, :], a["rw"].rearrange("(c p) n -> p c n", p=P)).then_inc(s_w[5], 16)
            if phases >= 3:
                sp.wait_ge(done[0].sem, done[0].past(TT))
                sp.dma_start(stage2.rearrange("p (c n) -> p c n", c=FF // P),
                             a["bw2"].rearrange("(c p) n -> p c n", p=P)).then_inc(s_w[3], 16)
            sp.wait_ge(s_setp.sem, s_setp.past(3))
            if phases >= 5:
                sp.dma_start(xs_d.rearrange("(j p) d -> p j d", p=P),
                             zeros.unsqueeze(1).broadcast_to([P, MT, D])).then_inc(s_zero, 16)
            if phases >= 6:
                def first(e):
                    sp.dma_start(experts[:, e * EW:(e + 1) * EW].rearrange("p (c n) -> p c n", c=CH),
                                 a["ew1"][e].rearrange("(c p) n -> p c n", p=P)).then_inc(s_we, 16)

                def second(e):
                    sp.dma_start(experts[:, late(e):late(e) + EW].rearrange("p (c n) -> p c n", c=FF // P),
                                 a["ew2"][e].rearrange("(c p) n -> p c n", p=P)).then_inc(s_we, 16)

                for e in range(EARLY):
                    first(e)
                sp.wait_ge(done[4].sem, done[4].past(TT))
                sp.wait_ge(s_zero, 16)
                for e in range(EARLY, E):
                    first(e)
                for e in range(2, E):
                    second(e)
                sp.wait_ge(routed.sem, routed.past(1))
                for e in range(2):
                    second(e)
                sp.wait_ge(s_sc, 2 * TT * 16)
                for w, key in ((w3a, "w3a"), (w3b, "w3b"), (w3f, "w3f")):
                    sp.dma_start(w, a[key].rearrange("(c p) n -> p c n", p=P)).then_inc(s_w[7], 16)
                sp.dma_start(bc3, a["bc3"].partition_broadcast(P)).then_inc(s_w[7], 16)

                def load(j, u, k):
                    sp.dma_start(xsb[u], xs_d[bass.ds(j * P, P), :]).then_inc(s_ld[u], 16)

                def store(j, u):
                    sp.wait_ge(m_ys.sem, m_ys.past(j + 1))
                    sp.dma_start(ys_d[bass.ds(j * P, P), :], ysb[u]).then_inc(s_st[u].sem, 16)

                for j in range(3):
                    load(j, j, 0)
                with sp.Fori(0, MT // 3 - 1) as r:
                    for u in range(3):
                        j = r * 3 + u
                        sp.wait_ge(m_xp.sem, m_xp.past(j + 1))
                        load(j + 3, u, r)
                        store(j, u)
                for j in range(MT - 3, MT):
                    store(j, j % 3)
            last = min(phases, 8)
            if last == 8:
                for b in range(B):
                    sp.wait_ge(done[8].sem, done[8].past(TB * (b + 1)))
                    sp.dma_start(out[b].rearrange("(t p) d -> p t d", p=P), x[:, TB * b:TB * b + TB, :]).then_inc(s_out, 16)
                sp.wait_ge(s_out, 16 * B)
            else:
                sp.wait_ge(done[last].sem, done[last].past(TT))
                sp.dma_start(out.rearrange("b (t p) d -> p (b t) d", p=P), x[:, :, :]).then_inc(s_out, 16)
                sp.wait_ge(s_out, 16)

        @block.gpsimd
        def _(gp):
            gp.wait_ge(s_seeded, 1)

            def ln_rstd(n, bb, eps, per=2, src=None, at=0):
                for p in range(2):
                    gp.wait_ge(stat[n].sem, stat[n].past(4 * bb + 2 * p + 2))
                    gp.wait_ge(nrm[n].sem, nrm[n].past(2 * bb))
                    apart(gp)
                    nc.gpsimd.tensor_scalar(rs[p][:, :], mv[p][:, :, 1], eps, None, ALU.add).then_inc(pool[n].sem, 1)
                    gp.wait_ge(pool[n].sem, pool[n].past(2 * bb + p + 1))
                    nc.gpsimd.tensor_tensor(rs[p][:, :], rs[p][:, :], mhalf[:, :], ALU.pow).then_inc(rstd[n].sem, 1)

            nc.gpsimd.memset(ones[:, :], 1.0).then_inc(s_setp.sem, 1)
            nc.gpsimd.memset(mhalf[:, :], -0.5).then_inc(s_setp.sem, 1)
            nc.gpsimd.memset(zeros, 0.0).then_inc(s_setp.sem, 1)
            nc.gpsimd.memset(mone[:, :], -1.0).then_inc(s_setp.sem, 1)

            def heads_keys(n, bb):
                for p in range(2):
                    b = 2 * bb + p
                    if not (isinstance(bb, int) and bb == 0):
                        gp.wait_ge(sc_p[n].sem, sc_p[n].past(ITEMS * bb - 1 + p))
                    dst = kb[p].rearrange("p g (h k) -> p g h k", h=HG)
                    if n == 0:
                        src = kall[:, :, bass.ds(b * KEYS, KEYS)].unsqueeze(2).broadcast_to([P, GR, HG, KEYS])
                        sel = hsel[:, 0:4].unsqueeze(1).unsqueeze(3).broadcast_to([P, GR, HG, KEYS])
                        nc.gpsimd.tensor_tensor(dst, src, sel, ALU.mult).then_inc(kb_s[n].sem, 1)
                    else:
                        for c in range(CH):
                            d2 = kb[p][:, 2 * c:2 * c + 2, :].rearrange("p g (h k) -> p (g h) k", h=HG)
                            src = kall[:, c, bass.ds(b * KEYS, KEYS)].unsqueeze(1).broadcast_to([P, 8, KEYS])
                            sel = hsel[:, 4:12].unsqueeze(2).broadcast_to([P, 8, KEYS])
                            ins = nc.gpsimd.tensor_tensor(d2, src, sel, ALU.mult)
                        ins.then_inc(kb_s[n].sem, 1)

            def biased(n, bb):
                gp.wait_ge(nrm[n].sem, nrm[n].past(2 * bb + 2))
                rows4 = x[:, bass.ds(4 * bb, 4), :]
                nc.gpsimd.tensor_tensor(rows4, rows4, gb[:, n // 4:n // 4 + 1, :].broadcast_to([P, 4, D]), ALU.add
                                        ).then_inc(xb_s[n].sem, 1)

            def heads(n, bb, ahead):
                if n == 0:
                    biased(n, bb)
                if n == 4:
                    for i in range(ITEMS):
                        u = i % 2
                        gp.wait_ge(tk_s.sem, tk_s.past(ITEMS * bb + i + 1))
                        dv = dd[u].rearrange("p t (h k) -> p t h k", h=HG)
                        mn = mx[u][:, :].rearrange("p (t h) -> p t h", t=TB).unsqueeze(3)
                        nc.gpsimd.tensor_tensor(dv, dv, mn.broadcast_to([P, TB, HG, KEYS]), ALU.subtract
                                                ).then_inc(sc_d.sem, 1)
                        if i == 2:
                            biased(n, bb)
                        if i == 4 and ahead:
                            ln_rstd(n, bb + 1, 1e-5)
                elif ahead:
                    ln_rstd(n, bb + 1, 1e-5)
                if ahead:
                    heads_keys(n, bb + 1)

            gp.wait_ge(prep_a[0].sem, prep_a[0].past(8))
            gp.wait_ge(s_cst, 8 * 16)
            gp.wait_ge(s_setp.sem, s_setp.past(2))
            ln_rstd(0, 0, 1e-5)
            heads_keys(0, 0)
            gp.wait_ge(s_set.sem, s_set.past(5))
            with gp.Fori(0, PAIRS - 1) as bb:
                heads(0, bb, True)
            heads(0, PAIRS - 1, False)
            if phases >= 1:
                with pairs(gp) as bb:
                    ln_rstd(1, bb, 1e-5)
            if phases >= 2:
                with pairs(gp) as bb:
                    ln_rstd(2, bb, 1e-5)
            if phases >= 3:
                gp.wait_ge(s_setp.sem, s_setp.past(4))
                gp.wait_ge(prep_v[3].sem, prep_v[3].past(16))

                def bit_rstd(b, p):
                    gp.wait_ge(stat[3].sem, stat[3].past(2 * b + 2))
                    apart(gp)
                    nc.gpsimd.tensor_scalar(rs[p][:, :], mv[p][:, :, 1], 1e-5, None, ALU.add).then_inc(pool[3].sem, 1)
                    gp.wait_ge(pool[3].sem, pool[3].past(b + 1))
                    nc.gpsimd.tensor_tensor(rs[p][:, :], rs[p][:, :], mhalf[:, :], ALU.pow).then_inc(rstd[3].sem, 1)

                def bit_scales(b, p):
                    big, fac = sm[:, p, 0, 0:TB], sm[:, p, 1, 0:TB]
                    gp.wait_ge(q_m.sem, q_m.past(b + 1))
                    apart(gp)
                    nc.gpsimd.tensor_scalar(fac, big, EPS_Q, 1.0 / QB, ALU.max, ALU.mult).then_inc(q_c.sem, 1)
                    nc.gpsimd.tensor_scalar(big, big, EPS_Q, wstat[:, 4:5], ALU.max, ALU.mult).then_inc(q_r.sem, 1)
                    gp.wait_ge(q_c.sem, q_c.past(b + 1))
                    nc.gpsimd.tensor_tensor(fac, fac, mone[:, :], ALU.pow).then_inc(q_r.sem, 1)
                    gp.wait_ge(nrm[3].sem, nrm[3].past(b + 1))
                    two = x[:, bass.ds(2 * b, 2), :]
                    nc.gpsimd.tensor_tensor(two, two, b2bc.unsqueeze(1).broadcast_to([P, TB, D]), ALU.add
                                            ).then_inc(xb_s[3].sem, 1)

                def bit_hidden(t, u):
                    big, fac = sm[:, u % 2, 2, u // 2:u // 2 + 1], sm[:, u % 2, 3, u // 2:u // 2 + 1]
                    gp.wait_ge(h_m.sem, h_m.past(t + 1))
                    apart(gp)
                    nc.gpsimd.tensor_scalar(fac, big, EPS_Q, 1.0 / QB, ALU.max, ALU.mult).then_inc(h_c.sem, 1)
                    nc.gpsimd.tensor_scalar(big, big, EPS_Q, wstat[:, 5:6], ALU.max, ALU.mult).then_inc(h_w.sem, 1)
                    gp.wait_ge(h_c.sem, h_c.past(t + 1))
                    nc.gpsimd.tensor_tensor(fac, fac, mone[:, 0:1], ALU.pow).then_inc(h_r.sem, 1)

                def bit_step(r, k):
                    t = 4 * r + k
                    if 1 <= k < TT + 1:
                        bit_hidden(t - 1, (k - 1) % 4)
                    if k % 2 == 0 and (k + 4) // 2 < B:
                        bit_rstd(2 * r + (k + 4) // 2, (k + 4) // 2 % 2)
                    if k % 2 and (k + 3) // 2 < B:
                        bit_scales(2 * r + (k + 3) // 2, (k + 3) // 2 % 2)

                bit_steps(gp, bit_step)
            if phases >= 4:
                gp.wait_ge(prep_a[4].sem, prep_a[4].past(4))
                ln_rstd(4, 0, 1e-5)
                heads_keys(4, 0)
                with gp.Fori(0, PAIRS - 1) as bb:
                    heads(4, bb, True)
                heads(4, PAIRS - 1, False)
            if phases >= 5:
                with pairs(gp) as bb:
                    ln_rstd(5, bb, 1e-5)
                gp.wait_ge(routed.sem, routed.past(1))
                gp.wait_ge(keep_s.sem, keep_s.past(B))
                gp.wait_ge(s_zero, 16)
                for t in range(TT):
                    for k in range(2):
                        gp.indirect_dma_start(xs_d, bass.IndirectOffsetOnAxis(ap=slot[:, k, t:t + 1], axis=0),
                                              xkeep[:, t, :], None).then_inc(s_sc, 16)
            if phases >= 6:
                gp.wait_ge(m_y.sem, m_y.past(MT))
                for u in range(3):
                    gp.wait_ge(s_st[u].sem, s_st[u].past(MT // 3 * 16))
                for t in range(TT):
                    for k in range(2):
                        gp.indirect_dma_start(got[:, k, t, :], None, ys_d,
                                              bass.IndirectOffsetOnAxis(ap=slot[:, k, t:t + 1], axis=0)
                                              ).then_inc(s_ga[t // 4], 16)
            if phases >= 7:
                with pairs(gp) as bb:
                    ln_rstd(7, bb, 1e-5)
                    for k in range(2):
                        for p in range(2):
                            gp.wait_ge(v2_s.sem, v2_s.past(4 * bb + 2 * k + p + 1))
                            apart(gp)
                            nc.gpsimd.tensor_scalar(rs[p][:, :], mv[p][:, :, 1], 1e-6, None, ALU.add
                                                    ).then_inc(r2_a.sem, 1)
                            gp.wait_ge(r2_a.sem, r2_a.past(4 * bb + 2 * k + p + 1))
                            nc.gpsimd.tensor_tensor(rs[p][:, :], rs[p][:, :], mhalf[:, :], ALU.pow).then_inc(r2_s.sem, 1)
            if phases >= 8:
                with pairs(gp) as bb:
                    ln_rstd(8, bb, 1e-5)

        @block.scalar
        def _(ac):
            ac.wait_ge(s_seeded, 1)

            def copy(dst, src):
                return nc.scalar.activation(dst, src, ACT.Copy)

            def turned(n, bb, used, per):
                for p in range(2):
                    ac.wait_ge(xtp[n].sem, xtp[n].past(2 * bb + p + 1))
                    ac.wait_ge(used.sem, used.past(per * bb))
                    copy(xnT[p][:, :, :].rearrange("p c s -> p (c s)"), bank(p)).then_inc(xts[n].sem, 1)

            ac.wait_ge(s_cst, 8 * 16)
            nc.scalar.activation(gates[:, :], graw[:, :], ACT.Tanh).then_inc(s_gate.sem, 1)
            for c in range(CH):
                for h in range(2):
                    ac.wait_ge(s_ctp.sem, s_ctp.past(2 * c + h + 1))
                    copy(ctxT[:, c, h * HALF:(h + 1) * HALF], bank(2 * c + h)[:, 0:HALF]).then_inc(s_cta.sem, 1)

            ac.wait_ge(s_set.sem, s_set.past(3))
            for j in range(2 * GR):
                ac.wait_ge(prep_p[0].sem, prep_p[0].past(j + 1))
                nc.scalar.activation(kall[:, j // 2, (j % 2) * HALF:(j % 2 + 1) * HALF], bank(j)[:, 0:HALF], ACT.Exp,
                                     bias=cols[:, 0:1]).then_inc(prep_a[0].sem, 1)

            def queries(n, bb):
                for p in range(2):
                    ac.wait_ge(q_p[n].sem, q_p[n].past(2 * bb + p + 1))
                    if n == 0:
                        nc.scalar.activation(wk[p][:, :, :].rearrange("p (u g) s -> p u (g s)", u=2),
                                             ps[1 - p][:, :, :], ACT.Exp, bias=cols[:, 0:1]).then_inc(q_s[n].sem, 1)
                    else:
                        for m in range(CH):
                            nc.scalar.activation(wk[p][:, m, :], bank(2 + p)[:, m * S:(m + 1) * S], ACT.Identity,
                                                 bias=cols[:, 12 + m:13 + m], scale=-0.25).then_inc(q_s[n].sem, 1)

            def heads(n, bb, ahead):
                top = n == 4
                w = 64 if top else P
                lag = 1 if top else 0
                for s in range(ITEMS + 3 + lag):
                    if ahead and s == ITEMS:
                        turned(n, bb + 1, q_p[n], 2)
                    if ahead and s == ITEMS + 1:
                        queries(n, bb + 1)
                    if top and s < ITEMS:
                        ac.wait_ge(sc_p[n].sem, sc_p[n].past(ITEMS * bb + s + 1))
                        nc.scalar.activation(dd[s % 2][:, :, :], ps[s % 2][:, :, 0:GK], ACT.Copy).then_inc(sc_r[n].sem, 1)
                    i = s - lag
                    if 0 <= i < ITEMS:
                        u = i % 2
                        row = pr[u]
                        if top:
                            ac.wait_ge(sc_d.sem, sc_d.past(ITEMS * bb + i + 1))
                            ac.wait_ge(pt_p[n].sem, pt_p[n].past(ITEMS * bb + max(i - 1, 0)))
                            nc.scalar.activation(row[:, :, :], dd[u][:, :, :], ACT.Abs).then_inc(s_ab.sem, 1)
                            ac.wait_ge(s_ab.sem, s_ab.past(ITEMS * bb + i + 1))
                            apart(ac)
                            nc.scalar.activation(row[:, :, :], row[:, :, :], ACT.Exp,
                                                 scale=mcol[:, bass.ds(2 * bb + u, 1)]).then_inc(ex_s[n].sem, 1)
                        else:
                            ac.wait_ge(sc_r[n].sem, sc_r[n].past(ITEMS * bb + i + 1))
                            nc.scalar.activation(row[:, :, :], row[:, :, :], ACT.Exp, scale=1.0 / 16).then_inc(ex_s[n].sem, 1)
                    i = s - 1 - lag
                    if 0 <= i < ITEMS:
                        ac.wait_ge(pt_p[n].sem, pt_p[n].past(ITEMS * bb + i + 1))
                        ac.wait_ge(pv_p[n].sem, pv_p[n].past(ITEMS * bb + max(i - 1, 0)))
                        nc.scalar.activation(pt[i % 2][:, :].rearrange("p (u n) -> p u n", u=2), ps[2][0:KEYS, :, :],
                                             ACT.Copy).then_inc(pt_s[n].sem, 1)
                    i = s - 3 - lag
                    if 0 <= i < ITEMS and (not top or i // 2 % 2):
                        k = ITEMS * bb + i if not top else ITEMS // 2 * bb + i // 4 * 2 + i % 2
                        ac.wait_ge(ot_p[n].sem, ot_p[n].past(k + 1))
                        if i < 4:
                            ac.wait_ge(f_p[n].sem, f_p[n].past(4 * bb))
                        copy(oT[i % 2][:, i // 4 if top else i // 2, :], bank(7)[:, 0:S]).then_inc(ot_s[n].sem, 1)

            turned(0, 0, q_p[0], 2)
            queries(0, 0)
            with ac.Fori(0, PAIRS - 1) as bb:
                heads(0, bb, True)
            heads(0, PAIRS - 1, False)

            def single(n, bb, vscale):
                for p in range(2):
                    ac.wait_ge(sc_r[n].sem, sc_r[n].past(2 * bb + p + 1))
                    nc.scalar.activation(pr[p][:, :, 0:KEYS], pr[p][:, :, 0:KEYS], ACT.Exp,
                                         scale=1.0 / 16).then_inc(ex_s[n].sem, 1)
                for p in range(2):
                    ac.wait_ge(pt_p[n].sem, pt_p[n].past(2 * bb + p + 1))
                    ac.wait_ge(pv_p[n].sem, pv_p[n].past(2 * bb))
                    copy(pt[p][:, 0:S], bank(6 + p)[0:KEYS, 0:S]).then_inc(pt_s[n].sem, 1)

            if phases >= 1:
                ac.wait_ge(done[0].sem, done[0].past(TT))
                with pairs(ac) as bb:
                    turned(1, bb, f_p[1], 4)
            if phases >= 2:
                ac.wait_ge(done[1].sem, done[1].past(TT))
                for j in range(4):
                    ac.wait_ge(prep_p[2].sem, prep_p[2].past(j + 1))
                    nc.scalar.activation(kall[:, j // 2, (j % 2) * HALF:(j % 2 + 1) * HALF], bank(j)[:, 0:HALF],
                                         ACT.Identity, bias=cols[:, 3 + j // 2:4 + j // 2]).then_inc(prep_a[2].sem, 1)
                with pairs(ac) as bb:
                    turned(2, bb, q_p[2], 2)
                    for p in range(2):
                        ac.wait_ge(q_p[2].sem, q_p[2].past(2 * bb + p + 1))
                        ac.wait_ge(sc_p[2].sem, sc_p[2].past(2 * bb))
                        for m in range(CH):
                            nc.scalar.activation(wk[p][:, m, :], bank(2 + p)[:, m * S:(m + 1) * S], ACT.Identity,
                                                 bias=cols[:, 1 + m:2 + m]).then_inc(q_s[2].sem, 1)
                    single(2, bb, 1)
            if phases >= 3:
                ac.wait_ge(done[2].sem, done[2].past(TT))

                def bit_step(r, k):
                    t, b, p = 4 * r + k, 2 * r + (k + 1) // 2, (k + 1) // 2 % 2
                    if k % 2 and (k + 1) // 2 < B and k >= -1:
                        ac.wait_ge(xtp[3].sem, xtp[3].past(b + 1))
                        ac.wait_ge(h_p.sem, h_p.past(least(2 * b - 2)))
                        copy(xnT[p][:, 0, :].bitcast(bf16), bank(4)[:, 0:S].bitcast(bf16)).then_inc(xts[3].sem, 1)
                    if 0 <= k < TT:
                        ac.wait_ge(h_b.sem, h_b.past(t + 1))
                        hrow = wk[k % 2][:, :, :].rearrange("p c s -> p (c s)")
                        nc.scalar.activation(hrow, hrow, ACT.Gelu).then_inc(g_s.sem, 1)
                    if 1 <= k < TT + 1:
                        u = (k - 1) % 4
                        ac.wait_ge(h_r.sem, h_r.past(t))
                        ac.wait_ge(h_z.sem, h_z.past(least(t - 2)))
                        hrow = wk[u % 2][:, :, :].rearrange("p c s -> p (c s)")
                        nc.scalar.activation(hmag[u % 2], hrow, ACT.Copy, scale=sm[:, u % 2, 3, u // 2:u // 2 + 1],
                                             bias=MAGIC).then_inc(hq_s.sem, 1)
                    if 2 <= k < TT + 2:
                        ac.wait_ge(ht_p.sem, ht_p.past(t - 1))
                        ac.wait_ge(f_p[3].sem, f_p[3].past(least(t - 3)))
                        copy(pr[k % 2].rearrange("p t n -> p (t n)")[:, 0:512].bitcast(bf16),
                             bank(5).bitcast(bf16)).then_inc(ht_s.sem, 1)

                bit_steps(ac, bit_step)
            if phases >= 4:
                ac.wait_ge(done[3].sem, done[3].past(TT))
                ac.wait_ge(s_w[4], 5 * 16)
                ac.wait_ge(s_set.sem, s_set.past(3))
                for j in range(4):
                    ac.wait_ge(prep_p[4].sem, prep_p[4].past(j + 1))
                    nc.scalar.activation(kall[:, j // 2, (j % 2) * HALF:(j % 2 + 1) * HALF], bank(j)[:, 0:HALF],
                                         ACT.Identity, bias=cols[:, 7 + j // 2:8 + j // 2]).then_inc(prep_a[4].sem, 1)
                ac.wait_ge(prep_v[4].sem, prep_v[4].past(7))
                turned(4, 0, q_p[4], 2)
                queries(4, 0)
                with ac.Fori(0, PAIRS - 1) as bb:
                    heads(4, bb, True)
                heads(4, PAIRS - 1, False)
            if phases >= 5:
                ac.wait_ge(done[4].sem, done[4].past(TT))
                with pairs(ac) as bb:
                    for p in range(2):
                        ac.wait_ge(nrm[5].sem, nrm[5].past(2 * bb + p + 1))
                        copy(xkeep[:, bass.ds(4 * bb + 2 * p, 2), :], xn[p][:, :, :]).then_inc(keep_s.sem, 1)
                    turned(5, bb, lg_p, 2)
                ac.wait_ge(rt_v.sem, rt_v.past(1))
                nc.scalar.activation(gate2[:, :, 1], gate2[:, :, 0], ACT.Exp).then_inc(rt_a.sem, 1)
            if phases >= 6:
                ac.wait_ge(routed.sem, routed.past(1))

                def gelu(j):
                    ac.wait_ge(m_h.sem, m_h.past(j + 1))
                    ac.wait_ge(m_tp.sem, m_tp.past(j))
                    nc.scalar.activation(hid[:, :, :].rearrange("p (v c) s -> p v (c s)", v=2), ps[0][:, :, :],
                                         ACT.Gelu).then_inc(m_g.sem, 1)

                def result(j, u, k):
                    ac.wait_ge(m_y.sem, m_y.past(j + 1))
                    ac.wait_ge(s_st[u].sem, s_st[u].past(16 * k))
                    copy(ysb[u], bank(4)[:, 0:D]).then_inc(m_ys.sem, 1)

                gelu(0)
                with ac.Fori(0, (MT - 3) // 3) as r:
                    for u in range(3):
                        j = r * 3 + u + 1
                        gelu(j)
                        result(j - 1, u, r)
                for j in range(MT - 2, MT):
                    gelu(j)
                    result(j - 1, (j - 1) % 3, (j - 1) // 3)
                result(MT - 1, (MT - 1) % 3, (MT - 1) // 3)
            if phases >= 7:
                ac.wait_ge(done[6].sem, done[6].past(TT))
                with pairs(ac) as bb:
                    turned(7, bb, h7_p, 2)
                    single(7, bb, 1)
                    for p in range(2):
                        ac.wait_ge(x7_p.sem, x7_p.past(2 * bb + p + 1))
                        copy(xnT[p][:, :, :].rearrange("p c s -> p (c s)"), bank(p)).then_inc(x7_t.sem, 1)
                    for p in range(2):
                        ac.wait_ge(h7_p.sem, h7_p.past(2 * bb + p + 1))
                        ac.wait_ge(f7_p.sem, f7_p.past(2 * bb))
                        for m in range(CH):
                            ins = nc.scalar.activation(wk[p][:, m, :], bank(2 + p)[:, m * S:(m + 1) * S], ACT.Relu,
                                                       bias=cols[:, 9 + m:10 + m])
                        ins.then_inc(h7_s.sem, 1)
            if phases >= 8:
                ac.wait_ge(done[7].sem, done[7].past(TT))
                with pairs(ac) as bb:
                    turned(8, bb, f_p[8], 4)

        @block.vector
        def _(ve):
            ve.wait_ge(s_seeded, 1)

            def ln_stats(n, bb):
                for p in range(2):
                    for t in range(TB):
                        nc.vector.bn_stats(st[p][:, t, :], x[:, 4 * bb + 2 * p + t, :]).then_inc(dve[n].sem, 1)
                for p in range(2):
                    for t in range(TB):
                        ve.wait_ge(dve[n].sem, dve[n].past(4 * bb + 2 * p + t + 1))
                        ve.wait_ge(rstd[n].sem, rstd[n].past(2 * bb))
                        apart(ve)
                        nc.vector.bn_aggr(mv[p][:, t, :], st[p][:, t, :]).then_inc(stat[n].sem, 1)

            def ln_rows(n, bb, used):
                for p in range(2):
                    ve.wait_ge(rstd[n].sem, rstd[n].past(2 * bb + p + 1))
                    ve.wait_ge(used.sem, used.past(2 * bb))
                    for t in range(TB):
                        ins = nc.vector.tensor_scalar(xn[p][:, t, :], x[:, 4 * bb + 2 * p + t, :], mv[p][:, t, 0:1],
                                                      rs[p][:, t:t + 1], ALU.subtract, ALU.mult)
                    ins.then_inc(nrm[n].sem, 1)

            def ln(n, bb, used):
                ln_stats(n, bb)
                ln_rows(n, bb, used)

            def residual(n, bb, p, t, src, factor):
                row = x[:, 4 * bb + 2 * p + t, :]
                nc.vector.scalar_tensor_tensor(row, src, factor, row, ALU.mult, ALU.add).then_inc(done[n].sem, 1)

            ve.wait_ge(s_cst, 8 * 16)
            ve.wait_ge(s_w[0], 3 * 16)
            nc.vector.tensor_copy(identb[:, :], ident[:, :]).then_inc(s_set.sem, 1)
            neg = fmw[:, :, :].rearrange("p g (h s e) -> p (g h) s e", h=HG, s=2)[:, :, 1, :]
            nc.vector.tensor_scalar(neg, neg, -1.0, None, ALU.mult).then_inc(s_set.sem, 1)
            nc.vector.tensor_tensor(cols[:, 0:1], cols[:, 0:1], cols[:, 15:16], ALU.mult).then_inc(s_set.sem, 1)
            v0 = vall[:, 0:B * HEADS * 33].rearrange("p (b h e) -> p b h e", b=B, h=HEADS)
            nc.vector.memset(vall[:, 0:B * HEADS * 33].rearrange("p (q e) -> p q e", e=33)[:, :, 32:33], 1.0)
            for b in range(B):
                ve.wait_ge(prep_p[0].sem, prep_p[0].past(8 + b + 1))
                nc.vector.tensor_copy(v0[:, b, :, 0:32], bank(b)[0:KEYS, :].rearrange("p (h e) -> p h e", h=HEADS)
                                      ).then_inc(prep_v[0].sem, 1)
            ve.wait_ge(s_x, 16)
            ve.wait_ge(s_gate.sem, s_gate.past(1))
            for k in range(2):
                nc.vector.tensor_scalar(gb[:, k, :], gb[:, k, :], gates[:, 2 * k:2 * k + 1], None, ALU.mult
                                        ).then_inc(s_set.sem, 1)

            def drop_least(bb, i):
                u, base = i % 2, (ITEMS * bb + i) * 9
                d = [dd[u][:, j // HG, (j % HG) * KEYS:(j % HG + 1) * KEYS] for j in range(8)]

                def wait(k):
                    ve.wait_ge(tk_r.sem, tk_r.past(base + k))
                    apart(ve)

                for half in range(2):
                    for j in range(4 * half, 4 * half + 4):
                        ins = nc.vector.max(m8[u][:, j, :], d[j])
                    ins.then_inc(tk_r.sem, 1)
                for half in range(2):
                    wait(1 + half)
                    for j in range(4 * half, 4 * half + 4):
                        ins = nc.vector.match_replace(d[j], m8[u][:, j, :], d[j], -BIG)
                    ins.then_inc(tk_r.sem, 1)
                for half in range(2):
                    wait(3 + half)
                    for j in range(4 * half, 4 * half + 4):
                        ins = nc.vector.max(m8b[u][:, j, :], d[j])
                    ins.then_inc(tk_r.sem, 1)
                for half in range(2):
                    wait(5 + half)
                    nc.vector.memset(m8b[u][:, 4 * half:4 * half + 4, DROP - 8:8], -BIG).then_inc(tk_r.sem, 1)
                for half in range(2):
                    wait(7 + half)
                    for j in range(4 * half, 4 * half + 4):
                        ins = nc.vector.match_replace(d[j], m8b[u][:, j, :], d[j], -BIG)
                    ins.then_inc((tk_s if half else tk_r).sem, 1)

            def heads(n, bb, ahead):
                top = n == 4
                vd = 16 if top else 32
                lag = 1 if top else 0
                for s in range(ITEMS + 2 + lag):
                    if ahead and s == 4:
                        ln_stats(n, bb + 1)
                    if ahead and s == 6:
                        ln_rows(n, bb + 1, xtp[n])
                    if s < ITEMS:
                        i, u = s, s % 2
                        mxv = mx[u][:, :].rearrange("p (t h) -> p t h", t=TB)
                        if not top:
                            sv = ps[u][:, :, 0:GK].rearrange("p t (h k) -> p t h k", h=HG)
                            ve.wait_ge(sc_p[n].sem, sc_p[n].past(ITEMS * bb + i + 1))
                            nc.vector.tensor_reduce(mxv, sv, AX.X, ALU.max).then_inc(act[n].sem, 1)
                            ve.wait_ge(act[n].sem, act[n].past(ITEMS * bb + i + 1))
                            ve.wait_ge(pt_p[n].sem, pt_p[n].past(ITEMS * bb + max(i - 1, 0)))
                            nc.vector.tensor_tensor(pr[u].rearrange("p t (h k) -> p t h k", h=HG), sv,
                                                    mxv.unsqueeze(3).broadcast_to([P, TB, HG, KEYS]), ALU.subtract
                                                    ).then_inc(sc_r[n].sem, 1)
                        else:
                            ve.wait_ge(sc_r[n].sem, sc_r[n].past(ITEMS * bb + i + 1))
                            ve.wait_ge(sc_d.sem, sc_d.past(ITEMS * bb + max(i - 1, 0)))
                            nc.vector.tensor_reduce(mxv, dd[u].rearrange("p t (h k) -> p t h k", h=HG), AX.X, ALU.min
                                                    ).then_inc(act[n].sem, 1)
                            drop_least(bb, i)
                    i = s - 2 - lag
                    if 0 <= i < ITEMS:
                        u = i % 2
                        ve.wait_ge(pv_p[n].sem, pv_p[n].past(ITEMS * bb + i + 1))
                        ov = bank(6)[:, 0:8 * (vd + 1)].rearrange("p (j e) -> p j e", j=8)
                        nc.vector.reciprocal(rden[u][:, :], ov[:, :, vd]).then_inc(s_rd[n].sem, 1)
                        ve.wait_ge(s_rd[n].sem, s_rd[n].past(ITEMS * bb + i + 1))
                        ve.wait_ge(ot_p[n].sem, ot_p[n].past(ITEMS * bb + max(i - 1, 0) if not top
                                                             else ITEMS // 2 * bb + (i // 4 * 2 if i < 4 else 1 + i % 2)))
                        at = i // 2 % 2 * HG * vd if top else 0
                        nc.vector.tensor_tensor(osb[u][:, :, at:at + HG * vd].rearrange("p t (h e) -> p t h e", h=HG),
                                                ov[:, :, 0:vd].rearrange("p (t h) e -> p t h e", t=TB),
                                                rden[u][:, :].rearrange("p (t h) -> p t h", t=TB).unsqueeze(3)
                                                .broadcast_to([P, TB, HG, vd]), ALU.mult).then_inc(o_s[n].sem, 1)
                ve.wait_ge(xb_s[n].sem, xb_s[n].past(bb + 1))
                for p in range(2):
                    for t in range(TB):
                        ve.wait_ge(f_p[n].sem, f_p[n].past(4 * bb + 2 * p + t + 1))
                        residual(n, bb, p, t, bank(4 + 2 * p + t)[:, 0:D], gates[:, n // 2:n // 2 + 1])

            ln(0, 0, xtp[0])
            with ve.Fori(0, PAIRS - 1) as bb:
                heads(0, bb, True)
            heads(0, PAIRS - 1, False)

            if phases >= 1:
                ve.wait_ge(s_w[1], 16)
                ve.wait_ge(done[0].sem, done[0].past(TT))
                c1 = Chain(ve, prep_v[1])
                wv = sgw[:, :, :].rearrange("p c n -> p (c n)")
                tmp = xkeep_tmp[:, 0:CH * D]
                c1.link(nc.vector.tensor_scalar(tmp, wv, 0.0, None, ALU.is_lt))
                c1.link(nc.vector.scalar_tensor_tensor(wv, wv, 0.0, tmp, ALU.is_gt, ALU.subtract))
                with pairs(ve) as bb:
                    ln(1, bb, xtp[1])
                    for p in range(2):
                        for t in range(TB):
                            ve.wait_ge(f_p[1].sem, f_p[1].past(4 * bb + 2 * p + t + 1))
                            residual(1, bb, p, t, bank(4 + 2 * p + t)[:, 0:D], gates[:, 4:5])

            def single_soft(n, bb, p):
                ve.wait_ge(sc_p[n].sem, sc_p[n].past(2 * bb + p + 1))
                sv = bank(4 + p)[:, 0:TB * KEYS].rearrange("p (t k) -> p t k", t=TB)
                nc.vector.tensor_reduce(mx[p][:, 0:TB], sv, AX.X, ALU.max).then_inc(act[n].sem, 1)
                ve.wait_ge(act[n].sem, act[n].past(3 * (2 * bb + p) + 1 if False else 2 * bb + p + 1))
                ve.wait_ge(pt_p[n].sem, pt_p[n].past(2 * bb))
                nc.vector.tensor_tensor(pr[p][:, :, 0:KEYS], sv, mx[p][:, 0:TB].unsqueeze(2)
                                        .broadcast_to([P, TB, KEYS]), ALU.subtract).then_inc(sc_r[n].sem, 1)

            def single_sum(n, bb, p):
                ve.wait_ge(ex_s[n].sem, ex_s[n].past(2 * bb + p + 1))
                nc.vector.tensor_reduce(rden[p][:, 0:TB], pr[p][:, :, 0:KEYS], AX.X, ALU.add).then_inc(s_rd[n].sem, 1)
                ve.wait_ge(s_rd[n].sem, s_rd[n].past(2 * (2 * bb + p) + 1))
                nc.vector.reciprocal(rden[p][:, TB:2 * TB], rden[p][:, 0:TB]).then_inc(s_rd[n].sem, 1)
                ve.wait_ge(s_rd[n].sem, s_rd[n].past(2 * (2 * bb + p) + 2))

            if phases >= 2:
                ve.wait_ge(done[1].sem, done[1].past(TT))
                for j in range(4):
                    ve.wait_ge(prep_p[2].sem, prep_p[2].past(4 + j + 1))
                    nc.vector.tensor_copy(vall[:, j * 512:(j + 1) * 512], bank(4 + j)[0:KEYS, :]).then_inc(prep_v[2].sem, 1)
                with pairs(ve) as bb:
                    ln(2, bb, xtp[2])
                    for p in range(2):
                        single_soft(2, bb, p)
                    for p in range(2):
                        single_sum(2, bb, p)
                        nc.vector.tensor_scalar(rden[p][:, 4:4 + TB], rden[p][:, TB:2 * TB], gates[:, 1:2], None,
                                                ALU.mult).then_inc(dvx[2].sem, 1)
                    ve.wait_ge(dvx[2].sem, dvx[2].past(2 * bb + 2))
                    for p in range(2):
                        ve.wait_ge(pv_p[2].sem, pv_p[2].past(2 * bb + p + 1))
                        for t in range(TB):
                            residual(2, bb, p, t, bank(p)[:, t * D:(t + 1) * D], rden[p][:, 4 + t:5 + t])

            if phases >= 3:
                ve.wait_ge(done[2].sem, done[2].past(TT))
                ve.wait_ge(s_w[3], 4 * 16)
                c3 = Chain(ve, prep_v[3])
                for k, (stg, tern) in enumerate(((stage1, tern1), (stage2, tern2))):
                    tv = tern[:, :, :].rearrange("p c n -> p (c n)")
                    tmp = vtmp
                    c3.link(nc.vector.tensor_reduce(wstat[:, k:k + 1], stg, AX.X, ALU.add, apply_absolute_value=True))
                    ve.wait_ge(prep_p[3].sem, prep_p[3].past(k + 1))
                    c3.link(nc.vector.tensor_scalar(wstat[:, 2 + k:3 + k], bank(k)[:, 0:1], 1.0 / (D * FF), EPS_Q,
                                                    ALU.mult, ALU.max))
                    c3.link(nc.vector.tensor_scalar(wstat[:, 4 + k:5 + k], wstat[:, 2 + k:3 + k], 0.5, None, ALU.mult))
                    c3.link(nc.vector.tensor_scalar(wstat[:, 6 + k:7 + k], wstat[:, 2 + k:3 + k], -0.5, None, ALU.mult))
                    c3.link(nc.vector.tensor_scalar(tmp, stg, wstat[:, 4 + k:5 + k], None, ALU.is_gt))
                    c3.link(nc.vector.scalar_tensor_tensor(tv, stg, wstat[:, 6 + k:7 + k], tmp, ALU.is_lt, ALU.subtract))
                    c3.link(nc.vector.tensor_scalar(wstat[:, 4 + k:5 + k], wstat[:, 2 + k:3 + k], -1.0 / QB, None,
                                                    ALU.mult))
                c3.link(nc.vector.tensor_tensor(wstat[:, 5:6], wstat[:, 5:6], gates[:, 5:6], ALU.mult))
                c3.link(nc.vector.tensor_scalar(b2bc, b2bc, gates[:, 5:6], None, ALU.mult))

                def bit_stats(b, p):
                    for t in range(TB):
                        nc.vector.bn_stats(st[p][:, t, :], x[:, 2 * b + t, :]).then_inc(dve[3].sem, 1)
                    ve.wait_ge(dve[3].sem, dve[3].past(2 * b + 2))
                    apart(ve)
                    for t in range(TB):
                        nc.vector.bn_aggr(mv[p][:, t, :], st[p][:, t, :]).then_inc(stat[3].sem, 1)

                def bit_rows(b, p):
                    ve.wait_ge(rstd[3].sem, rstd[3].past(b + 1))
                    for t in range(TB):
                        ins = nc.vector.tensor_scalar(xn[p][:, t, :], x[:, 2 * b + t, :], mv[p][:, t, 0:1],
                                                      rs[p][:, t:t + 1], ALU.subtract, ALU.mult)
                    ins.then_inc(nrm[3].sem, 1)
                    ve.wait_ge(nrm[3].sem, nrm[3].past(b + 1))
                    nc.vector.tensor_reduce(sm[:, p, 0, 0:TB], xn[p][:, :, :], AX.X, ALU.max,
                                            apply_absolute_value=True).then_inc(q_m.sem, 1)

                def bit_quant(b, p):
                    ve.wait_ge(q_r.sem, q_r.past(2 * b + 2))
                    for t in range(TB):
                        ins = nc.vector.tensor_scalar(xn[p][:, t, :], xn[p][:, t, :], sm[:, p, 1, t:t + 1], MAGIC,
                                                      ALU.mult, ALU.add)
                    ins.then_inc(dvx[3].sem, 1)
                    ve.wait_ge(dvx[3].sem, dvx[3].past(b + 1))
                    ve.wait_ge(xtp[3].sem, xtp[3].past(least(b - 1)))
                    nc.vector.tensor_scalar(xq[p][:, :, :], xn[p][:, :, :], MAGIC, QB, ALU.subtract, ALU.min
                                            ).then_inc(q_s[3].sem, 1)

                def bit_step(r, k):
                    t = 4 * r + k
                    if 0 <= k < TT:
                        u = k % 4
                        ve.wait_ge(h_p.sem, h_p.past(t + 1))
                        ve.wait_ge(hq_s.sem, hq_s.past(least(t - 1)))
                        hrow = wk[u % 2][:, :, :].rearrange("p (v c) s -> p v (c s)", v=2)
                        nc.vector.scalar_tensor_tensor(hrow, ps[u % 2][:, :, :], sm[:, u // 2, 0, u % 2:u % 2 + 1],
                                                       b1bc.rearrange("p (v n) -> p v n", v=2),
                                                       ALU.mult, ALU.add).then_inc(h_b.sem, 1)
                    if 1 <= k < TT + 1:
                        u = (k - 1) % 4
                        ve.wait_ge(g_s.sem, g_s.past(t))
                        nc.vector.tensor_reduce(sm[:, u % 2, 2, u // 2:u // 2 + 1],
                                                wk[u % 2][:, :, :].rearrange("p c s -> p (c s)"), AX.X, ALU.max,
                                                apply_absolute_value=True).then_inc(h_m.sem, 1)
                    if k % 2 == 0:
                        if -2 <= k and (k + 2) // 2 < B:
                            bit_quant(2 * r + (k + 2) // 2, (k + 2) // 2 % 2)
                        if (k + 4) // 2 < B:
                            bit_stats(2 * r + (k + 4) // 2, (k + 4) // 2 % 2)
                    elif (k + 3) // 2 < B:
                        bit_rows(2 * r + (k + 3) // 2, (k + 3) // 2 % 2)
                    if k >= 3:
                        u = (k - 3) % 4
                        ve.wait_ge(f_p[3].sem, f_p[3].past(t - 2))
                        ve.wait_ge(h_w.sem, h_w.past(t - 2))
                        ve.wait_ge(xb_s[3].sem, xb_s[3].past(2 * r + (k - 3) // 2 + 1))
                        row = x[:, t - 3, :]
                        nc.vector.scalar_tensor_tensor(row, bank(6 + u % 2)[:, 0:D], sm[:, u % 2, 2, u // 2:u // 2 + 1],
                                                       row, ALU.mult, ALU.add).then_inc(done[3].sem, 1)
                    if 1 <= k < TT + 1:
                        u = (k - 1) % 4
                        ve.wait_ge(hq_s.sem, hq_s.past(t))
                        ve.wait_ge(ht_p.sem, ht_p.past(least(t - 2)))
                        nc.vector.tensor_scalar(hq[u % 2], hmag[u % 2], MAGIC, QB, ALU.subtract, ALU.min
                                                ).then_inc(h_z.sem, 1)

                bit_steps(ve, bit_step)

            if phases >= 4:
                ve.wait_ge(done[3].sem, done[3].past(TT))
                ve.wait_ge(s_w[4], 5 * 16)
                c4 = Chain(ve, prep_v[4])
                v2 = vall[:, 0:B * HEADS * 17].rearrange("p (b h e) -> p b h e", b=B, h=HEADS)
                c4.link(nc.vector.tensor_copy(mrow, mrow8[:, :]))
                c4.link(nc.vector.tensor_reduce(mcol[:, :], mrow.rearrange("p (b k) -> p b k", b=B), AX.X, ALU.max))
                c4.link(nc.vector.tensor_scalar(mcol[:, :], mcol[:, :], -1.0, None, ALU.mult))
                c4.link(nc.vector.tensor_scalar(mrow, mrow, -BIG, BIG, ALU.mult, ALU.add))
                c4.link(nc.vector.tensor_scalar(cols[:, 12:14], cols[:, 5:7], -0.25, None, ALU.mult))
                c4.link(nc.vector.memset(vall[:, 0:B * HEADS * 17].rearrange("p (q e) -> p q e", e=17)[:, :, 16:17], 1.0))
                for j in range(4):
                    ve.wait_ge(prep_p[4].sem, prep_p[4].past(4 + j + 1))
                    for h in range(2):
                        ins = nc.vector.tensor_copy(v2[:, 2 * j + h, :, 0:16],
                                                    bank(4 + j)[0:KEYS, h * D:(h + 1) * D]
                                                    .rearrange("p (h e) -> p h e", h=HEADS))
                    c4.step(ins)
                ln(4, 0, xtp[4])
                with ve.Fori(0, PAIRS - 1) as bb:
                    heads(4, bb, True)
                heads(4, PAIRS - 1, False)

            if phases >= 5:
                ve.wait_ge(done[4].sem, done[4].past(TT))
                with pairs(ve) as bb:
                    ve.wait_ge(keep_s.sem, keep_s.past(2 * bb))
                    ln(5, bb, xtp[5])
                    for p in range(2):
                        ve.wait_ge(lg_p.sem, lg_p.past(2 * bb + p + 1))
                        nc.vector.tensor_copy(lg[p][:, :, :], bank(2 + p)[:, 0:TB * E].rearrange(
                            "p (t e) -> p t e", t=TB)).then_inc(rt_l.sem, 1)
                    for p in range(2):
                        ve.wait_ge(rt_l.sem, rt_l.past(2 * bb + p + 1))
                        apart(ve)
                        for t in range(TB):
                            nc.vector.max(m8[p][:, t, :], lg[p][:, t, :]).then_inc(rt_m.sem, 1)
                    for p in range(2):
                        for t in range(TB):
                            ve.wait_ge(rt_m.sem, rt_m.past(4 * bb + 2 * p + t + 1))
                            apart(ve)
                            nc.vector.max_index(ix[p][:, t, :], m8[p][:, t, :], lg[p][:, t, :]).then_inc(rt_i.sem, 1)
                    for p in range(2):
                        ve.wait_ge(rt_i.sem, rt_i.past(4 * bb + 2 * p + 2))
                        nc.vector.tensor_copy(topv[:, bass.ds(4 * bb + 2 * p, 2), :], m8[p][:, 0:2, 0:2]).then_inc(rt_c.sem, 1)
                        nc.vector.tensor_copy(topi[:, bass.ds(4 * bb + 2 * p, 2), :], ix[p][:, :, 0:2]).then_inc(rt_c.sem, 1)
                ve.wait_ge(rt_c.sem, rt_c.past(16))
                c5 = Chain(ve, rt_v)
                c5.link(nc.vector.tensor_tensor(gate2[:, :, 0], topv[:, :, 1], topv[:, :, 0], ALU.subtract))
                oh = rt[:, 0:256]
                cum = rt[:, 256:512]
                tot = rt[:, 512:768]
                base = rt[:, 768:1024]
                cnt = rt[:, 1024:1040]
                off = rt[:, 1040:1056]
                til = rt[:, 1056:1064]
                end = rt[:, 1064:1072]
                tmp = rt[:, 1280:1536]
                pos = rt[:, 1536:1568]
                where = rt[:, 1568:1600]
                one = rt[:, 1600:1632]
                ef = rt[:, 1632:1632 + 64]
                oh3 = oh.rearrange("p (q e) -> p q e", e=E)
                c5.link(nc.vector.tensor_tensor(oh3, iota[:, 0:E].unsqueeze(1).broadcast_to([P, 2 * TT, E]),
                                                topi[:, :, :].rearrange("p t k -> p (t k)").unsqueeze(2)
                                                .broadcast_to([P, 2 * TT, E]), ALU.is_equal))
                ve.wait_ge(rt_p.sem, rt_p.past(2))
                c5.step(nc.vector.tensor_copy(cum, bank(0)[:, 0:256]))
                c5.link(nc.vector.tensor_copy(tot, bank(1)[:, 0:256]))
                c5.link(nc.vector.memset(base[:, 0:16], 0.0))
                for t in range(1, TT):
                    c5.link(nc.vector.tensor_tensor(base[:, 16 * t:16 * t + 16], base[:, 16 * t - 16:16 * t],
                                                    tot[:, 16 * t - 16:16 * t], ALU.add))
                c5.link(nc.vector.tensor_tensor(cnt, base[:, 240:256], tot[:, 240:256], ALU.add))
                c5.link(nc.vector.tensor_tensor(til, cnt[:, 0:8], cnt[:, 8:16], ALU.add))
                c5.link(nc.vector.tensor_scalar(til, til, 1.0 / P, 127.0 / 256, ALU.mult, ALU.add))
                c5.link(nc.vector.tensor_scalar(til, til, MAGIC, None, ALU.add))
                c5.link(nc.vector.tensor_scalar(til, til, MAGIC, None, ALU.subtract))
                c5.link(nc.vector.tensor_copy(end[:, 0:1], til[:, 0:1]))
                for e in range(1, E):
                    c5.link(nc.vector.tensor_tensor(end[:, e:e + 1], end[:, e - 1:e], til[:, e:e + 1], ALU.add))
                c5.link(nc.vector.tensor_tensor(off[:, 0:8], end, til, ALU.subtract))
                c5.link(nc.vector.tensor_scalar(off[:, 0:8], off[:, 0:8], float(P), -1.0, ALU.mult, ALU.add))
                c5.link(nc.vector.tensor_tensor(off[:, 8:16], off[:, 0:8], cnt[:, 0:8], ALU.add))
                c5.link(nc.vector.tensor_tensor(cum, cum, base, ALU.add))
                c5.link(nc.vector.tensor_tensor(tmp, cum, oh, ALU.mult))
                c5.link(nc.vector.tensor_reduce(pos, tmp.rearrange("p (q e) -> p q e", e=E), AX.X, ALU.add))
                c5.link(nc.vector.tensor_tensor(cum.rearrange("p (t n) -> p t n", t=TT),
                                                cum.rearrange("p (t n) -> p t n", t=TT),
                                                off.unsqueeze(1).broadcast_to([P, TT, 16]), ALU.add))
                c5.link(nc.vector.tensor_tensor(tmp, cum, oh, ALU.mult))
                c5.link(nc.vector.tensor_reduce(where, tmp.rearrange("p (q e) -> p q e", e=E), AX.X, ALU.add))
                c5.link(nc.vector.tensor_copy(slot[:, :, :].rearrange("p k t -> p t k"),
                                              where.rearrange("p (t k) -> p t k", k=2)))
                ve.wait_ge(rt_a.sem, rt_a.past(1))
                c5.link(nc.vector.tensor_scalar(one[:, 0:16], gate2[:, :, 1], 1.0, None, ALU.add))
                c5.link(nc.vector.reciprocal(gate2[:, :, 0], one[:, 0:16]))
                c5.link(nc.vector.tensor_tensor(gate2[:, :, 1], gate2[:, :, 1], gate2[:, :, 0], ALU.mult))
                c5.link(nc.vector.tensor_scalar(pos, pos, float(CAP), gates[:, 6:7], ALU.is_le, ALU.mult))
                g2 = gate2[:, :, :].rearrange("p t k -> p (t k)")
                c5.link(nc.vector.tensor_tensor(g2, g2, pos, ALU.mult))
                c5.link(nc.vector.tensor_scalar(ef, iota[:, 0:64], end[:, 0:1], None, ALU.is_ge))
                for e in range(1, E - 1):
                    c5.link(nc.vector.scalar_tensor_tensor(ef, iota[:, 0:64], end[:, e:e + 1], ef, ALU.is_ge, ALU.add))
                c5.link(nc.vector.tensor_copy(eid[:, :], ef))
                ve.sem_inc(routed.sem, 1)
            if phases >= 6:
                def rows_in(j, u):
                    ve.wait_ge(m_xp.sem, m_xp.past(j + 1))
                    nc.vector.tensor_copy(xTb[u], bank(5)[:, 0:D].rearrange("p (c s) -> p c s", c=CH)).then_inc(m_xs.sem, 1)

                def hidden(j):
                    ve.wait_ge(m_tp.sem, m_tp.past(j + 1))
                    ve.wait_ge(m_y.sem, m_y.past(j))
                    nc.vector.tensor_copy(hidT.rearrange("p (v n) -> p v n", v=2), ps[1][:, :, :]).then_inc(m_ts.sem, 1)

                rows_in(0, 0)
                with ve.Fori(0, (MT - 3) // 3) as r:
                    for u in range(3):
                        j = r * 3 + u + 1
                        rows_in(j, (u + 1) % 3)
                        hidden(j - 1)
                for j in range(MT - 2, MT):
                    rows_in(j, j % 3)
                    hidden(j - 1)
                hidden(MT - 1)
                for t in range(TT):
                    if t % 4 == 0:
                        ve.wait_ge(s_ga[t // 4], 8 * 16)
                    nc.vector.scalar_tensor_tensor(x[:, t, :], got[:, 0, t, :], gate2[:, t, 0:1], x[:, t, :], ALU.mult,
                                                   ALU.add).then_inc(cmb.sem, 1)
                for t in range(TT):
                    ve.wait_ge(cmb.sem, cmb.past(t + 1))
                    nc.vector.scalar_tensor_tensor(x[:, t, :], got[:, 1, t, :], gate2[:, t, 1:2], x[:, t, :], ALU.mult,
                                                   ALU.add).then_inc(done[6].sem, 1)
            if phases >= 7:
                ve.wait_ge(s_w[7], 4 * 16)
                ve.wait_ge(done[6].sem, done[6].past(TT))
                gam = bc3[:, 0:1, :].broadcast_to([P, TB, D])
                bet = bc3[:, 1:2, :].broadcast_to([P, TB, D])
                N7 = 2 * 2 + 2 * 2 + 2 * 2 + 2 * 3
                with pairs(ve) as bb:
                    ln(7, bb, xtp[7])
                    ch = Chain(ve, dvx[7], N7 * bb)

                    def spread(p):
                        for t in range(TB):
                            ins = nc.vector.bn_stats(st[p][:, t, :], xn[p][:, t, :])
                        ch.link(ins)
                        apart(ve)
                        for t in range(TB):
                            ins = nc.vector.bn_aggr(mv[p][:, t, :], st[p][:, t, :])
                        ins.then_inc(v2_s.sem, 1)

                    def normed(p, count):
                        ve.wait_ge(r2_s.sem, r2_s.past(count))
                        for t in range(TB):
                            ins = nc.vector.tensor_scalar(xn[p][:, t, :], xn[p][:, t, :], mv[p][:, t, 0:1],
                                                          rs[p][:, t:t + 1], ALU.subtract, ALU.mult)
                        ch.link(ins)
                        ch.link(nc.vector.tensor_tensor(xn[p][:, :, :], xn[p][:, :, :], gam, ALU.mult))
                        return nc.vector.tensor_tensor(xn[p][:, :, :], xn[p][:, :, :], bet, ALU.add)

                    for p in range(2):
                        single_soft(7, bb, p)
                    for p in range(2):
                        single_sum(7, bb, p)
                    for p in range(2):
                        ve.wait_ge(pv_p[7].sem, pv_p[7].past(2 * bb + p + 1))
                        for t in range(TB):
                            ins = nc.vector.scalar_tensor_tensor(xn[p][:, t, :], bank(p)[:, t * D:(t + 1) * D],
                                                                 rden[p][:, TB + t:TB + t + 1], xn[p][:, t, :],
                                                                 ALU.mult, ALU.add)
                        ch.link(ins)
                        spread(p)
                    for p in range(2):
                        normed(p, 4 * bb + p + 1).then_inc(x7_s.sem, 1)
                    for p in range(2):
                        ve.wait_ge(f7_p.sem, f7_p.past(2 * bb + p + 1))
                        ve.wait_ge(x7_s.sem, x7_s.past(2 * bb + p + 1))
                        ch.link(nc.vector.tensor_tensor(xn[p][:, :, :], xn[p][:, :, :],
                                                        bank(4 + p).rearrange("p (t d) -> p t d", t=TB), ALU.add))
                        spread(p)
                    for p in range(2):
                        ch.link(normed(p, 4 * bb + 2 + p + 1))
                        for t in range(TB):
                            residual(7, bb, p, t, xn[p][:, t, :], gates[:, 3:4])

                    assert ch.n == N7, ch.n
            if phases >= 8:
                c8 = Chain(ve, prep_8)
                ve.wait_ge(done[7].sem, done[7].past(TT))
                c8.link(nc.vector.tensor_scalar(w3f, w3f, 0.0, 2.0, ALU.is_ge, ALU.mult))
                c8.link(nc.vector.tensor_scalar(w3f, w3f, -1.0, None, ALU.add))
                with pairs(ve) as bb:
                    ln(8, bb, xtp[8])
                    ch = Chain(ve, dvx[8], 12 * bb)
                    for p in range(2):
                        for t in range(TB):
                            y = xkeep[:, 12 + 2 * p + t, :]
                            ve.wait_ge(f_p[8].sem, f_p[8].past(4 * bb + 2 * p + t + 1))
                            ch.link(nc.vector.tensor_tensor(y, bank(4 + 2 * p + t)[:, 0:D], bc3[:, 2, :], ALU.mult))
                            ch.link(nc.vector.tensor_tensor(y, y, bc3[:, 3, :], ALU.add))
                            ch.link(nc.vector.tensor_scalar(y, y, -100.0, 100.0, ALU.max, ALU.min))
                            residual(8, bb, p, t, y, gates[:, 7:8])

        @block.tensor
        def _(pe):
            pe.wait_ge(s_seeded, 1)

            def turn(n, bb):
                for p in range(2):
                    pe.wait_ge(nrm[n].sem, nrm[n].past(2 * bb + p + 1))
                    pe.wait_ge(done[n].sem, done[n].past(4 * bb))
                    for c in range(CH):
                        for t in range(TB):
                            ins = nc.tensor.transpose(bank(p)[:, c * S + t * P:c * S + (t + 1) * P],
                                                      xn[p][:, t, c * P:(c + 1) * P], ident[:, :])
                    ins.then_inc(xtp[n].sem, 1)

            pe.wait_ge(s_cst, 8 * 16)
            pe.wait_ge(s_ctx, 16)
            for c in range(CH):
                for h in range(2):
                    for b in range(4):
                        ins = nc.tensor.transpose(bank(2 * c + h)[:, b * KEYS:(b + 1) * KEYS],
                                                  ctxn[:, 4 * h + b, c * P:(c + 1) * P], ident[0:KEYS, 0:KEYS])
                    ins.then_inc(s_ctp.sem, 1)
            pe.wait_ge(s_cta.sem, s_cta.past(4))
            pe.wait_ge(s_set.sem, s_set.past(3))
            for j in range(2 * GR):
                nc.tensor.matmul(bank(j)[:, 0:HALF], fmw[:, j // 2 % 2, :],
                                 ctxT[:, j // 4, (j % 2) * HALF:(j % 2 + 1) * HALF],
                                 start=True, stop=True).then_inc(prep_p[0].sem, 1)
            pe.wait_ge(prep_a[0].sem, prep_a[0].past(8))
            for b in range(B):
                for g in range(GR):
                    ins = nc.tensor.transpose(bank(b)[0:KEYS, g * P:(g + 1) * P], kall[:, g, b * KEYS:(b + 1) * KEYS],
                                              ident[:, :])
                ins.then_inc(prep_p[0].sem, 1)
            pe.wait_ge(prep_v[0].sem, prep_v[0].past(8))
            pe.wait_ge(s_setp.sem, s_setp.past(2))

            def turn_ahead(n, bb):
                for p in range(2):
                    pe.wait_ge(nrm[n].sem, nrm[n].past(2 * bb + p + 1))
                    for c in range(CH):
                        for t in range(TB):
                            ins = nc.tensor.transpose(bank(p)[:, c * S + t * P:c * S + (t + 1) * P],
                                                      xn[p][:, t, c * P:(c + 1) * P], ident[:, :])
                    ins.then_inc(xtp[n].sem, 1)

            def queries(n, bb):
                for p in range(2):
                    pe.wait_ge(xts[n].sem, xts[n].past(2 * bb + (2 if n == 0 else p + 1)))
                    if n == 0:
                        for g in range(GR):
                            ins = nc.tensor.matmul(ps[1 - p][:, g // 2, (g % 2) * S:(g % 2 + 1) * S], fmw[:, g % 2, :],
                                                   xnT[p][:, g // 2, :], start=True, stop=True)
                    else:
                        for m in range(CH):
                            for c in range(CH):
                                ins = nc.tensor.matmul(bank(2 + p)[:, m * S:(m + 1) * S], w2q[:, c, m * P:(m + 1) * P],
                                                       xnT[p][:, c, :], start=c == 0, stop=c == CH - 1)
                    ins.then_inc(q_p[n].sem, 1)

            def heads(n, bb, ahead):
                top = n == 4
                vd = 16 if top else 32
                w = HG * vd
                lag = 1 if top else 0
                vv = vall[:, 0:B * HEADS * (vd + 1)].rearrange("p (b h e) -> p b h e", b=B, h=HEADS)
                for s in range(ITEMS + 3 + lag):
                    if s < ITEMS:
                        i, g, u = s, s // 2, s % 2
                        if s == 0:
                            pe.wait_ge(q_s[n].sem, q_s[n].past((4 if top else 2) * (bb + 1)))
                        if s < 2:
                            pe.wait_ge(kb_s[n].sem, kb_s[n].past(2 * bb + s + 1))
                        if s >= 2:
                            pe.wait_ge(sc_r[n].sem, sc_r[n].past(ITEMS * bb + i - 1))
                        for t in range(TB):
                            ins = nc.tensor.matmul(ps[u][:, t, 0:GK], wk[u][:, g // 2 if top else g, t * P:(t + 1) * P],
                                                   kb[u][:, g, :], start=True, stop=not top)
                            if top:
                                ins = nc.tensor.matmul(ps[u][:, t, 0:GK], row0[:, :],
                                                       mrow[:, bass.ds((2 * bb + u) * KEYS, KEYS)].unsqueeze(1)
                                                       .broadcast_to([P, HG, KEYS]), start=False, stop=True)
                        ins.then_inc(sc_p[n].sem, 1)
                    if ahead and s == ITEMS:
                        pe.wait_ge(sc_r[n].sem, sc_r[n].past(ITEMS * bb + ITEMS - 1))
                        turn_ahead(n, bb + 1)
                    if ahead and s == ITEMS + 1:
                        pe.wait_ge(sc_r[n].sem, sc_r[n].past(ITEMS * bb + ITEMS))
                        queries(n, bb + 1)
                    i = s - 1 - lag
                    if 0 <= i < ITEMS:
                        pe.wait_ge(ex_s[n].sem, ex_s[n].past(ITEMS * bb + i + 1))
                        pe.wait_ge(pt_s[n].sem, pt_s[n].past(ITEMS * bb + i))
                        if i == 0:
                            pe.wait_ge(done[n].sem, done[n].past(4 * bb))
                        for h in range(HG):
                            for t in range(TB):
                                at = (h % 2) * S + t * P
                                ins = nc.tensor.transpose(ps[2][0:KEYS, h // 2, at:at + P],
                                                          pr[i % 2][:, t, h * KEYS:(h + 1) * KEYS], ident[:, :])
                        ins.then_inc(pt_p[n].sem, 1)
                    i = s - 2 - lag
                    if 0 <= i < ITEMS:
                        pe.wait_ge(pt_s[n].sem, pt_s[n].past(ITEMS * bb + i + 1))
                        pe.wait_ge(o_s[n].sem, o_s[n].past(ITEMS * bb + i))
                        for t in range(TB):
                            for h in range(HG):
                                j = t * HG + h
                                ins = nc.tensor.matmul(bank(6)[:, j * (vd + 1):(j + 1) * (vd + 1)],
                                                       pt[i % 2][:, h * S + t * P:h * S + (t + 1) * P],
                                                       vv[:, 2 * bb + i % 2, i // 2 * HG + h, :], start=True, stop=True)
                        ins.then_inc(pv_p[n].sem, 1)
                    i = s - 3 - lag
                    if 0 <= i < ITEMS:
                        if not top or i // 2 % 2:
                            k = ITEMS * bb + i if not top else ITEMS // 2 * bb + i // 4 * 2 + i % 2
                            pe.wait_ge(o_s[n].sem, o_s[n].past(ITEMS * bb + i + 1))
                            pe.wait_ge(ot_s[n].sem, ot_s[n].past(k))
                            for t in range(TB):
                                ins = nc.tensor.transpose(bank(7)[:, t * P:(t + 1) * P], osb[i % 2][:, t, :],
                                                          ident[:, :])
                            ins.then_inc(ot_p[n].sem, 1)
                wo = w2o if top else fcw
                nch = CH if top else GR
                for p in range(2):
                    pe.wait_ge(ot_s[n].sem, ot_s[n].past(2 * nch * bb + 2 * nch - 1 + p))
                    for t in range(TB):
                        if p == 1 and t == 1:
                            pe.wait_ge(o_s[n].sem, o_s[n].past(ITEMS * bb + ITEMS))
                        for g in range(nch):
                            ins = nc.tensor.matmul(bank(4 + 2 * p + t)[:, 0:D], oT[p][:, g, t * P:(t + 1) * P],
                                                   wo[:, g, :], start=g == 0, stop=g == nch - 1)
                        ins.then_inc(f_p[n].sem, 1)

            pe.wait_ge(s_w[0], 3 * 16)
            turn_ahead(0, 0)
            queries(0, 0)
            with pe.Fori(0, PAIRS - 1) as bb:
                heads(0, bb, True)
            heads(0, PAIRS - 1, False)

            def plain(n, bb, w):
                turn(n, bb)
                for p in range(2):
                    pe.wait_ge(xts[n].sem, xts[n].past(2 * bb + p + 1))
                    for t in range(TB):
                        for c in range(CH):
                            ins = nc.tensor.matmul(bank(4 + 2 * p + t)[:, 0:D], xnT[p][:, c, t * P:(t + 1) * P],
                                                   w[:, c, :], start=c == 0, stop=c == CH - 1)
                        ins.then_inc(f_p[n].sem, 1)

            if phases >= 1:
                pe.wait_ge(done[0].sem, done[0].past(TT))
                pe.wait_ge(prep_v[1].sem, prep_v[1].past(2))
                with pairs(pe) as bb:
                    plain(1, bb, sgw)

            def keys(n, wkey):
                for j in range(4):
                    m, h = j // 2, j % 2
                    for c in range(CH):
                        ins = nc.tensor.matmul(bank(j)[:, 0:HALF], wkey[:, c, m * P:(m + 1) * P],
                                               ctxT[:, c, h * HALF:(h + 1) * HALF], start=c == 0, stop=c == CH - 1)
                    ins.then_inc(prep_p[n].sem, 1)

            def values(n, wval, bias):
                for b in range(B):
                    dst = bank(4 + b // 2)[0:KEYS, (b % 2) * D:(b % 2 + 1) * D]
                    for c in range(CH):
                        nc.tensor.matmul(dst, ctxT[:, c, b * KEYS:(b + 1) * KEYS], wval[:, c, :], start=c == 0,
                                         stop=False)
                    ins = nc.tensor.matmul(dst, ones[0:1, 0:KEYS], rows[0:1, bias, :], start=False, stop=True)
                    if b % 2:
                        ins.then_inc(prep_p[n].sem, 1)

            def single(n, bb, keyT, val):
                nk = 4 if n == 2 else 2
                for p in range(2):
                    q = wk[p] if n == 2 else xnT[p]
                    if n == 2:
                        pe.wait_ge(q_s[2].sem, q_s[2].past(4 * bb + 2 * p + 2))
                    for t in range(TB):
                        for m in range(CH):
                            ins = nc.tensor.matmul(bank(4 + p)[:, t * KEYS:(t + 1) * KEYS], q[:, m, t * P:(t + 1) * P],
                                                   keyT[:, m, bass.ds((2 * bb + p) * KEYS, KEYS)],
                                                   start=m == 0, stop=m == CH - 1)
                    ins.then_inc(sc_p[n].sem, 1)
                for p in range(2):
                    pe.wait_ge(ex_s[n].sem, ex_s[n].past(2 * bb + p + 1))
                    pe.wait_ge(pt_s[n].sem, pt_s[n].past(2 * bb))
                    for t in range(TB):
                        ins = nc.tensor.transpose(bank(6 + p)[0:KEYS, t * P:(t + 1) * P],
                                                  pr[p][:, t, 0:KEYS], ident[:, :])
                    ins.then_inc(pt_p[n].sem, 1)
                for p in range(2):
                    pe.wait_ge(pt_s[n].sem, pt_s[n].past(2 * bb + p + 1))
                    for t in range(TB):
                        ins = nc.tensor.matmul(bank(p)[:, t * D:(t + 1) * D], pt[p][:, t * P:(t + 1) * P],
                                               val(2 * bb + p), start=True, stop=True)
                    ins.then_inc(pv_p[n].sem, 1)

            if phases >= 2:
                pe.wait_ge(done[1].sem, done[1].past(TT))
                pe.wait_ge(s_w[2], 3 * 16)
                keys(2, w1k)
                values(2, w1v, 0)
                pe.wait_ge(prep_a[2].sem, prep_a[2].past(4))
                pe.wait_ge(prep_v[2].sem, prep_v[2].past(4))
                with pairs(pe) as bb:
                    turn(2, bb)
                    for p in range(2):
                        pe.wait_ge(xts[2].sem, xts[2].past(2 * bb + p + 1))
                        for m in range(CH):
                            for c in range(CH):
                                ins = nc.tensor.matmul(bank(2 + p)[:, m * S:(m + 1) * S], w1q[:, c, m * P:(m + 1) * P],
                                                       xnT[p][:, c, :], start=c == 0, stop=c == CH - 1)
                        ins.then_inc(q_p[2].sem, 1)
                    single(2, bb, kall, lambda b: vall[:, bass.ds(b * D, D)])
            if phases >= 3:
                pe.wait_ge(done[2].sem, done[2].past(TT))
                for k in range(2):
                    pe.wait_ge(prep_v[3].sem, prep_v[3].past(1 + 7 * k))
                    nc.tensor.matmul(bank(k)[:, 0:1], ones[:, :], wstat[:, k:k + 1], start=True,
                                     stop=True).then_inc(prep_p[3].sem, 1)
                pe.wait_ge(prep_v[3].sem, prep_v[3].past(16))

                def bit_step(r, k):
                    t = 4 * r + k
                    if k >= 3:
                        u = (k - 3) % 4
                        pe.wait_ge(ht_s.sem, ht_s.past(t - 2))
                        pe.wait_ge(done[3].sem, done[3].past(least(t - 4)))
                        hT = pr[u % 2].rearrange("p t n -> p (t n)")[:, 0:512].bitcast(bf16)
                        for j in range(FF // P):
                            ins = nc.tensor.matmul(bank(6 + u % 2)[:, 0:D], hT[:, j * P:(j + 1) * P],
                                                   tern2[:, j, :], start=j == 0, stop=j == FF // P - 1)
                        ins.then_inc(f_p[3].sem, 1)
                    if 2 <= k < TT + 2:
                        pe.wait_ge(h_z.sem, h_z.past(t - 1))
                        pe.wait_ge(ht_s.sem, ht_s.past(t - 2))
                        tb = bank(5).bitcast(bf16)
                        for j in range(FF // P):
                            ins = nc.tensor.transpose(tb[:, j * P:(j + 1) * P], hq[k % 2][:, j * P:(j + 1) * P],
                                                      identb[:, :])
                        ins.then_inc(ht_p.sem, 1)
                    if -1 <= k < TT - 1:
                        u = (k + 1) % 4
                        pe.wait_ge(xts[3].sem, xts[3].past(2 * r + (k + 1) // 2 + 1))
                        pe.wait_ge(h_b.sem, h_b.past(least(t)))
                        xT = xnT[u // 2][:, 0, :].bitcast(bf16).rearrange("p (c s) -> p c s", c=CH)
                        for v in range(2):
                            for c in range(CH):
                                ins = nc.tensor.matmul(ps[u % 2][:, v, :], xT[:, c, (u % 2) * P:(u % 2 + 1) * P],
                                                       tern1[:, c, v * 512:(v + 1) * 512], start=c == 0,
                                                       stop=c == CH - 1)
                        ins.then_inc(h_p.sem, 1)
                    if k % 2 == 0 and -2 <= k and (k + 2) // 2 < B:
                        b, p = 2 * r + (k + 2) // 2, (k + 2) // 2 % 2
                        pe.wait_ge(q_s[3].sem, q_s[3].past(b + 1))
                        pe.wait_ge(xts[3].sem, xts[3].past(b))
                        tb = bank(4).bitcast(bf16)
                        for c in range(CH):
                            for q in range(TB):
                                ins = nc.tensor.transpose(tb[:, c * S + q * P:c * S + (q + 1) * P],
                                                          xq[p][:, q, c * P:(c + 1) * P], identb[:, :])
                        ins.then_inc(xtp[3].sem, 1)

                bit_steps(pe, bit_step)
            if phases >= 4:
                pe.wait_ge(done[3].sem, done[3].past(TT))
                pe.wait_ge(s_w[4], 5 * 16)
                keys(4, w2k)
                values(4, w2v, 1)
                pe.wait_ge(prep_a[4].sem, prep_a[4].past(4))
                pe.wait_ge(prep_v[4].sem, prep_v[4].past(10))
                turn_ahead(4, 0)
                queries(4, 0)
                with pe.Fori(0, PAIRS - 1) as bb:
                    heads(4, bb, True)
                heads(4, PAIRS - 1, False)

            if phases >= 5:
                pe.wait_ge(done[4].sem, done[4].past(TT))
                pe.wait_ge(s_w[5], 16)
                with pairs(pe) as bb:
                    for p in range(2):
                        pe.wait_ge(nrm[5].sem, nrm[5].past(2 * bb + p + 1))
                        pe.wait_ge(xts[5].sem, xts[5].past(2 * bb))
                        for c in range(CH):
                            for t in range(TB):
                                ins = nc.tensor.transpose(bank(p)[:, c * S + t * P:c * S + (t + 1) * P],
                                                          xn[p][:, t, c * P:(c + 1) * P], ident[:, :])
                        ins.then_inc(xtp[5].sem, 1)
                    for p in range(2):
                        pe.wait_ge(xts[5].sem, xts[5].past(2 * bb + p + 1))
                        pe.wait_ge(rt_l.sem, rt_l.past(2 * bb))
                        for t in range(TB):
                            for c in range(CH):
                                ins = nc.tensor.matmul(bank(2 + p)[:, t * E:(t + 1) * E],
                                                       xnT[p][:, c, t * P:(t + 1) * P], rwT[:, c, :], start=c == 0,
                                                       stop=c == CH - 1)
                        ins.then_inc(lg_p.sem, 1)
                pe.wait_ge(rt_v.sem, rt_v.past(2))
                nc.tensor.matmul(bank(0)[:, 0:256], lower[:, :], rt[:, 0:256], start=True, stop=True).then_inc(rt_p.sem, 1)
                nc.tensor.matmul(bank(1)[:, 0:256], ones[:, :], rt[:, 0:256], start=True, stop=True).then_inc(rt_p.sem, 1)
            if phases >= 6:
                pe.wait_ge(routed.sem, routed.past(1))
                pe.wait_ge(s_we, 2 * E * 16)

                def rows_t(j, u, k):
                    pe.wait_ge(s_ld[u], 16 * k + 16)
                    pe.wait_ge(m_xs.sem, m_xs.past(j))
                    for c in range(CH):
                        ins = nc.tensor.transpose(bank(5)[:, c * P:(c + 1) * P], xsb[u][:, c * P:(c + 1) * P],
                                                  ident[:, :])
                    ins.then_inc(m_xp.sem, 1)

                def first(j, u):
                    pe.wait_ge(m_xs.sem, m_xs.past(j + 1))
                    pe.wait_ge(m_g.sem, m_g.past(j))
                    apart(pe)
                    e = pe.value_load(eid[0:1, bass.ds(j, 1)], min_val=0, max_val=E - 1)
                    for v in range(2):
                        for c in range(CH):
                            ins = nc.tensor.matmul(ps[0][:, v, :], xTb[u][:, c, :],
                                                   experts[:, bass.ds(e * EW + (c * FF + v * 512), 512)],
                                                   start=c == 0, stop=c == CH - 1)
                    ins.then_inc(m_h.sem, 1)

                def hidden_t(j):
                    pe.wait_ge(m_g.sem, m_g.past(j + 1))
                    pe.wait_ge(m_ts.sem, m_ts.past(j))
                    hv = hid[:, :, :].rearrange("p c s -> p (c s)")
                    for k in range(FF // P):
                        ins = nc.tensor.transpose(ps[1][:, k // 4, (k % 4) * P:(k % 4 + 1) * P],
                                                  hv[:, k * P:(k + 1) * P], ident[:, :])
                    ins.then_inc(m_tp.sem, 1)

                def second(j):
                    pe.wait_ge(m_ts.sem, m_ts.past(j + 1))
                    pe.wait_ge(m_ys.sem, m_ys.past(j))
                    apart(pe)
                    e = pe.value_load(eid[0:1, bass.ds(j, 1)], min_val=0, max_val=E - 1)
                    for k in range(FF // P):
                        ins = nc.tensor.matmul(bank(4)[:, 0:D], hidT[:, k * P:(k + 1) * P],
                                               experts[:, bass.ds(e * EW + (E * EW + k * D), D)], start=k == 0,
                                               stop=k == FF // P - 1)
                    ins.then_inc(m_y.sem, 1)

                rows_t(0, 0, 0)
                rows_t(1, 1, 0)
                first(0, 0)
                with pe.Fori(0, (MT - 3) // 3) as r:
                    for u in range(3):
                        j = r * 3 + u + 1
                        rows_t(j + 1, (u + 2) % 3, r if u == 0 else r + 1)
                        hidden_t(j - 1)
                        first(j, (u + 1) % 3)
                        second(j - 1)
                for j in range(MT - 2, MT):
                    if j + 1 < MT:
                        rows_t(j + 1, (j + 1) % 3, (j + 1) // 3)
                    hidden_t(j - 1)
                    first(j, j % 3)
                    second(j - 1)
                hidden_t(MT - 1)
                second(MT - 1)
            if phases >= 7:
                pe.wait_ge(done[6].sem, done[6].past(TT))
                pe.wait_ge(s_w[7], 4 * 16)
                with pairs(pe) as bb:
                    turn(7, bb)
                    for p in range(2):
                        pe.wait_ge(xts[7].sem, xts[7].past(2 * bb + p + 1))
                    single(7, bb, ctxT, lambda b: ctxn[:, b, :])
                    for p in range(2):
                        pe.wait_ge(x7_s.sem, x7_s.past(2 * bb + p + 1))
                        for c in range(CH):
                            for t in range(TB):
                                ins = nc.tensor.transpose(bank(p)[:, c * S + t * P:c * S + (t + 1) * P],
                                                          xn[p][:, t, c * P:(c + 1) * P], ident[:, :])
                        ins.then_inc(x7_p.sem, 1)
                    for p in range(2):
                        pe.wait_ge(x7_t.sem, x7_t.past(2 * bb + p + 1))
                        for m in range(CH):
                            for c in range(CH):
                                ins = nc.tensor.matmul(bank(2 + p)[:, m * S:(m + 1) * S], w3a[:, c, m * P:(m + 1) * P],
                                                       xnT[p][:, c, :], start=c == 0, stop=c == CH - 1)
                        ins.then_inc(h7_p.sem, 1)
                    for p in range(2):
                        pe.wait_ge(h7_s.sem, h7_s.past(2 * bb + p + 1))
                        for t in range(TB):
                            dst = bank(4 + p)[:, t * D:(t + 1) * D]
                            for c in range(CH):
                                nc.tensor.matmul(dst, wk[p][:, c, t * P:(t + 1) * P], w3b[:, c, :], start=c == 0,
                                                 stop=False)
                            ins = nc.tensor.matmul(dst, ones[0:1, :], rows[0:1, 2, :], start=False, stop=True)
                        ins.then_inc(f7_p.sem, 1)
            if phases >= 8:
                pe.wait_ge(done[7].sem, done[7].past(TT))
                pe.wait_ge(prep_8.sem, prep_8.past(2))
                with pairs(pe) as bb:
                    plain(8, bb, w3f)


def kernel(**inputs):
    import numpy as np
    import concourse.bacc as bacc
    from concourse import mybir
    from concourse.bass_utils import run_bass_kernel_spmd

    i = {k: np.asarray(v) for k, v in inputs.items()}
    p = np.arange(128)
    fm = i["L0_xattn_fm_w"].T
    fmw = np.zeros((128, 2, 4, 2, 16), fm.dtype)
    for g in range(2):
        for h in range(4):
            for s in range(2):
                fmw[g * 64 + h * 16:g * 64 + h * 16 + 16, g, h, s, :] = fm
    cols = np.zeros((128, 16), np.float32)
    cols[:, 0] = np.tile(i["L0_xattn_fm_b"], 8)
    cols[:, 15] = np.where(p // 16 % 2 == 0, 1.0, -1.0)
    for n, key in ((1, "L1_xattn_bq"), (3, "L1_xattn_bk"), (5, "L2_xattn_wq_b"), (7, "L2_xattn_wk_b"), (9, "L3_xattn_b1")):
        cols[:, n:n + 2] = i[key].reshape(2, 128).T
    hsel = np.zeros((128, 12), np.float32)
    hsel[p, p // 32] = 1.0
    hsel[p, 4 + p // 16] = 1.0
    iota = np.tile(np.arange(64, dtype=np.float32), (128, 1))
    given = {
        "x": i["x"],
        "ctx": i["ctx_1024"][:, ::-1],
        "mask": i["mask_BxS2_bf1"][:, ::-1].reshape(-1).view(np.uint8),
        "g": np.concatenate([i["g_xattn"], i["g_ffn"]]),
        "ident": np.eye(128, dtype=np.float32),
        "lower": np.triu(np.ones((128, 128), np.float32)),
        "iota": iota, "hsel": hsel, "cols": cols,
        "rows": np.stack([i["L1_xattn_bv"], i["L2_xattn_wv_b"], i["L3_xattn_b2"]]),
        "outb": np.stack([i["L0_xattn_fc_b"], i["L2_xattn_wo_b"]]),
        "row0": (p == 0)[:, None] * np.ones((128, 128), np.float32),
        "fmw": fmw.reshape(128, 2, 128),
        "fcw": i["L0_xattn_fc_w"].T, "sgw": i["L0_ffn_weight"].T,
        "w1q": i["L1_xattn_Wq"], "w1k": i["L1_xattn_Wk"], "w1v": i["L1_xattn_Wv"],
        "bw1": i["L1_ffn_W1"].T, "bw2": i["L1_ffn_W2"].T, "bb1": i["L1_ffn_b1"], "bb2": i["L1_ffn_b2"],
        "w2q": i["L2_xattn_wq_w"].T, "w2k": i["L2_xattn_wk_w"].T, "w2v": i["L2_xattn_wv_w"].T,
        "w2o": i["L2_xattn_wo_w"].T, "rw": i["L2_ffn_router_w"].T,
        "ew1": i["L2_ffn_w1"], "ew2": i["L2_ffn_w2"],
        "w3a": i["L3_xattn_W1"], "w3b": i["L3_xattn_W2"],
        "bc3": np.stack([i["L3_xattn_gamma"], i["L3_xattn_beta"], i["L3_ffn_scale"], i["L3_ffn_bias"]]),
        "w3f": i["L3_ffn_weights"].T,
    }
    nc = bacc.Bacc("TRN2", target_bir_lowering=False, num_devices=1)
    arrays, aps = {}, {}
    for key, v in given.items():
        v = np.ascontiguousarray(v)
        arrays["in_" + key] = v
        aps[key] = nc.dram_tensor("in_" + key, v.shape, mybir.dt.from_np(v.dtype), kind="ExternalInput").ap()
    res = nc.dram_tensor("out_0", (B, S, D), mybir.dt.float32, kind="ExternalOutput").ap()
    build(nc, aps, res, PHASES)
    r = run_bass_kernel_spmd(nc, [arrays], core_ids=[0])
    return r.results[0]["out_0"]


PHASES = 8
```

```python
B, S, D = 8, 256, 256
P = 128
CH = D // P
TT = B * S // P
TB = S // P
KEYS = 77
NK = B * KEYS
HALF = NK // 2
HEADS = 16
HG = 4
GR = HEADS // HG
GK = HG * KEYS
FF = 4 * D
E = 8
CAP = int(1.25 * B * S / E * 2)
DROP = KEYS - 64
MT = B * S * 2 // P + E - 1
PAIRS = B // 2
ITEMS = 2 * GR
BIG = 1e38
MAGIC = 12582912.0
QB = 127.0
EPS_Q = 1e-5


def build(nc, a, out, phases=8):
    from concourse import mybir
    import concourse.bass as bass
    from contextlib import ExitStack

    f32, bf16, i32, u32, u8 = (mybir.dt.float32, mybir.dt.bfloat16, mybir.dt.int32,
                               mybir.dt.uint32, mybir.dt.uint8)
    ALU = mybir.AluOpType
    ACT = mybir.ActivationFunctionType
    AX = mybir.AxisListType
    ctx = ExitStack()
    with ctx:
        def sb(name, shape, dt=f32):
            return ctx.enter_context(nc.sbuf_tensor(name, shape, dt))

        def sem(name):
            return ctx.enter_context(nc.semaphore(name))

        seeds = []

        def counted(name):
            s = sem(name)
            seeds.append(s)
            return Share(s, 0)

        class Share:

            def __init__(self, s, base):
                self.sem, self.base = s, base

            def past(self, n):
                return n + (self.base + 1)

        def shared(name, per_phase):
            s, base, out = counted(name).sem, 0, {}
            for n, k in per_phase.items():
                out[n] = Share(s, base)
                base += k
            return out

        class Chain:

            def __init__(self, eng, s, base=0):
                self.eng, self.s, self.base, self.n = eng, s, base, 0

            def step(self, ins):
                self.n += 1
                ins.then_inc(self.s.sem, 1)

            def settle(self):
                self.eng.wait_ge(self.s.sem, self.s.past(self.base + self.n))

            def link(self, ins):
                self.step(ins)
                self.settle()

        def apart(eng):
            eng.sem_inc(s_apart, 1)

        x = sb("x", [P, TT, D])
        xkeep = sb("xkeep", [P, TT, D])
        experts = sb("experts", [P, 2 * E * CH * FF])
        EW = CH * FF
        EARLY = 5
        arena_at = [EARLY * EW]

        def arena(n, parts=P):
            at = arena_at[0]
            arena_at[0] += n
            assert arena_at[0] <= 2 * E * EW
            return experts[0:parts, at:at + n]

        fcw = arena(4 * D).rearrange("p (c n) -> p c n", c=4)
        sgw = arena(CH * D).rearrange("p (c n) -> p c n", c=CH)
        w1q = arena(CH * D).rearrange("p (c n) -> p c n", c=CH)
        w1k = arena(CH * D).rearrange("p (c n) -> p c n", c=CH)
        w1v = arena(CH * D).rearrange("p (c n) -> p c n", c=CH)
        w2q = arena(CH * D).rearrange("p (c n) -> p c n", c=CH)
        w2k = arena(CH * D).rearrange("p (c n) -> p c n", c=CH)
        w2v = arena(CH * D).rearrange("p (c n) -> p c n", c=CH)
        w2o = arena(CH * D).rearrange("p (c n) -> p c n", c=CH)
        gb = arena(2 * D).rearrange("p (c n) -> p c n", c=2)
        tern1 = arena(EW // 2).bitcast(bf16).rearrange("p (c n) -> p c n", c=CH)
        tern2 = arena(EW // 2).bitcast(bf16).rearrange("p (c n) -> p c n", c=FF // P)
        kall = arena(GR * NK).rearrange("p (g n) -> p g n", g=GR)
        vall = arena(B * HEADS * 33, KEYS)
        kb_at = arena_at[0]
        kb = [arena(GR * GK).rearrange("p (g n) -> p g n", g=GR) for _ in range(2)]
        pr = [arena(TB * GK).rearrange("p (t n) -> p t n", t=TB) for _ in range(2)]
        dd = [arena(TB * GK).rearrange("p (t n) -> p t n", t=TB) for _ in range(2)]
        fmw = arena(2 * P).rearrange("p (g n) -> p g n", g=2)
        b1bc = arena(FF)
        b2bc = arena(D)
        osb = [arena(TB * P).rearrange("p (t n) -> p t n", t=TB) for _ in range(2)]
        ktmp = kall[:, :, :].rearrange("p g n -> p (g n)")
        vtmp = experts[:, kb_at:kb_at + EW]
        hmag = [xkeep[:, 4 * u:4 * u + 4, :].rearrange("p t d -> p (t d)") for u in range(2)]
        kb0, kb1 = (k[:, :, :].rearrange("p g n -> p (g n)") for k in kb)
        xq = [k[:, 0:S].bitcast(bf16).rearrange("p (t d) -> p t d", t=TB) for k in (kb0, kb1)]
        hq = [k[:, S:S + FF // 2].bitcast(bf16) for k in (kb0, kb1)]
        stage1 = xkeep[:, 0:8, :].rearrange("p t d -> p (t d)")
        stage2 = xkeep[:, 8:16, :].rearrange("p t d -> p (t d)")

        ident = sb("ident", [P, P])
        identb = sb("identb", [P, P], bf16)
        ones = sb("ones", [P, P])
        ctxT = sb("ctxT", [P, CH, NK])
        ctxn = sb("ctxn", [KEYS, B, D])
        xn = [sb(f"xn{i}", [P, TB, D]) for i in range(2)]
        xnT = [sb(f"xnT{i}", [P, CH, S]) for i in range(2)]
        wk = [sb(f"wk{i}", [P, 4, S]) for i in range(2)]
        pt = [sb(f"pt{i}", [KEYS, HG * S]) for i in range(2)]
        oT = [xkeep[:, 8 + 4 * i:12 + 4 * i, :] for i in range(2)]
        row0 = sb("row0", [P, P])
        rows = arena(2 * D, KEYS).rearrange("p (k n) -> p k n", k=2)
        cols = sb("cols", [P, 16])
        gates = sb("gates", [P, 2 * 4])
        graw = sb("graw", [P, 2 * 4])
        st = [sb(f"st{i}", [P, TB, 6]) for i in range(2)]
        mv = [sb(f"mv{i}", [P, TB, 2]) for i in range(2)]
        rs = [sb(f"rs{i}", [P, TB]) for i in range(2)]
        st_a, mv_a, rs_a = ([sb(f"{n}_a{i}", [P, TB, w]) for i in range(2)] for n, w in (("st", 6), ("mv", 2), ("rs", 1)))
        st_b, mv_b, rs_b = ([sb(f"{n}_b{i}", [P, TB, w]) for i in range(2)] for n, w in (("st", 6), ("mv", 2), ("rs", 1)))
        mhalf = sb("mhalf", [P, TB])
        mone = sb("mone", [P, TB])
        sm = sb("sm", [P, 2, 4, 8])
        m8 = [sb(f"m8{i}", [P, 8, 8]) for i in range(2)]
        m8b = [sb(f"m8b{i}", [P, 8, 8]) for i in range(2)]
        rden = [sb(f"rden{i}", [P, 8]) for i in range(2)]
        mx = [sb(f"mx{i}", [P, 8]) for i in range(2)]
        hsel = sb("hsel", [P, 4 + 8])
        mrow8 = sb("mrow8", [P, NK], u8)
        mrow = arena(NK)
        mcol = sb("mcol", [P, B])
        wstat = sb("wstat", [P, 8])
        w3a, w3b, w3f = (xkeep[:, 2 * k:2 * k + 2, :] for k in range(3))
        bc3 = xkeep[:, 6:10, :]
        b2row, gamg, betg = (xkeep[:, 13 + k, :] for k in range(3))
        def rows7(k):
            at = EARLY * EW + 2 * k * TB * D
            return [experts[:, at + p * TB * D:at + (p + 1) * TB * D].rearrange("p (t d) -> p t d", t=TB)
                    for p in range(2)]
        xl, xa, xb, ya, xbT = (rows7(k) for k in range(5))
        rwT = sb("rwT", [P, CH, E])
        lg = [sb(f"lg{i}", [P, TB, E]) for i in range(2)]
        ix = [sb(f"ix{i}", [P, TB, 8], u32) for i in range(2)]
        topv = sb("topv", [P, TT, 2])
        topi = sb("topi", [P, TT, 2])
        lower = sb("lower", [P, P])
        iota = sb("iota", [P, P + 2 * TT])
        rown = sb("rown", [P, MT], i32)
        gate2 = sb("gate2", [P, TT, 2])
        slot = sb("slot", [P, 2, TT], i32)
        eid = sb("eid", [P, 64], i32)
        xsb = [xn[0][:, 0, :], xn[0][:, 1, :], xn[1][:, 0, :]]
        xTb = [v.rearrange("p (c s) -> p c s", c=CH) for v in (xnT[0][:, 0, :], xnT[0][:, 1, :], xnT[1][:, 0, :])]
        hid = wk[0]
        hidT = wk[1][:, :, :].rearrange("p c s -> p (c s)")
        ysb = [xkeep[:, 10 + u, :] for u in range(3)]
        got = experts[:, 0:2 * TT * D].rearrange("p (k t d) -> p k t d", k=2, t=TT)
        rt = experts[:, E * EW:E * EW + 4096]
        ps = [ctx.enter_context(nc.psum_tensor(f"ps{i}", [P, 2, 512], f32)) for i in range(4)]

        def bank(i):
            return ps[i // 2][:, i % 2, :]

        xs_d = nc.dram_tensor("expert_in", [TT * P, D], f32).ap()
        ys_d = nc.dram_tensor("expert_out", [MT * P, D], f32).ap()

        L = (0, 1, 2, 3, 4, 5, 6, 7, 8)
        SC = B * GR
        NORMS = (0, 1, 2, 3, 4, 5, 7, 8)
        s_x = sem("s_x")
        s_ctx = sem("s_ctx")
        s_cst = sem("s_cst")
        s_w = {n: sem(f"s_w{n}") for n in (0, 1, 2, 3, 4, 5, 7)}
        s_we = sem("s_we")
        s_out = sem("s_out")
        s_seeded = sem("s_seeded")
        s_apart = sem("s_apart")
        s_set = counted("s_set")
        s_setp = counted("s_setp")
        s_ctp = counted("s_ctp")
        s_cta = counted("s_cta")
        s_gate = counted("s_gate")
        stat = shared("stat", {n: TT for n in NORMS})
        rstd = shared("rstd", {n: B for n in NORMS})
        nrm = shared("nrm", {n: B for n in NORMS})
        xtp = shared("xtp", {n: B for n in NORMS})
        xts = shared("xts", {n: B for n in NORMS})
        done = shared("done", {n: 0 if n == 5 else TT for n in L})
        pool = shared("pool", {n: B for n in NORMS})
        dve = shared("dve", {n: TT for n in NORMS})
        act = shared("act", {0: SC, 2: B, 4: SC, 7: B})
        prep_p = {n: counted(f"prep_p{n}") for n in (0, 2, 3, 4)}
        prep_a = {n: counted(f"prep_a{n}") for n in (0, 2, 4)}
        prep_v = {n: counted(f"prep_v{n}") for n in (0, 1, 2, 3, 4)}
        q_p = shared("q_p", {0: B, 2: B, 4: B, 7: B})
        q_s = shared("q_s", {0: B, 2: 2 * B, 3: B, 4: 2 * B, 7: B})
        xb_s = shared("xb_s", {0: PAIRS, 3: B, 4: PAIRS, 7: PAIRS})
        kb_s = shared("kb_s", {0: B, 4: B})
        sc_p = shared("sc_p", {0: SC, 2: B, 4: SC, 7: B})
        sc_r = shared("sc_r", {0: SC, 2: B, 4: SC, 7: B})
        sc_d = counted("sc_d")
        tk_s = counted("tk_s")
        ex_s = shared("ex_s", {0: SC, 2: B, 4: SC, 7: B})
        pt_p = shared("pt_p", {0: SC, 2: B, 4: SC, 7: B})
        pt_s = shared("pt_s", {0: SC, 2: B, 4: SC, 7: B})
        pv_p = shared("pv_p", {0: SC, 2: B, 4: SC, 7: B})
        o_s = shared("o_s", {0: SC, 4: SC})
        ot_p = shared("ot_p", {0: SC, 4: SC // 2})
        ot_s = shared("ot_s", {0: SC, 4: SC // 2})
        f_p = shared("f_p", {n: TT for n in (0, 1, 3, 4, 8)})
        g_s = counted("g_s")
        hq_s = counted("hq_s")
        ht_p = counted("ht_p")
        ht_s = counted("ht_s")
        h_p = counted("h_p")
        h_b = counted("h_b")
        h_r = counted("h_r")
        s_ab = counted("s_ab")
        tk_r = counted("tk_r")
        h_z = counted("h_z")
        q_m = counted("q_m")
        q_c = counted("q_c")
        q_r = counted("q_r")
        h_m = counted("h_m")
        h_c = counted("h_c")
        h_w = counted("h_w")
        s_rd = shared("s_rd", {0: SC, 2: 2 * B, 4: SC, 7: 2 * B})
        keep_s = counted("keep_s")
        lg_p = counted("lg_p")
        rt_v = counted("rt_v")
        rt_a = counted("rt_a")
        rt_p = counted("rt_p")
        routed = counted("routed")
        s_kd = sem("s_kd")
        inv_v = counted("inv_v")
        inv_p = counted("inv_p")
        inv_s = counted("inv_s")
        s_ld = [sem(f"s_ld{u}") for u in range(3)]
        s_st = [counted(f"s_st{u}") for u in range(3)]
        s_ga = [sem(f"s_ga{u}") for u in range(PAIRS)]
        m_xp = counted("m_xp")
        m_xs = counted("m_xs")
        m_h = counted("m_h")
        m_g = counted("m_g")
        m_tp = counted("m_tp")
        m_ts = counted("m_ts")
        m_y = counted("m_y")
        m_ys = counted("m_ys")
        xa_s = counted("xa_s")
        sa_s = counted("sa_s")
        va_s = counted("va_s")
        ra_c = counted("ra_c")
        ra_s = counted("ra_s")
        na_s = counted("na_s")
        yb_s = counted("yb_s")
        sb_s = counted("sb_s")
        vb_s = counted("vb_s")
        rb_c = counted("rb_c")
        rb_s = counted("rb_s")
        nb_s = counted("nb_s")
        g7_s = counted("g7_s")
        x7_s = counted("x7_s")
        x7_p = counted("x7_p")
        x7_t = counted("x7_t")
        h7_p = counted("h7_p")
        h7_s = counted("h7_s")
        f7_p = counted("f7_p")
        prep_8 = counted("prep_8")
        rt_l = counted("rt_l")
        rt_m = counted("rt_m")
        rt_i = counted("rt_i")
        rt_c = counted("rt_c")
        cmb = counted("cmb")
        dvx = {n: counted(f"dvx{n}") for n in (2, 3, 8)}

        block = ctx.enter_context(nc.Block())

        def least(n):
            return max(n, 0) if isinstance(n, int) else n

        def bit_steps(eng, step):
            for k in range(-4, 3):
                step(0, k)
            with eng.Fori(0, 2) as r:
                for k in range(3, 7):
                    step(r, k)
            for k in range(11, TT + 3):
                step(0, k)

        def last_steps(eng, step, start=-1):
            for q in range(start, 1):
                step(q)
            with eng.Fori(1, PAIRS - 1) as q:
                step(q)
            step(PAIRS - 1)
            step(PAIRS)

        def ahead_steps(eng, step):
            step(-1, False, True)
            with eng.Fori(0, PAIRS - 1) as q:
                step(q, True, True)
            step(PAIRS - 1, True, False)

        def head_steps(eng, n, step):
            lag = 4 if n == 4 else 3
            for s in range(lag):
                step(0, s, True)
            with eng.Fori(0, PAIRS - 1) as bb:
                for s in range(lag, ITEMS + lag):
                    step(bb, s, True)
            for s in range(lag, ITEMS + lag):
                step(PAIRS - 1, s, False)

        def live(i, ahead):
            return 0 <= i and (ahead or i < ITEMS)

        def has(q):
            if not isinstance(q, int):
                return True, True, True
            return 0 <= q < PAIRS, 1 <= q, q + 1 < PAIRS

        def late(n):
            return E * EW + n * EW

        @block.sync
        def _(sp):
            xv = a["x"].rearrange("b (t p) d -> p (b t) d", p=P)
            sp.dma_start(ident[:, :], a["ident"]).then_inc(s_ctx, 16)
            sp.dma_start(ctxn[:, :, :], a["ctx"].rearrange("b k d -> k b d")).then_inc(s_ctx, 16)
            for dst, key in ((lower, "lower"), (iota, "iota"), (hsel, "hsel"), (cols, "cols")):
                sp.dma_start(dst[:, :], a[key]).then_inc(s_cst, 16)
            sp.dma_start(graw[:, :], a["g"].partition_broadcast(P)).then_inc(s_cst, 16)
            sp.dma_start(rows, a["rows"].partition_broadcast(KEYS)).then_inc(s_cst, 16)
            sp.dma_start(row0[:, :], a["row0"]).then_inc(s_cst, 16)
            sp.dma_start(fmw[:, :, :], a["fmw"]).then_inc(s_w[0], 16)
            sp.dma_start(gb[:, :, :], a["outb"].partition_broadcast(P)).then_inc(s_w[0], 16)
            sp.dma_start(x[:, :, :], xv).then_inc(s_x, 16)
            sp.dma_start(fcw[:, :, :], a["fcw"].rearrange("(c p) n -> p c n", p=P)).then_inc(s_w[0], 16)
            sp.dma_start(sgw[:, :, :], a["sgw"].rearrange("(c p) n -> p c n", p=P)).then_inc(s_w[1], 16)
            for w, key in ((w1q, "w1q"), (w1k, "w1k"), (w1v, "w1v")):
                sp.dma_start(w[:, :, :], a[key].rearrange("(c p) n -> p c n", p=P)).then_inc(s_w[2], 16)
            sp.dma_start(stage1.rearrange("p (c n) -> p c n", c=CH), a["bw1"].rearrange("(c p) n -> p c n", p=P)).then_inc(s_w[3], 16)
            sp.dma_start(b1bc, a["bb1"].partition_broadcast(P)).then_inc(s_w[3], 16)
            sp.dma_start(b2bc, a["bb2"].partition_broadcast(P)).then_inc(s_w[3], 16)
            for w, key in ((w2q, "w2q"), (w2k, "w2k"), (w2v, "w2v")):
                sp.dma_start(w[:, :, :], a[key].rearrange("(c p) n -> p c n", p=P)).then_inc(s_w[4], 16)
            sp.dma_start(w2o[:, :, :], a["w2o"].rearrange("(c p) n -> p c n", p=P)).then_inc(s_w[4], 16)
            sp.dma_start(mrow8[:, :], a["mask"].partition_broadcast(P)).then_inc(s_w[4], 16)
            sp.dma_start(rwT[:, :, :], a["rw"].rearrange("(c p) n -> p c n", p=P)).then_inc(s_w[5], 16)
            sp.wait_ge(s_seeded, 1)
            if phases >= 3:
                sp.wait_ge(done[0].sem, done[0].past(TT))
                sp.dma_start(stage2.rearrange("p (c n) -> p c n", c=FF // P),
                             a["bw2"].rearrange("(c p) n -> p c n", p=P)).then_inc(s_w[3], 16)
            if phases >= 6:
                def first(e):
                    sp.dma_start(experts[:, e * EW:(e + 1) * EW].rearrange("p (c n) -> p c n", c=CH),
                                 a["ew1"][e].rearrange("(c p) n -> p c n", p=P)).then_inc(s_we, 16)

                def second(e):
                    sp.dma_start(experts[:, late(e):late(e) + EW].rearrange("p (c n) -> p c n", c=FF // P),
                                 a["ew2"][e].rearrange("(c p) n -> p c n", p=P)).then_inc(s_we, 16)

                for e in range(EARLY):
                    first(e)
                sp.wait_ge(done[4].sem, done[4].past(TT))
                for e in range(EARLY, E):
                    first(e)
                for e in range(2, E):
                    second(e)
                for b in range(B):
                    sp.wait_ge(keep_s.sem, keep_s.past(b + 1))
                    sp.dma_start(xs_d[b * S:(b + 1) * S, :].rearrange("(t p) d -> p t d", p=P),
                                 xkeep[:, TB * b:TB * b + TB, :]).then_inc(s_kd, 16)
                sp.wait_ge(routed.sem, routed.past(1))
                for e in range(2):
                    second(e)
                sp.wait_ge(s_kd, B * 16)
                for w, key in ((w3a, "w3a"), (w3b, "w3b"), (w3f, "w3f")):
                    sp.dma_start(w, a[key].rearrange("(c p) n -> p c n", p=P)).then_inc(s_w[7], 16)
                sp.dma_start(bc3, a["bc3"].partition_broadcast(P)).then_inc(s_w[7], 16)
                sp.dma_start(xkeep[:, 13:14, :], a["b2"].partition_broadcast(P)).then_inc(s_w[7], 16)

                def store(j, u):
                    sp.wait_ge(m_ys.sem, m_ys.past(j + 1))
                    sp.dma_start(ys_d[bass.ds(j * P, P), :], ysb[u]).then_inc(s_st[u].sem, 16)

                with sp.Fori(0, MT // 3) as r:
                    for u in range(3):
                        store(r * 3 + u, u)
            last = min(phases, 8)
            if last == 8:
                for b in range(B):
                    sp.wait_ge(done[8].sem, done[8].past(TB * (b + 1)))
                    sp.dma_start(out[b].rearrange("(t p) d -> p t d", p=P), x[:, TB * b:TB * b + TB, :]).then_inc(s_out, 16)
                sp.wait_ge(s_out, 16 * B)
            else:
                sp.wait_ge(done[last].sem, done[last].past(TT))
                sp.dma_start(out.rearrange("b (t p) d -> p (b t) d", p=P), x[:, :, :]).then_inc(s_out, 16)
                sp.wait_ge(s_out, 16)

        @block.gpsimd
        def _(gp):
            gp.wait_ge(s_seeded, 1)

            def ln_rstd(n, bb, eps):
                for p in range(2):
                    gp.wait_ge(stat[n].sem, stat[n].past(4 * bb + 2 * p + 2))
                    gp.wait_ge(nrm[n].sem, nrm[n].past(2 * bb))
                    apart(gp)
                    nc.gpsimd.tensor_scalar(rs[p][:, :], mv[p][:, :, 1], eps, None, ALU.add).then_inc(pool[n].sem, 1)
                    gp.wait_ge(pool[n].sem, pool[n].past(2 * bb + p + 1))
                    nc.gpsimd.tensor_tensor(rs[p][:, :], rs[p][:, :], mhalf[:, :], ALU.pow).then_inc(rstd[n].sem, 1)

            nc.gpsimd.memset(ones[:, :], 1.0).then_inc(s_setp.sem, 1)
            nc.gpsimd.memset(mhalf[:, :], -0.5).then_inc(s_setp.sem, 1)
            nc.gpsimd.memset(mone[:, :], -1.0).then_inc(s_setp.sem, 1)

            def heads_keys(n, bb, batches=(0, 1)):
                for p in batches:
                    b = 2 * bb + p
                    if not (isinstance(bb, int) and bb == 0):
                        gp.wait_ge(sc_p[n].sem, sc_p[n].past(ITEMS * bb - 1 + p))
                    dst = kb[p].rearrange("p g (h k) -> p g h k", h=HG)
                    if n == 0:
                        src = kall[:, :, bass.ds(b * KEYS, KEYS)].unsqueeze(2).broadcast_to([P, GR, HG, KEYS])
                        sel = hsel[:, 0:4].unsqueeze(1).unsqueeze(3).broadcast_to([P, GR, HG, KEYS])
                        nc.gpsimd.tensor_tensor(dst, src, sel, ALU.mult).then_inc(kb_s[n].sem, 1)
                    else:
                        for c in range(CH):
                            d2 = kb[p][:, 2 * c:2 * c + 2, :].rearrange("p g (h k) -> p (g h) k", h=HG)
                            src = kall[:, c, bass.ds(b * KEYS, KEYS)].unsqueeze(1).broadcast_to([P, 8, KEYS])
                            sel = hsel[:, 4:12].unsqueeze(2).broadcast_to([P, 8, KEYS])
                            ins = nc.gpsimd.tensor_tensor(d2, src, sel, ALU.mult)
                        ins.then_inc(kb_s[n].sem, 1)

            def biased(n, bb):
                gp.wait_ge(nrm[n].sem, nrm[n].past(2 * bb + 2))
                rows4 = x[:, bass.ds(4 * bb, 4), :]
                nc.gpsimd.tensor_tensor(rows4, rows4, gb[:, n // 4:n // 4 + 1, :].broadcast_to([P, 4, D]), ALU.add
                                        ).then_inc(xb_s[n].sem, 1)

            def heads(n, bb, ahead):
                if n == 0:
                    biased(n, bb)
                if n == 4:
                    for i in range(ITEMS):
                        u = i % 2
                        gp.wait_ge(tk_s.sem, tk_s.past(ITEMS * bb + i + 1))
                        dv = dd[u].rearrange("p t (h k) -> p t h k", h=HG)
                        mn = mx[u][:, :].rearrange("p (t h) -> p t h", t=TB).unsqueeze(3)
                        nc.gpsimd.tensor_tensor(dv, dv, mn.broadcast_to([P, TB, HG, KEYS]), ALU.subtract
                                                ).then_inc(sc_d.sem, 1)
                        if i == 2:
                            biased(n, bb)
                        if i == 4 and ahead:
                            ln_rstd(n, bb + 1, 1e-5)
                        if i in (5, 6) and ahead:
                            heads_keys(n, bb + 1, (i - 5,))
                elif ahead:
                    ln_rstd(n, bb + 1, 1e-5)
                    heads_keys(n, bb + 1)

            gp.wait_ge(s_setp.sem, s_setp.past(2))
            ln_rstd(0, 0, 1e-5)
            gp.wait_ge(prep_a[0].sem, prep_a[0].past(8))
            gp.wait_ge(s_cst, 7 * 16)
            heads_keys(0, 0)
            gp.wait_ge(s_set.sem, s_set.past(5))
            with gp.Fori(0, PAIRS - 1) as bb:
                heads(0, bb, True)
            heads(0, PAIRS - 1, False)
            if phases >= 1:
                ahead_steps(gp, lambda q, own, ahead: ln_rstd(1, q + 1, 1e-5) if ahead else None)
            if phases >= 2:
                ahead_steps(gp, lambda q, own, ahead: ln_rstd(2, q + 1, 1e-5) if ahead else None)
            if phases >= 3:
                gp.wait_ge(s_setp.sem, s_setp.past(3))
                gp.wait_ge(prep_v[3].sem, prep_v[3].past(16))

                def bit_rstd(b, p):
                    gp.wait_ge(stat[3].sem, stat[3].past(2 * b + 2))
                    apart(gp)
                    nc.gpsimd.tensor_scalar(rs[p][:, :], mv[p][:, :, 1], 1e-5, None, ALU.add).then_inc(pool[3].sem, 1)
                    gp.wait_ge(pool[3].sem, pool[3].past(b + 1))
                    nc.gpsimd.tensor_tensor(rs[p][:, :], rs[p][:, :], mhalf[:, :], ALU.pow).then_inc(rstd[3].sem, 1)

                def bit_scales(b, p):
                    big, fac = sm[:, p, 0, 0:TB], sm[:, p, 1, 0:TB]
                    gp.wait_ge(q_m.sem, q_m.past(b + 1))
                    apart(gp)
                    nc.gpsimd.tensor_scalar(fac, big, EPS_Q, 1.0 / QB, ALU.max, ALU.mult).then_inc(q_c.sem, 1)
                    nc.gpsimd.tensor_scalar(big, big, EPS_Q, wstat[:, 4:5], ALU.max, ALU.mult).then_inc(q_r.sem, 1)
                    gp.wait_ge(q_c.sem, q_c.past(b + 1))
                    nc.gpsimd.tensor_tensor(fac, fac, mone[:, :], ALU.pow).then_inc(q_r.sem, 1)
                    gp.wait_ge(nrm[3].sem, nrm[3].past(b + 1))
                    two = x[:, bass.ds(2 * b, 2), :]
                    nc.gpsimd.tensor_tensor(two, two, b2bc.unsqueeze(1).broadcast_to([P, TB, D]), ALU.add
                                            ).then_inc(xb_s[3].sem, 1)

                def bit_hidden(t, u):
                    big, fac = sm[:, u % 2, 2, u // 2:u // 2 + 1], sm[:, u % 2, 3, u // 2:u // 2 + 1]
                    gp.wait_ge(h_m.sem, h_m.past(t + 1))
                    apart(gp)
                    nc.gpsimd.tensor_scalar(fac, big, EPS_Q, 1.0 / QB, ALU.max, ALU.mult).then_inc(h_c.sem, 1)
                    nc.gpsimd.tensor_scalar(big, big, EPS_Q, wstat[:, 5:6], ALU.max, ALU.mult).then_inc(h_w.sem, 1)
                    gp.wait_ge(h_c.sem, h_c.past(t + 1))
                    nc.gpsimd.tensor_tensor(fac, fac, mone[:, 0:1], ALU.pow).then_inc(h_r.sem, 1)

                def bit_step(r, k):
                    t = 4 * r + k
                    if 1 <= k < TT + 1:
                        bit_hidden(t - 1, (k - 1) % 4)
                    if k % 2 == 0 and (k + 4) // 2 < B:
                        bit_rstd(2 * r + (k + 4) // 2, (k + 4) // 2 % 2)
                    if k % 2 and (k + 3) // 2 < B:
                        bit_scales(2 * r + (k + 3) // 2, (k + 3) // 2 % 2)

                bit_steps(gp, bit_step)
            if phases >= 4:
                gp.wait_ge(prep_a[4].sem, prep_a[4].past(4))
                ln_rstd(4, 0, 1e-5)
                heads_keys(4, 0)
                with gp.Fori(0, PAIRS - 1) as bb:
                    heads(4, bb, True)
                heads(4, PAIRS - 1, False)
            if phases >= 5:
                ahead_steps(gp, lambda q, own, ahead: ln_rstd(5, q + 1, 1e-5) if ahead else None)
            if phases >= 6:
                gp.wait_ge(s_kd, B * 16)
                gp.wait_ge(keep_s.sem, keep_s.past(B))
                gp.wait_ge(inv_s.sem, inv_s.past(1))
                for j in range(MT):
                    gp.wait_ge(m_xp.sem, m_xp.past(max(j - 2, 0)))
                    gp.indirect_dma_start(xsb[j % 3], None, xs_d,
                                          bass.IndirectOffsetOnAxis(ap=rown[:, j:j + 1], axis=0)).then_inc(s_ld[j % 3], 16)
                gp.wait_ge(m_y.sem, m_y.past(MT))
                for u in range(3):
                    gp.wait_ge(s_st[u].sem, s_st[u].past(MT // 3 * 16))

                def gather(q):
                    for t in range(4 * q, 4 * q + 4):
                        for k in range(2):
                            gp.indirect_dma_start(got[:, k, t, :], None, ys_d,
                                                  bass.IndirectOffsetOnAxis(ap=slot[:, k, t:t + 1], axis=0)
                                                  ).then_inc(s_ga[q], 16)

                gather(0)
                gather(1)
                if phases == 6:
                    gather(2)
                    gather(3)
            if phases >= 7:
                gp.wait_ge(g7_s.sem, g7_s.past(2))

                def step7(q):
                    attn, ff, norms = has(q)
                    if norms:
                        ln_rstd(7, q + 1, 1e-5)
                    if attn:
                        for p in range(2):
                            b = 2 * q + p
                            gp.wait_ge(va_s.sem, va_s.past(b + 1))
                            apart(gp)
                            nc.gpsimd.tensor_scalar(rs_a[p][:, :, 0], mv_a[p][:, :, 1], 1e-6, None, ALU.add
                                                    ).then_inc(ra_c.sem, 1)
                            gp.wait_ge(ra_c.sem, ra_c.past(b + 1))
                            nc.gpsimd.tensor_tensor(rs_a[p][:, :, 0], rs_a[p][:, :, 0], mhalf[:, :], ALU.pow
                                                    ).then_inc(ra_s.sem, 1)
                    if ff:
                        for p in range(2):
                            b = 2 * q - 2 + p
                            gp.wait_ge(vb_s.sem, vb_s.past(b + 1))
                            apart(gp)
                            nc.gpsimd.tensor_scalar(rs_b[p][:, :, 0], mv_b[p][:, :, 1], 1e-6, None, ALU.add
                                                    ).then_inc(rb_c.sem, 1)
                            gp.wait_ge(rb_c.sem, rb_c.past(b + 1))
                            nc.gpsimd.tensor_tensor(rs_b[p][:, :, 0], rs_b[p][:, :, 0], mhalf[:, :], ALU.pow
                                                    ).then_inc(rb_s.sem, 1)
                    if norms:
                        gp.wait_ge(nrm[7].sem, nrm[7].past(2 * q + 4))
                        rows4 = x[:, bass.ds(4 * (q + 1), 4), :]
                        nc.gpsimd.tensor_tensor(rows4, rows4, betg.unsqueeze(1).broadcast_to([P, 4, D]), ALU.add
                                                ).then_inc(xb_s[7].sem, 1)

                step7(-1)
                gather(2)
                step7(0)
                gather(3)
                last_steps(gp, step7, 1)
            if phases >= 8:
                ahead_steps(gp, lambda q, own, ahead: ln_rstd(8, q + 1, 1e-5) if ahead else None)

        @block.scalar
        def _(ac):
            for s in seeds:
                ac.sem_inc(s, 1)
            ac.sem_inc(s_seeded, 1)

            def copy(dst, src):
                return nc.scalar.activation(dst, src, ACT.Copy)

            def turned(n, bb, used, per):
                for p in range(2):
                    ac.wait_ge(xtp[n].sem, xtp[n].past(2 * bb + p + 1))
                    ac.wait_ge(used.sem, used.past(per * bb))
                    copy(xnT[p][:, :, :].rearrange("p c s -> p (c s)"), bank(p)).then_inc(xts[n].sem, 1)

            ac.wait_ge(s_cst, 7 * 16)
            nc.scalar.activation(gates[:, :], graw[:, :], ACT.Tanh).then_inc(s_gate.sem, 1)
            for c in range(CH):
                for h in range(2):
                    ac.wait_ge(s_ctp.sem, s_ctp.past(2 * c + h + 1))
                    copy(ctxT[:, c, h * HALF:(h + 1) * HALF], bank(2 * c + h)[:, 0:HALF]).then_inc(s_cta.sem, 1)

            ac.wait_ge(s_set.sem, s_set.past(3))
            for j in range(2 * GR):
                ac.wait_ge(prep_p[0].sem, prep_p[0].past(j + 1))
                nc.scalar.activation(kall[:, j // 2, (j % 2) * HALF:(j % 2 + 1) * HALF], bank(j)[:, 0:HALF], ACT.Exp,
                                     bias=cols[:, 0:1]).then_inc(prep_a[0].sem, 1)

            def queries(n, bb):
                for p in range(2):
                    ac.wait_ge(q_p[n].sem, q_p[n].past(2 * bb + p + 1))
                    if n == 0:
                        nc.scalar.activation(wk[p][:, :, :].rearrange("p (u g) s -> p u (g s)", u=2),
                                             ps[1 - p][:, :, :], ACT.Exp, bias=cols[:, 0:1]).then_inc(q_s[n].sem, 1)
                    else:
                        for m in range(CH):
                            nc.scalar.activation(wk[p][:, m, :], bank(2 + p)[:, m * S:(m + 1) * S], ACT.Identity,
                                                 bias=cols[:, 12 + m:13 + m], scale=-0.25).then_inc(q_s[n].sem, 1)

            def heads(n):
                top = n == 4
                lag = 1 if top else 0

                def step(bb, s, ahead):
                    if ahead and s == ITEMS:
                        queries(n, bb + 1)
                    if top and live(s, ahead):
                        ac.wait_ge(sc_p[n].sem, sc_p[n].past(ITEMS * bb + s + 1))
                        nc.scalar.activation(dd[s % 2][:, :, :], ps[s % 2][:, :, 0:GK], ACT.Copy).then_inc(sc_r[n].sem, 1)
                    if ahead and s == ITEMS - 1:
                        turned(n, bb + 1, q_p[n], 2)
                    i = s - lag
                    if live(i, ahead):
                        u = i % 2
                        row = pr[u]
                        if top:
                            ac.wait_ge(sc_d.sem, sc_d.past(ITEMS * bb + i + 1))
                            ac.wait_ge(pt_p[n].sem, pt_p[n].past(least(ITEMS * bb + i - 1)))
                            nc.scalar.activation(row[:, :, :], dd[u][:, :, :], ACT.Abs).then_inc(s_ab.sem, 1)
                            ac.wait_ge(s_ab.sem, s_ab.past(ITEMS * bb + i + 1))
                            apart(ac)
                            nc.scalar.activation(row[:, :, :], row[:, :, :], ACT.Exp,
                                                 scale=mcol[:, bass.ds(2 * (bb + i // ITEMS) + u, 1)]
                                                 ).then_inc(ex_s[n].sem, 1)
                        else:
                            ac.wait_ge(sc_r[n].sem, sc_r[n].past(ITEMS * bb + i + 1))
                            nc.scalar.activation(row[:, :, :], row[:, :, :], ACT.Exp, scale=1.0 / 16).then_inc(ex_s[n].sem, 1)
                    i = s - 1 - lag
                    if live(i, ahead):
                        ac.wait_ge(pt_p[n].sem, pt_p[n].past(ITEMS * bb + i + 1))
                        ac.wait_ge(pv_p[n].sem, pv_p[n].past(least(ITEMS * bb + i - 1)))
                        nc.scalar.activation(pt[i % 2][:, :].rearrange("p (u n) -> p u n", u=2), ps[2][0:KEYS, :, :],
                                             ACT.Copy).then_inc(pt_s[n].sem, 1)
                    i = s - 3 - lag
                    if live(i, ahead) and (not top or i // 2 % 2):
                        j = i % ITEMS
                        k = ITEMS * bb + i if not top else ITEMS // 2 * (bb + i // ITEMS) + j // 4 * 2 + i % 2
                        ac.wait_ge(ot_p[n].sem, ot_p[n].past(k + 1))
                        if j < 4:
                            ac.wait_ge(f_p[n].sem, f_p[n].past(4 * (bb + i // ITEMS)))
                        copy(oT[i % 2][:, j // 4 if top else j // 2, :], bank(7)[:, 0:S]).then_inc(ot_s[n].sem, 1)

                head_steps(ac, n, step)

            turned(0, 0, q_p[0], 2)
            queries(0, 0)
            heads(0)

            def single(n, bb):
                for p in range(2):
                    ac.wait_ge(sc_r[n].sem, sc_r[n].past(2 * bb + p + 1))
                    nc.scalar.activation(pr[p][:, :, 0:KEYS], pr[p][:, :, 0:KEYS], ACT.Exp,
                                         scale=1.0 / 16).then_inc(ex_s[n].sem, 1)
                for p in range(2):
                    ac.wait_ge(pt_p[n].sem, pt_p[n].past(2 * bb + p + 1))
                    ac.wait_ge(pv_p[n].sem, pv_p[n].past(2 * bb))
                    copy(pt[p][:, 0:S], bank(6 + p)[0:KEYS, 0:S]).then_inc(pt_s[n].sem, 1)

            if phases >= 1:
                ac.wait_ge(done[0].sem, done[0].past(TT))
                ahead_steps(ac, lambda q, own, ahead: turned(1, q + 1, f_p[1], 4) if ahead else None)
            if phases >= 2:
                ac.wait_ge(done[1].sem, done[1].past(TT))
                for j in range(4):
                    ac.wait_ge(prep_p[2].sem, prep_p[2].past(j + 1))
                    nc.scalar.activation(kall[:, j // 2, (j % 2) * HALF:(j % 2 + 1) * HALF], bank(j)[:, 0:HALF],
                                         ACT.Identity, bias=cols[:, 3 + j // 2:4 + j // 2]).then_inc(prep_a[2].sem, 1)

                def step2(q, own, ahead):
                    if own:
                        single(2, q)
                    if ahead:
                        turned(2, q + 1, q_p[2], 2)
                        for p in range(2):
                            ac.wait_ge(q_p[2].sem, q_p[2].past(2 * q + 2 + p + 1))
                            ac.wait_ge(sc_p[2].sem, sc_p[2].past(2 * q + 2))
                            for m in range(CH):
                                nc.scalar.activation(wk[p][:, m, :], bank(2 + p)[:, m * S:(m + 1) * S], ACT.Identity,
                                                     bias=cols[:, 1 + m:2 + m]).then_inc(q_s[2].sem, 1)

                ahead_steps(ac, step2)
            if phases >= 3:
                ac.wait_ge(done[2].sem, done[2].past(TT))

                def bit_step(r, k):
                    t, b, p = 4 * r + k, 2 * r + (k + 1) // 2, (k + 1) // 2 % 2
                    if k % 2 and (k + 1) // 2 < B and k >= -1:
                        ac.wait_ge(xtp[3].sem, xtp[3].past(b + 1))
                        ac.wait_ge(h_p.sem, h_p.past(least(2 * b - 2)))
                        copy(xnT[p][:, 0, :].bitcast(bf16), bank(4)[:, 0:S].bitcast(bf16)).then_inc(xts[3].sem, 1)
                    if 0 <= k < TT:
                        ac.wait_ge(h_b.sem, h_b.past(t + 1))
                        hrow = wk[k % 2][:, :, :].rearrange("p c s -> p (c s)")
                        nc.scalar.activation(hrow, hrow, ACT.Gelu).then_inc(g_s.sem, 1)
                    if 1 <= k < TT + 1:
                        u = (k - 1) % 4
                        ac.wait_ge(h_r.sem, h_r.past(t))
                        ac.wait_ge(h_z.sem, h_z.past(least(t - 2)))
                        hrow = wk[u % 2][:, :, :].rearrange("p c s -> p (c s)")
                        nc.scalar.activation(hmag[u % 2], hrow, ACT.Copy, scale=sm[:, u % 2, 3, u // 2:u // 2 + 1],
                                             bias=MAGIC).then_inc(hq_s.sem, 1)
                    if 2 <= k < TT + 2:
                        ac.wait_ge(ht_p.sem, ht_p.past(t - 1))
                        ac.wait_ge(f_p[3].sem, f_p[3].past(least(t - 3)))
                        copy(pr[k % 2].rearrange("p t n -> p (t n)")[:, 0:512].bitcast(bf16),
                             bank(5).bitcast(bf16)).then_inc(ht_s.sem, 1)

                bit_steps(ac, bit_step)
            if phases >= 4:
                ac.wait_ge(done[3].sem, done[3].past(TT))
                ac.wait_ge(s_w[4], 5 * 16)
                ac.wait_ge(s_set.sem, s_set.past(3))
                for j in range(4):
                    ac.wait_ge(prep_p[4].sem, prep_p[4].past(j + 1))
                    nc.scalar.activation(kall[:, j // 2, (j % 2) * HALF:(j % 2 + 1) * HALF], bank(j)[:, 0:HALF],
                                         ACT.Identity, bias=cols[:, 7 + j // 2:8 + j // 2]).then_inc(prep_a[4].sem, 1)
                ac.wait_ge(prep_v[4].sem, prep_v[4].past(6))
                turned(4, 0, q_p[4], 2)
                queries(4, 0)
                heads(4)
            if phases >= 5:
                ac.wait_ge(done[4].sem, done[4].past(TT))

                def step5(q, own, ahead):
                    if ahead:
                        for p in range(2):
                            ac.wait_ge(nrm[5].sem, nrm[5].past(2 * q + 2 + p + 1))
                            copy(xkeep[:, bass.ds(4 * q + 4 + 2 * p, 2), :], xn[p][:, :, :]).then_inc(keep_s.sem, 1)
                        turned(5, q + 1, lg_p, 2)

                ahead_steps(ac, step5)
                ac.wait_ge(rt_v.sem, rt_v.past(1))
                nc.scalar.activation(gate2[:, :, 1], gate2[:, :, 0], ACT.Exp).then_inc(rt_a.sem, 1)
            if phases >= 6:
                ac.wait_ge(routed.sem, routed.past(1))

                def gelu(j):
                    ac.wait_ge(m_h.sem, m_h.past(j + 1))
                    ac.wait_ge(m_tp.sem, m_tp.past(j))
                    nc.scalar.activation(hid[:, :, :].rearrange("p (v c) s -> p v (c s)", v=2), ps[0][:, :, :],
                                         ACT.Gelu).then_inc(m_g.sem, 1)

                def result(j, u, k):
                    ac.wait_ge(m_y.sem, m_y.past(j + 1))
                    ac.wait_ge(s_st[u].sem, s_st[u].past(16 * k))
                    copy(ysb[u], bank(4)[:, 0:D]).then_inc(m_ys.sem, 1)

                gelu(0)
                with ac.Fori(0, (MT - 3) // 3) as r:
                    for u in range(3):
                        j = r * 3 + u + 1
                        gelu(j)
                        result(j - 1, u, r)
                for j in range(MT - 2, MT):
                    gelu(j)
                    result(j - 1, (j - 1) % 3, (j - 1) // 3)
                result(MT - 1, (MT - 1) % 3, (MT - 1) // 3)
            if phases >= 7:

                def step7(q):
                    attn, ff, norms = has(q)
                    if ff:
                        for p in range(2):
                            b = 2 * q - 2 + p
                            ac.wait_ge(x7_p.sem, x7_p.past(b + 1))
                            copy(xbT[p].rearrange("p c s -> p (c s)"), bank(2 + p)).then_inc(x7_t.sem, 1)
                    if attn:
                        for p in range(2):
                            ac.wait_ge(sc_r[7].sem, sc_r[7].past(2 * q + p + 1))
                            nc.scalar.activation(pr[p][:, :, 0:KEYS], pr[p][:, :, 0:KEYS], ACT.Exp,
                                                 scale=1.0 / 16).then_inc(ex_s[7].sem, 1)
                    if ff:
                        for p in range(2):
                            b = 2 * q - 2 + p
                            ac.wait_ge(h7_p.sem, h7_p.past(b + 1))
                            for m in range(CH):
                                ins = nc.scalar.activation(wk[p][:, m, :], bank(4 + p)[:, m * S:(m + 1) * S], ACT.Relu,
                                                           bias=cols[:, 9 + m:10 + m])
                            ins.then_inc(h7_s.sem, 1)
                    if attn:
                        for p in range(2):
                            ac.wait_ge(pt_p[7].sem, pt_p[7].past(2 * q + p + 1))
                            copy(pt[p][:, 0:S], bank(6 + p)[0:KEYS, 0:S]).then_inc(pt_s[7].sem, 1)
                    if norms:
                        for p in range(2):
                            ac.wait_ge(xtp[7].sem, xtp[7].past(2 * q + 2 + p + 1))
                            copy(xnT[p][:, :, :].rearrange("p c s -> p (c s)"), bank(p)).then_inc(xts[7].sem, 1)

                last_steps(ac, step7)
            if phases >= 8:
                ac.wait_ge(done[7].sem, done[7].past(TT))
                ahead_steps(ac, lambda q, own, ahead: turned(8, q + 1, f_p[8], 4) if ahead else None)

        @block.vector
        def _(ve):
            ve.wait_ge(s_seeded, 1)

            def ln_stats(n, bb):
                for p in range(2):
                    for t in range(TB):
                        nc.vector.bn_stats(st[p][:, t, :], x[:, 4 * bb + 2 * p + t, :]).then_inc(dve[n].sem, 1)
                for p in range(2):
                    for t in range(TB):
                        ve.wait_ge(dve[n].sem, dve[n].past(4 * bb + 2 * p + t + 1))
                        ve.wait_ge(rstd[n].sem, rstd[n].past(2 * bb))
                        apart(ve)
                        nc.vector.bn_aggr(mv[p][:, t, :], st[p][:, t, :]).then_inc(stat[n].sem, 1)

            def ln_rows(n, bb, used):
                for p in range(2):
                    ve.wait_ge(rstd[n].sem, rstd[n].past(2 * bb + p + 1))
                    ve.wait_ge(used.sem, used.past(2 * bb))
                    for t in range(TB):
                        ins = nc.vector.tensor_scalar(xn[p][:, t, :], x[:, 4 * bb + 2 * p + t, :], mv[p][:, t, 0:1],
                                                      rs[p][:, t:t + 1], ALU.subtract, ALU.mult)
                    ins.then_inc(nrm[n].sem, 1)

            def ln(n, bb, used):
                ln_stats(n, bb)
                ln_rows(n, bb, used)

            def residual(n, bb, p, t, src, factor):
                row = x[:, 4 * bb + 2 * p + t, :]
                nc.vector.scalar_tensor_tensor(row, src, factor, row, ALU.mult, ALU.add).then_inc(done[n].sem, 1)

            ve.wait_ge(s_cst, 7 * 16)
            ve.wait_ge(s_w[0], 3 * 16)
            ve.wait_ge(s_ctx, 2 * 16)
            nc.vector.tensor_copy(identb[:, :], ident[:, :]).then_inc(s_set.sem, 1)
            neg = fmw[:, :, :].rearrange("p g (h s e) -> p (g h) s e", h=HG, s=2)[:, :, 1, :]
            nc.vector.tensor_scalar(neg, neg, -1.0, None, ALU.mult).then_inc(s_set.sem, 1)
            nc.vector.tensor_tensor(cols[:, 0:1], cols[:, 0:1], cols[:, 15:16], ALU.mult).then_inc(s_set.sem, 1)
            v0 = vall[:, 0:B * HEADS * 33].rearrange("p (b h e) -> p b h e", b=B, h=HEADS)
            nc.vector.memset(vall[:, 0:B * HEADS * 33].rearrange("p (q e) -> p q e", e=33)[:, :, 32:33], 1.0)
            ve.wait_ge(s_x, 16)
            ln(0, 0, xtp[0])
            for b in range(B):
                ve.wait_ge(prep_p[0].sem, prep_p[0].past(8 + b + 1))
                nc.vector.tensor_copy(v0[:, b, :, 0:32], bank(b)[0:KEYS, :].rearrange("p (h e) -> p h e", h=HEADS)
                                      ).then_inc(prep_v[0].sem, 1)
            ve.wait_ge(s_gate.sem, s_gate.past(1))
            for k in range(2):
                nc.vector.tensor_scalar(gb[:, k, :], gb[:, k, :], gates[:, 2 * k:2 * k + 1], None, ALU.mult
                                        ).then_inc(s_set.sem, 1)

            def drop_least(bb, i):
                u, base = i % 2, (ITEMS * bb + i) * 9
                d = [dd[u][:, j // HG, (j % HG) * KEYS:(j % HG + 1) * KEYS] for j in range(8)]

                def wait(k):
                    ve.wait_ge(tk_r.sem, tk_r.past(base + k))
                    apart(ve)

                for half in range(2):
                    for j in range(4 * half, 4 * half + 4):
                        ins = nc.vector.max(m8[u][:, j, :], d[j])
                    ins.then_inc(tk_r.sem, 1)
                for half in range(2):
                    wait(1 + half)
                    for j in range(4 * half, 4 * half + 4):
                        ins = nc.vector.match_replace(d[j], m8[u][:, j, :], d[j], -BIG)
                    ins.then_inc(tk_r.sem, 1)
                for half in range(2):
                    wait(3 + half)
                    for j in range(4 * half, 4 * half + 4):
                        ins = nc.vector.max(m8b[u][:, j, :], d[j])
                    ins.then_inc(tk_r.sem, 1)
                for half in range(2):
                    wait(5 + half)
                    nc.vector.memset(m8b[u][:, 4 * half:4 * half + 4, DROP - 8:8], -BIG).then_inc(tk_r.sem, 1)
                for half in range(2):
                    wait(7 + half)
                    for j in range(4 * half, 4 * half + 4):
                        ins = nc.vector.match_replace(d[j], m8b[u][:, j, :], d[j], -BIG)
                    ins.then_inc((tk_s if half else tk_r).sem, 1)

            def heads(n):
                top = n == 4
                vd = 16 if top else 32
                lag = 1 if top else 0

                def step(bb, s, ahead):
                    if ahead and s == 4:
                        ln_stats(n, bb + 1)
                    if ahead and s == 6:
                        ln_rows(n, bb + 1, xtp[n])
                    if live(s, ahead):
                        i, u = s, s % 2
                        mxv = mx[u][:, :].rearrange("p (t h) -> p t h", t=TB)
                        if not top:
                            sv = ps[u][:, :, 0:GK].rearrange("p t (h k) -> p t h k", h=HG)
                            ve.wait_ge(sc_p[n].sem, sc_p[n].past(ITEMS * bb + i + 1))
                            nc.vector.tensor_reduce(mxv, sv, AX.X, ALU.max).then_inc(act[n].sem, 1)
                            ve.wait_ge(act[n].sem, act[n].past(ITEMS * bb + i + 1))
                            ve.wait_ge(pt_p[n].sem, pt_p[n].past(least(ITEMS * bb + i - 1)))
                            nc.vector.tensor_tensor(pr[u].rearrange("p t (h k) -> p t h k", h=HG), sv,
                                                    mxv.unsqueeze(3).broadcast_to([P, TB, HG, KEYS]), ALU.subtract
                                                    ).then_inc(sc_r[n].sem, 1)
                        else:
                            ve.wait_ge(sc_r[n].sem, sc_r[n].past(ITEMS * bb + i + 1))
                            ve.wait_ge(sc_d.sem, sc_d.past(least(ITEMS * bb + i - 1)))
                            nc.vector.tensor_reduce(mxv, dd[u].rearrange("p t (h k) -> p t h k", h=HG), AX.X, ALU.min
                                                    ).then_inc(act[n].sem, 1)
                            drop_least(bb, i)
                    i = s - 2 - lag
                    if live(i, ahead):
                        u, j = i % 2, i % ITEMS
                        ve.wait_ge(pv_p[n].sem, pv_p[n].past(ITEMS * bb + i + 1))
                        ov = bank(6)[:, 0:8 * (vd + 1)].rearrange("p (j e) -> p j e", j=8)
                        nc.vector.reciprocal(rden[u][:, :], ov[:, :, vd]).then_inc(s_rd[n].sem, 1)
                        ve.wait_ge(s_rd[n].sem, s_rd[n].past(ITEMS * bb + i + 1))
                        ve.wait_ge(ot_p[n].sem, ot_p[n].past(least(ITEMS * bb + i - 1) if not top else ITEMS // 2
                                                             * (bb + i // ITEMS) + (0 if j < 4 else 1 + i % 2)))
                        at = i // 2 % 2 * HG * vd if top else 0
                        nc.vector.tensor_tensor(osb[u][:, :, at:at + HG * vd].rearrange("p t (h e) -> p t h e", h=HG),
                                                ov[:, :, 0:vd].rearrange("p (t h) e -> p t h e", t=TB),
                                                rden[u][:, :].rearrange("p (t h) -> p t h", t=TB).unsqueeze(3)
                                                .broadcast_to([P, TB, HG, vd]), ALU.mult).then_inc(o_s[n].sem, 1)
                    if s == ITEMS + 2 + lag:
                        ve.wait_ge(xb_s[n].sem, xb_s[n].past(bb + 1))
                        for p in range(2):
                            ve.wait_ge(f_p[n].sem, f_p[n].past(4 * bb + 2 * p + 2))
                            two = x[:, bass.ds(4 * bb + 2 * p, 2), :]
                            nc.vector.scalar_tensor_tensor(two, bank(7 - p).rearrange("p (t d) -> p t d", t=TB),
                                                           gates[:, n // 2:n // 2 + 1], two, ALU.mult, ALU.add
                                                           ).then_inc(done[n].sem, 2)

                head_steps(ve, n, step)

            heads(0)

            if phases >= 1:
                ve.wait_ge(s_w[1], 16)
                ve.wait_ge(done[0].sem, done[0].past(TT))
                c1 = Chain(ve, prep_v[1])
                wv = sgw[:, :, :].rearrange("p c n -> p (c n)")
                tmp = ktmp[:, 0:CH * D]
                c1.link(nc.vector.tensor_scalar(tmp, wv, 0.0, None, ALU.is_lt))
                c1.link(nc.vector.scalar_tensor_tensor(wv, wv, 0.0, tmp, ALU.is_gt, ALU.subtract))

                def step1(q, own, ahead):
                    if ahead:
                        ln(1, q + 1, xtp[1])
                    if own:
                        for p in range(2):
                            ve.wait_ge(f_p[1].sem, f_p[1].past(4 * q + 2 * p + 2))
                            two = x[:, bass.ds(4 * q + 2 * p, 2), :]
                            nc.vector.scalar_tensor_tensor(two, ps[2 + p][:, :, 0:D], gates[:, 4:5], two, ALU.mult,
                                                           ALU.add).then_inc(done[1].sem, 2)

                ahead_steps(ve, step1)

            def single_soft(n, bb, p):
                ve.wait_ge(sc_p[n].sem, sc_p[n].past(2 * bb + p + 1))
                sv = (bank(4 + p)[:, 0:TB * KEYS] if n == 2 else bank(6 + p)[:, S:S + TB * KEYS]
                      ).rearrange("p (t k) -> p t k", t=TB)
                nc.vector.tensor_reduce(mx[p][:, 0:TB], sv, AX.X, ALU.max).then_inc(act[n].sem, 1)
                ve.wait_ge(act[n].sem, act[n].past(2 * bb + p + 1))
                ve.wait_ge(pt_p[n].sem, pt_p[n].past(2 * bb))
                nc.vector.tensor_tensor(pr[p][:, :, 0:KEYS], sv, mx[p][:, 0:TB].unsqueeze(2)
                                        .broadcast_to([P, TB, KEYS]), ALU.subtract).then_inc(sc_r[n].sem, 1)

            def single_sum(n, bb, p):
                ve.wait_ge(ex_s[n].sem, ex_s[n].past(2 * bb + p + 1))
                nc.vector.tensor_reduce(rden[p][:, 0:TB], pr[p][:, :, 0:KEYS], AX.X, ALU.add).then_inc(s_rd[n].sem, 1)
                ve.wait_ge(s_rd[n].sem, s_rd[n].past(2 * (2 * bb + p) + 1))
                nc.vector.reciprocal(rden[p][:, TB:2 * TB], rden[p][:, 0:TB]).then_inc(s_rd[n].sem, 1)
                ve.wait_ge(s_rd[n].sem, s_rd[n].past(2 * (2 * bb + p) + 2))

            if phases >= 2:
                ve.wait_ge(done[1].sem, done[1].past(TT))
                if phases >= 3:
                    ve.wait_ge(s_w[3], 4 * 16)
                    c3 = Chain(ve, prep_v[3])
                    for k, stg in enumerate((stage1, stage2)):
                        c3.link(nc.vector.tensor_reduce(wstat[:, k:k + 1], stg, AX.X, ALU.add,
                                                        apply_absolute_value=True))
                    for k in range(2):
                        ve.wait_ge(prep_p[3].sem, prep_p[3].past(k + 1))
                        c3.link(nc.vector.tensor_scalar(wstat[:, 2 + k:3 + k], bank(6 + k)[:, 0:1], 1.0 / (D * FF), EPS_Q,
                                                        ALU.mult, ALU.max))
                    for k, (stg, tern) in enumerate(((stage1, tern1), (stage2, tern2))):
                        tv = tern[:, :, :].rearrange("p c n -> p (c n)")
                        c3.link(nc.vector.tensor_scalar(wstat[:, 4 + k:5 + k], wstat[:, 2 + k:3 + k], 0.5, None, ALU.mult))
                        c3.link(nc.vector.tensor_scalar(wstat[:, 6 + k:7 + k], wstat[:, 2 + k:3 + k], -0.5, None, ALU.mult))
                        c3.link(nc.vector.tensor_scalar(vtmp, stg, wstat[:, 4 + k:5 + k], None, ALU.is_gt))
                        c3.link(nc.vector.scalar_tensor_tensor(tv, stg, wstat[:, 6 + k:7 + k], vtmp, ALU.is_lt,
                                                               ALU.subtract))
                        c3.link(nc.vector.tensor_scalar(wstat[:, 4 + k:5 + k], wstat[:, 2 + k:3 + k], -1.0 / QB, None,
                                                        ALU.mult))
                    c3.link(nc.vector.tensor_tensor(wstat[:, 5:6], wstat[:, 5:6], gates[:, 5:6], ALU.mult))
                    c3.link(nc.vector.tensor_scalar(b2bc, b2bc, gates[:, 5:6], None, ALU.mult))
                for j in range(4):
                    ve.wait_ge(prep_p[2].sem, prep_p[2].past(4 + j + 1))
                    nc.vector.tensor_tensor(vall[:, j * 512:(j + 1) * 512].rearrange("p (h d) -> p h d", h=2),
                                            bank(4 + j)[0:KEYS, :].rearrange("p (h d) -> p h d", h=2),
                                            rows[:, 0:1, :].broadcast_to([KEYS, 2, D]), ALU.add).then_inc(prep_v[2].sem, 1)

                def step2(q, own, ahead):
                    if own:
                        for p in range(2):
                            single_soft(2, q, p)
                    if ahead:
                        ln_stats(2, q + 1)
                    if own:
                        for p in range(2):
                            single_sum(2, q, p)
                            nc.vector.tensor_scalar(rden[p][:, 4:4 + TB], rden[p][:, TB:2 * TB], gates[:, 1:2], None,
                                                    ALU.mult).then_inc(dvx[2].sem, 1)
                    if ahead:
                        ln_rows(2, q + 1, xtp[2])
                    if own:
                        ve.wait_ge(dvx[2].sem, dvx[2].past(2 * q + 2))
                        for p in range(2):
                            ve.wait_ge(pv_p[2].sem, pv_p[2].past(2 * q + p + 1))
                            for t in range(TB):
                                residual(2, q, p, t, bank(4 + p)[:, t * D:(t + 1) * D], rden[p][:, 4 + t:5 + t])

                ahead_steps(ve, step2)

            if phases >= 3:
                ve.wait_ge(done[2].sem, done[2].past(TT))

                def bit_stats(b, p):
                    for t in range(TB):
                        nc.vector.bn_stats(st[p][:, t, :], x[:, 2 * b + t, :]).then_inc(dve[3].sem, 1)
                    ve.wait_ge(dve[3].sem, dve[3].past(2 * b + 2))
                    apart(ve)
                    for t in range(TB):
                        nc.vector.bn_aggr(mv[p][:, t, :], st[p][:, t, :]).then_inc(stat[3].sem, 1)

                def bit_rows(b, p):
                    ve.wait_ge(rstd[3].sem, rstd[3].past(b + 1))
                    for t in range(TB):
                        ins = nc.vector.tensor_scalar(xn[p][:, t, :], x[:, 2 * b + t, :], mv[p][:, t, 0:1],
                                                      rs[p][:, t:t + 1], ALU.subtract, ALU.mult)
                    ins.then_inc(nrm[3].sem, 1)
                    ve.wait_ge(nrm[3].sem, nrm[3].past(b + 1))
                    nc.vector.tensor_reduce(sm[:, p, 0, 0:TB], xn[p][:, :, :], AX.X, ALU.max,
                                            apply_absolute_value=True).then_inc(q_m.sem, 1)

                def bit_quant(b, p):
                    ve.wait_ge(q_r.sem, q_r.past(2 * b + 2))
                    for t in range(TB):
                        ins = nc.vector.tensor_scalar(xn[p][:, t, :], xn[p][:, t, :], sm[:, p, 1, t:t + 1], MAGIC,
                                                      ALU.mult, ALU.add)
                    ins.then_inc(dvx[3].sem, 1)
                    ve.wait_ge(dvx[3].sem, dvx[3].past(b + 1))
                    ve.wait_ge(xtp[3].sem, xtp[3].past(least(b - 1)))
                    nc.vector.tensor_scalar(xq[p][:, :, :], xn[p][:, :, :], MAGIC, QB, ALU.subtract, ALU.min
                                            ).then_inc(q_s[3].sem, 1)

                def bit_step(r, k):
                    t = 4 * r + k
                    if 0 <= k < TT:
                        u = k % 4
                        ve.wait_ge(h_p.sem, h_p.past(t + 1))
                        ve.wait_ge(hq_s.sem, hq_s.past(least(t - 1)))
                        hrow = wk[u % 2][:, :, :].rearrange("p (v c) s -> p v (c s)", v=2)
                        nc.vector.scalar_tensor_tensor(hrow, ps[u % 2][:, :, :], sm[:, u // 2, 0, u % 2:u % 2 + 1],
                                                       b1bc.rearrange("p (v n) -> p v n", v=2),
                                                       ALU.mult, ALU.add).then_inc(h_b.sem, 1)
                    if 1 <= k < TT + 1:
                        u = (k - 1) % 4
                        ve.wait_ge(g_s.sem, g_s.past(t))
                        nc.vector.tensor_reduce(sm[:, u % 2, 2, u // 2:u // 2 + 1],
                                                wk[u % 2][:, :, :].rearrange("p c s -> p (c s)"), AX.X, ALU.max,
                                                apply_absolute_value=True).then_inc(h_m.sem, 1)
                    if k % 2 == 0:
                        if -2 <= k and (k + 2) // 2 < B:
                            bit_quant(2 * r + (k + 2) // 2, (k + 2) // 2 % 2)
                        if (k + 4) // 2 < B:
                            bit_stats(2 * r + (k + 4) // 2, (k + 4) // 2 % 2)
                    elif (k + 3) // 2 < B:
                        bit_rows(2 * r + (k + 3) // 2, (k + 3) // 2 % 2)
                    if k >= 3:
                        u = (k - 3) % 4
                        ve.wait_ge(f_p[3].sem, f_p[3].past(t - 2))
                        ve.wait_ge(h_w.sem, h_w.past(t - 2))
                        ve.wait_ge(xb_s[3].sem, xb_s[3].past(2 * r + (k - 3) // 2 + 1))
                        row = x[:, t - 3, :]
                        nc.vector.scalar_tensor_tensor(row, bank(6 + u % 2)[:, 0:D], sm[:, u % 2, 2, u // 2:u // 2 + 1],
                                                       row, ALU.mult, ALU.add).then_inc(done[3].sem, 1)
                    if 1 <= k < TT + 1:
                        u = (k - 1) % 4
                        ve.wait_ge(hq_s.sem, hq_s.past(t))
                        ve.wait_ge(ht_p.sem, ht_p.past(least(t - 2)))
                        nc.vector.tensor_scalar(hq[u % 2], hmag[u % 2], MAGIC, QB, ALU.subtract, ALU.min
                                                ).then_inc(h_z.sem, 1)

                bit_steps(ve, bit_step)

            if phases >= 4:
                ve.wait_ge(done[3].sem, done[3].past(TT))
                ve.wait_ge(s_w[4], 5 * 16)
                c4 = Chain(ve, prep_v[4])
                v2 = vall[:, 0:B * HEADS * 17].rearrange("p (b h e) -> p b h e", b=B, h=HEADS)
                c4.link(nc.vector.tensor_copy(mrow, mrow8[:, :]))
                c4.link(nc.vector.tensor_reduce(mcol[:, :], mrow.rearrange("p (b k) -> p b k", b=B), AX.X, ALU.max))
                c4.link(nc.vector.tensor_scalar(mcol[:, :], mcol[:, :], -1.0, None, ALU.mult))
                c4.link(nc.vector.tensor_scalar(mrow, mrow, -BIG, BIG, ALU.mult, ALU.add))
                c4.link(nc.vector.tensor_scalar(cols[:, 12:14], cols[:, 5:7], -0.25, None, ALU.mult))
                c4.link(nc.vector.memset(vall[:, 0:B * HEADS * 17].rearrange("p (q e) -> p q e", e=17)[:, :, 16:17], 1.0))
                ln(4, 0, xtp[4])
                for j in range(4):
                    ve.wait_ge(prep_p[4].sem, prep_p[4].past(4 + j + 1))
                    for h in range(2):
                        ins = nc.vector.tensor_tensor(v2[:, 2 * j + h, :, 0:16],
                                                      bank(4 + j)[0:KEYS, h * D:(h + 1) * D]
                                                      .rearrange("p (h e) -> p h e", h=HEADS),
                                                      rows[:, 1, :].rearrange("p (h e) -> p h e", h=HEADS), ALU.add)
                    c4.step(ins)
                heads(4)

            if phases >= 5:
                ve.wait_ge(done[4].sem, done[4].past(TT))

                def step5(q, own, ahead):
                    if ahead:
                        ve.wait_ge(keep_s.sem, keep_s.past(2 * q + 2))
                        ln(5, q + 1, xtp[5])
                    if not own:
                        return
                    for p in range(2):
                        ve.wait_ge(lg_p.sem, lg_p.past(2 * q + p + 1))
                        nc.vector.tensor_copy(lg[p][:, :, :], bank(2 + p)[:, 0:TB * E].rearrange(
                            "p (t e) -> p t e", t=TB)).then_inc(rt_l.sem, 1)
                    for p in range(2):
                        ve.wait_ge(rt_l.sem, rt_l.past(2 * q + p + 1))
                        apart(ve)
                        for t in range(TB):
                            nc.vector.max(m8[p][:, t, :], lg[p][:, t, :]).then_inc(rt_m.sem, 1)
                    for p in range(2):
                        for t in range(TB):
                            ve.wait_ge(rt_m.sem, rt_m.past(4 * q + 2 * p + t + 1))
                            apart(ve)
                            nc.vector.max_index(ix[p][:, t, :], m8[p][:, t, :], lg[p][:, t, :]).then_inc(rt_i.sem, 1)
                    for p in range(2):
                        ve.wait_ge(rt_i.sem, rt_i.past(4 * q + 2 * p + 2))
                        nc.vector.tensor_copy(topv[:, bass.ds(4 * q + 2 * p, 2), :], m8[p][:, 0:2, 0:2]).then_inc(rt_c.sem, 1)
                        nc.vector.tensor_copy(topi[:, bass.ds(4 * q + 2 * p, 2), :], ix[p][:, :, 0:2]).then_inc(rt_c.sem, 1)

                ahead_steps(ve, step5)
                ve.wait_ge(rt_c.sem, rt_c.past(16))
                c5 = Chain(ve, rt_v)
                c5.link(nc.vector.tensor_tensor(gate2[:, :, 0], topv[:, :, 1], topv[:, :, 0], ALU.subtract))
                oh = rt[:, 0:256]
                cum = rt[:, 256:512]
                tot = rt[:, 512:768]
                base = rt[:, 768:1024]
                cnt = rt[:, 1024:1040]
                off = rt[:, 1040:1056]
                til = rt[:, 1056:1064]
                end = rt[:, 1064:1072]
                tmp = rt[:, 1280:1536]
                pos = rt[:, 1536:1568]
                where = rt[:, 1568:1600]
                one = rt[:, 1600:1632]
                ef = rt[:, 1632:1632 + 64]
                oh3 = oh.rearrange("p (q e) -> p q e", e=E)
                c5.link(nc.vector.tensor_tensor(oh3, iota[:, 0:E].unsqueeze(1).broadcast_to([P, 2 * TT, E]),
                                                topi[:, :, :].rearrange("p t k -> p (t k)").unsqueeze(2)
                                                .broadcast_to([P, 2 * TT, E]), ALU.is_equal))
                ve.wait_ge(rt_p.sem, rt_p.past(2))
                c5.step(nc.vector.tensor_copy(cum, bank(0)[:, 0:256]))
                c5.link(nc.vector.tensor_copy(tot, bank(1)[:, 0:256]))
                c5.link(nc.vector.memset(base[:, 0:16], 0.0))
                for t in range(1, TT):
                    c5.link(nc.vector.tensor_tensor(base[:, 16 * t:16 * t + 16], base[:, 16 * t - 16:16 * t],
                                                    tot[:, 16 * t - 16:16 * t], ALU.add))
                c5.link(nc.vector.tensor_tensor(cnt, base[:, 240:256], tot[:, 240:256], ALU.add))
                c5.link(nc.vector.tensor_tensor(til, cnt[:, 0:8], cnt[:, 8:16], ALU.add))
                c5.link(nc.vector.tensor_scalar(til, til, 1.0 / P, 127.0 / 256, ALU.mult, ALU.add))
                c5.link(nc.vector.tensor_scalar(til, til, MAGIC, None, ALU.add))
                c5.link(nc.vector.tensor_scalar(til, til, MAGIC, None, ALU.subtract))
                c5.link(nc.vector.tensor_copy(end[:, 0:1], til[:, 0:1]))
                for e in range(1, E):
                    c5.link(nc.vector.tensor_tensor(end[:, e:e + 1], end[:, e - 1:e], til[:, e:e + 1], ALU.add))
                c5.link(nc.vector.tensor_tensor(off[:, 0:8], end, til, ALU.subtract))
                c5.link(nc.vector.tensor_scalar(off[:, 0:8], off[:, 0:8], float(P), -1.0, ALU.mult, ALU.add))
                c5.link(nc.vector.tensor_tensor(off[:, 8:16], off[:, 0:8], cnt[:, 0:8], ALU.add))
                c5.link(nc.vector.tensor_tensor(cum, cum, base, ALU.add))
                c5.link(nc.vector.tensor_tensor(tmp, cum, oh, ALU.mult))
                c5.link(nc.vector.tensor_reduce(pos, tmp.rearrange("p (q e) -> p q e", e=E), AX.X, ALU.add))
                c5.link(nc.vector.tensor_tensor(cum.rearrange("p (t n) -> p t n", t=TT),
                                                cum.rearrange("p (t n) -> p t n", t=TT),
                                                off.unsqueeze(1).broadcast_to([P, TT, 16]), ALU.add))
                c5.link(nc.vector.tensor_tensor(tmp, cum, oh, ALU.mult))
                c5.link(nc.vector.tensor_reduce(where, tmp.rearrange("p (q e) -> p q e", e=E), AX.X, ALU.add))
                c5.link(nc.vector.tensor_copy(slot[:, :, :].rearrange("p k t -> p t k"),
                                              where.rearrange("p (t k) -> p t k", k=2)))
                tl, rr = rt[:, 3400:3432], rt[:, 3440:3472]
                tile1 = rt[:, 2048:2048 + 2 * TT * MT].rearrange("p (q j) -> p q j", j=MT)
                c5.link(nc.vector.tensor_scalar(tl, where, 1.0 / P, -(P - 1) / (2.0 * P), ALU.mult, ALU.add))
                c5.link(nc.vector.tensor_scalar(tl, tl, MAGIC, None, ALU.add))
                c5.link(nc.vector.tensor_scalar(tl, tl, MAGIC, None, ALU.subtract))
                c5.link(nc.vector.scalar_tensor_tensor(rr, tl, -float(P), where, ALU.mult, ALU.add))
                c5.link(nc.vector.tensor_tensor(tile1, iota[:, 0:MT].unsqueeze(1).broadcast_to([P, 2 * TT, MT]),
                                                tl.unsqueeze(2).broadcast_to([P, 2 * TT, MT]), ALU.is_equal))
                c5.link(nc.vector.tensor_tensor(tile1, tile1, iota[:, P:P + 2 * TT].unsqueeze(2)
                                                .broadcast_to([P, 2 * TT, MT]), ALU.mult))

                def places(k):
                    if k >= 2:
                        ve.wait_ge(inv_p.sem, inv_p.past(k - 1))
                    nc.vector.tensor_tensor(wk[k % 2][:, :, :].rearrange("p c (v n) -> p (c v) n", n=P),
                                            iota[:, 0:P].unsqueeze(1).broadcast_to([P, 8, P]),
                                            rr[:, 8 * k:8 * k + 8].unsqueeze(2).broadcast_to([P, 8, P]), ALU.is_equal
                                            ).then_inc(inv_v.sem, 1)

                places(0)
                places(1)
                ve.wait_ge(rt_a.sem, rt_a.past(1))
                c5.link(nc.vector.tensor_scalar(one[:, 0:16], gate2[:, :, 1], 1.0, None, ALU.add))
                c5.link(nc.vector.reciprocal(gate2[:, :, 0], one[:, 0:16]))
                c5.link(nc.vector.tensor_tensor(gate2[:, :, 1], gate2[:, :, 1], gate2[:, :, 0], ALU.mult))
                c5.link(nc.vector.tensor_scalar(pos, pos, float(CAP), gates[:, 6:7], ALU.is_le, ALU.mult))
                g2 = gate2[:, :, :].rearrange("p t k -> p (t k)")
                c5.link(nc.vector.tensor_tensor(g2, g2, pos, ALU.mult))
                places(2)
                c5.link(nc.vector.tensor_scalar(ef, iota[:, 0:64], end[:, 0:1], None, ALU.is_ge))
                for e in range(1, E - 1):
                    c5.link(nc.vector.scalar_tensor_tensor(ef, iota[:, 0:64], end[:, e:e + 1], ef, ALU.is_ge, ALU.add))
                places(3)
                c5.link(nc.vector.tensor_copy(eid[:, :], ef))
                ve.wait_ge(inv_p.sem, inv_p.past(4))
                nc.vector.tensor_copy(rown[:, :], bank(2)[:, 0:MT]).then_inc(inv_s.sem, 1)
                ve.sem_inc(routed.sem, 1)
            if phases >= 6:
                def rows_in(j, u):
                    ve.wait_ge(m_xp.sem, m_xp.past(j + 1))
                    nc.vector.tensor_copy(xTb[u], bank(5)[:, 0:D].rearrange("p (c s) -> p c s", c=CH)).then_inc(m_xs.sem, 1)

                def hidden(j):
                    ve.wait_ge(m_tp.sem, m_tp.past(j + 1))
                    ve.wait_ge(m_y.sem, m_y.past(j))
                    nc.vector.tensor_copy(hidT.rearrange("p (v n) -> p v n", v=2), ps[1][:, :, :]).then_inc(m_ts.sem, 1)

                rows_in(0, 0)
                with ve.Fori(0, (MT - 3) // 3) as r:
                    for u in range(3):
                        j = r * 3 + u + 1
                        rows_in(j, (u + 1) % 3)
                        hidden(j - 1)
                for j in range(MT - 2, MT):
                    rows_in(j, j % 3)
                    hidden(j - 1)
                hidden(MT - 1)

                def combine(q):
                    ve.wait_ge(s_ga[q], 8 * 16)
                    for t in range(4 * q, 4 * q + 4):
                        nc.vector.scalar_tensor_tensor(x[:, t, :], got[:, 0, t, :], gate2[:, t, 0:1], x[:, t, :], ALU.mult,
                                                       ALU.add).then_inc(cmb.sem, 1)
                    for t in range(4 * q, 4 * q + 4):
                        ve.wait_ge(cmb.sem, cmb.past(t + 1))
                        nc.vector.scalar_tensor_tensor(x[:, t, :], got[:, 1, t, :], gate2[:, t, 1:2], x[:, t, :], ALU.mult,
                                                       ALU.add).then_inc(done[6].sem, 1)

                if phases == 6:
                    for q in range(PAIRS):
                        combine(q)
            if phases >= 7:
                ve.wait_ge(s_w[7], 5 * 16)
                for dst, k in ((gamg, 0), (betg, 1)):
                    nc.vector.tensor_scalar(dst, bc3[:, k, :], gates[:, 3:4], None, ALU.mult).then_inc(g7_s.sem, 1)

                def spread(b, p, src, stats, means, summed, taken, own, out):
                    ve.wait_ge(summed.sem, summed.past(b + 1))
                    for t in range(TB):
                        ins = nc.vector.bn_stats(stats[p][:, t, :], src[p][:, t, :])
                    ins.then_inc(own.sem, 1)
                    ve.wait_ge(own.sem, own.past(b + 1))
                    ve.wait_ge(taken.sem, taken.past(b - p))
                    apart(ve)
                    for t in range(TB):
                        ins = nc.vector.bn_aggr(means[p][:, t, :], stats[p][:, t, :])
                    ins.then_inc(out.sem, 1)

                def step7(q):
                    attn, ff, norms = has(q)
                    if attn:
                        for p in range(2):
                            single_soft(7, q, p)
                    if norms:
                        ve.wait_ge(done[6].sem, done[6].past(4 * q + 8))
                        ln_stats(7, q + 1)
                    if attn:
                        for p in range(2):
                            single_sum(7, q, p)
                        for p in range(2):
                            b = 2 * q + p
                            ve.wait_ge(pv_p[7].sem, pv_p[7].past(b + 1))
                            ve.wait_ge(x7_s.sem, x7_s.past(b - p))
                            for t in range(TB):
                                ins = nc.vector.scalar_tensor_tensor(xa[p][:, t, :], bank(p)[:, t * D:(t + 1) * D],
                                                                     rden[p][:, TB + t:TB + t + 1], xl[p][:, t, :],
                                                                     ALU.mult, ALU.add)
                            ins.then_inc(xa_s.sem, 1)
                            spread(b, p, xa, st_a, mv_a, xa_s, ra_s, sa_s, va_s)
                    if norms:
                        for p in range(2):
                            b = 2 * (q + 1) + p
                            ve.wait_ge(rstd[7].sem, rstd[7].past(b + 1))
                            ve.wait_ge(xtp[7].sem, xtp[7].past(b - p))
                            ve.wait_ge(xa_s.sem, xa_s.past(b - p))
                            for t in range(TB):
                                ins = nc.vector.tensor_scalar(xl[p][:, t, :], x[:, 2 * b + t, :], mv[p][:, t, 0:1],
                                                              rs[p][:, t:t + 1], ALU.subtract, ALU.mult)
                            ins.then_inc(nrm[7].sem, 1)
                    if ff:
                        for p in range(2):
                            b = 2 * q - 2 + p
                            ve.wait_ge(f7_p.sem, f7_p.past(b + 1))
                            ve.wait_ge(x7_s.sem, x7_s.past(b + 1))
                            ve.wait_ge(done[7].sem, done[7].past(4 * (q - 1)))
                            nc.vector.tensor_tensor(ya[p], xb[p], bank(2 + p).rearrange("p (t d) -> p t d", t=TB),
                                                    ALU.add).then_inc(yb_s.sem, 1)
                            spread(b, p, ya, st_b, mv_b, yb_s, rb_s, sb_s, vb_s)
                    if attn:
                        for p in range(2):
                            b = 2 * q + p
                            ve.wait_ge(ra_s.sem, ra_s.past(b + 1))
                            for t in range(TB):
                                ins = nc.vector.scalar_tensor_tensor(xa[p][:, t, :], xa[p][:, t, :], mv_a[p][:, t, 0:1],
                                                                     bc3[:, 0, :], ALU.subtract, ALU.mult)
                            ins.then_inc(na_s.sem, 1)
                        for p in range(2):
                            b = 2 * q + p
                            ve.wait_ge(na_s.sem, na_s.past(b + 1))
                            ve.wait_ge(x7_p.sem, x7_p.past(b - p))
                            ve.wait_ge(yb_s.sem, yb_s.past(b - p))
                            for t in range(TB):
                                ins = nc.vector.scalar_tensor_tensor(xb[p][:, t, :], xa[p][:, t, :], rs_a[p][:, t, 0:1],
                                                                     bc3[:, 1, :], ALU.mult, ALU.add)
                            ins.then_inc(x7_s.sem, 1)
                    if ff:
                        for p in range(2):
                            b = 2 * q - 2 + p
                            ve.wait_ge(rb_s.sem, rb_s.past(b + 1))
                            for t in range(TB):
                                ins = nc.vector.scalar_tensor_tensor(ya[p][:, t, :], ya[p][:, t, :], mv_b[p][:, t, 0:1],
                                                                     gamg, ALU.subtract, ALU.mult)
                            ins.then_inc(nb_s.sem, 1)
                        ve.wait_ge(xb_s[7].sem, xb_s[7].past(q))
                        for p in range(2):
                            b = 2 * q - 2 + p
                            ve.wait_ge(nb_s.sem, nb_s.past(b + 1))
                            for t in range(TB):
                                row = x[:, 2 * b + t, :]
                                nc.vector.scalar_tensor_tensor(row, ya[p][:, t, :], rs_b[p][:, t, 0:1], row,
                                                               ALU.mult, ALU.add).then_inc(done[7].sem, 1)

                combine(0)
                step7(-1)
                combine(1)
                step7(0)
                combine(2)
                combine(3)
                last_steps(ve, step7, 1)
            if phases >= 8:
                c8 = Chain(ve, prep_8)
                ve.wait_ge(done[7].sem, done[7].past(TT))
                c8.link(nc.vector.tensor_scalar(w3f, w3f, 0.0, 2.0, ALU.is_ge, ALU.mult))
                c8.link(nc.vector.tensor_scalar(w3f, w3f, -1.0, None, ALU.add))

                def step8(q, own, ahead):
                    if ahead:
                        ln(8, q + 1, xtp[8])
                    if own:
                        def each(k, op):
                            for p in range(2):
                                if k:
                                    ve.wait_ge(dvx[8].sem, dvx[8].past(6 * q + 2 * (k - 1) + p + 1))
                                op(p, xkeep[:, 12 + 2 * p:14 + 2 * p, :]).then_inc(dvx[8].sem, 1)

                        def scaled(p, y):
                            ve.wait_ge(f_p[8].sem, f_p[8].past(4 * q + 2 * p + 2))
                            return nc.vector.tensor_tensor(y, ps[2 + p][:, :, 0:D],
                                                           bc3[:, 2:3, :].broadcast_to([P, TB, D]), ALU.mult)

                        each(0, scaled)
                        each(1, lambda p, y: nc.vector.tensor_tensor(y, y, bc3[:, 3:4, :].broadcast_to([P, TB, D]),
                                                                     ALU.add))
                        each(2, lambda p, y: nc.vector.tensor_scalar(y, y, -100.0, 100.0, ALU.max, ALU.min))
                        for p in range(2):
                            ve.wait_ge(dvx[8].sem, dvx[8].past(6 * q + 4 + p + 1))
                            two = x[:, bass.ds(4 * q + 2 * p, 2), :]
                            nc.vector.scalar_tensor_tensor(two, xkeep[:, 12 + 2 * p:14 + 2 * p, :], gates[:, 7:8], two,
                                                           ALU.mult, ALU.add).then_inc(done[8].sem, 2)

                ahead_steps(ve, step8)

        @block.tensor
        def _(pe):
            pe.wait_ge(s_seeded, 1)

            def turn(n, bb):
                for p in range(2):
                    pe.wait_ge(nrm[n].sem, nrm[n].past(2 * bb + p + 1))
                    pe.wait_ge(xts[n].sem, xts[n].past(2 * bb))
                    for c in range(CH):
                        for t in range(TB):
                            ins = nc.tensor.transpose(bank(p)[:, c * S + t * P:c * S + (t + 1) * P],
                                                      xn[p][:, t, c * P:(c + 1) * P], ident[:, :])
                    ins.then_inc(xtp[n].sem, 1)

            pe.wait_ge(s_ctx, 2 * 16)
            for c in range(CH):
                for h in range(2):
                    for b in range(4):
                        ins = nc.tensor.transpose(bank(2 * c + h)[:, b * KEYS:(b + 1) * KEYS],
                                                  ctxn[:, 4 * h + b, c * P:(c + 1) * P], ident[0:KEYS, 0:KEYS])
                    ins.then_inc(s_ctp.sem, 1)
            pe.wait_ge(s_cst, 7 * 16)
            pe.wait_ge(s_cta.sem, s_cta.past(4))
            pe.wait_ge(s_set.sem, s_set.past(3))
            for j in range(2 * GR):
                nc.tensor.matmul(bank(j)[:, 0:HALF], fmw[:, j // 2 % 2, :],
                                 ctxT[:, j // 4, (j % 2) * HALF:(j % 2 + 1) * HALF],
                                 start=True, stop=True).then_inc(prep_p[0].sem, 1)
            pe.wait_ge(prep_a[0].sem, prep_a[0].past(8))
            for b in range(B):
                for g in range(GR):
                    ins = nc.tensor.transpose(bank(b)[0:KEYS, g * P:(g + 1) * P], kall[:, g, b * KEYS:(b + 1) * KEYS],
                                              ident[:, :])
                ins.then_inc(prep_p[0].sem, 1)
            pe.wait_ge(prep_v[0].sem, prep_v[0].past(8))
            pe.wait_ge(s_setp.sem, s_setp.past(2))

            def turn_ahead(n, bb):
                for p in range(2):
                    pe.wait_ge(nrm[n].sem, nrm[n].past(2 * bb + p + 1))
                    for c in range(CH):
                        for t in range(TB):
                            ins = nc.tensor.transpose(bank(p)[:, c * S + t * P:c * S + (t + 1) * P],
                                                      xn[p][:, t, c * P:(c + 1) * P], ident[:, :])
                    ins.then_inc(xtp[n].sem, 1)

            def queries(n, bb):
                for p in range(2):
                    pe.wait_ge(xts[n].sem, xts[n].past(2 * bb + (2 if n == 0 else p + 1)))
                    if n == 0:
                        for g in range(GR):
                            ins = nc.tensor.matmul(ps[1 - p][:, g // 2, (g % 2) * S:(g % 2 + 1) * S], fmw[:, g % 2, :],
                                                   xnT[p][:, g // 2, :], start=True, stop=True)
                    else:
                        for m in range(CH):
                            for c in range(CH):
                                ins = nc.tensor.matmul(bank(2 + p)[:, m * S:(m + 1) * S], w2q[:, c, m * P:(m + 1) * P],
                                                       xnT[p][:, c, :], start=c == 0, stop=c == CH - 1)
                    ins.then_inc(q_p[n].sem, 1)

            def heads(n):
                top = n == 4
                vd = 16 if top else 32
                lag = 1 if top else 0
                wo = w2o if top else fcw
                nch = CH if top else GR
                vv = vall[:, 0:B * HEADS * (vd + 1)].rearrange("p (b h e) -> p b h e", b=B, h=HEADS)

                def step(bb, s, ahead):
                    if ahead and s == ITEMS:
                        pe.wait_ge(sc_r[n].sem, sc_r[n].past(ITEMS * bb + ITEMS))
                        queries(n, bb + 1)
                    if live(s, ahead):
                        j, u, pair = s % ITEMS, s % 2, bb + s // ITEMS
                        if j == 0:
                            pe.wait_ge(q_s[n].sem, q_s[n].past((4 if top else 2) * (pair + 1)))
                        if j < 2:
                            pe.wait_ge(kb_s[n].sem, kb_s[n].past(2 * pair + j + 1))
                        pe.wait_ge(sc_r[n].sem, sc_r[n].past(least(ITEMS * bb + s - 1)))
                        for t in range(TB):
                            ins = nc.tensor.matmul(ps[u][:, t, 0:GK],
                                                   wk[u][:, j // 4 if top else j // 2, t * P:(t + 1) * P],
                                                   kb[u][:, j // 2, :], start=True, stop=not top)
                            if top:
                                ins = nc.tensor.matmul(ps[u][:, t, 0:GK], row0[:, :],
                                                       mrow[:, bass.ds((2 * pair + u) * KEYS, KEYS)].unsqueeze(1)
                                                       .broadcast_to([P, HG, KEYS]), start=False, stop=True)
                        ins.then_inc(sc_p[n].sem, 1)
                    if ahead and s == ITEMS - 1:
                        pe.wait_ge(sc_r[n].sem, sc_r[n].past(ITEMS * bb + ITEMS - 1))
                        turn_ahead(n, bb + 1)
                    i = s - 1 - lag
                    if live(i, ahead):
                        pe.wait_ge(ex_s[n].sem, ex_s[n].past(ITEMS * bb + i + 1))
                        pe.wait_ge(pt_s[n].sem, pt_s[n].past(ITEMS * bb + i))
                        for h in range(HG):
                            for t in range(TB):
                                at = (h % 2) * S + t * P
                                ins = nc.tensor.transpose(ps[2][0:KEYS, h // 2, at:at + P],
                                                          pr[i % 2][:, t, h * KEYS:(h + 1) * KEYS], ident[:, :])
                        ins.then_inc(pt_p[n].sem, 1)
                    i = s - 2 - lag
                    if live(i, ahead):
                        pair = bb + i // ITEMS
                        pe.wait_ge(pt_s[n].sem, pt_s[n].past(ITEMS * bb + i + 1))
                        pe.wait_ge(o_s[n].sem, o_s[n].past(ITEMS * bb + i))
                        if i % ITEMS == 1:
                            pe.wait_ge(done[n].sem, done[n].past(4 * pair))
                        for t in range(TB):
                            for h in range(HG):
                                j = t * HG + h
                                ins = nc.tensor.matmul(bank(6)[:, j * (vd + 1):(j + 1) * (vd + 1)],
                                                       pt[i % 2][:, h * S + t * P:h * S + (t + 1) * P],
                                                       vv[:, 2 * pair + i % 2, i % ITEMS // 2 * HG + h, :],
                                                       start=True, stop=True)
                        ins.then_inc(pv_p[n].sem, 1)
                    i = s - 3 - lag
                    if live(i, ahead) and (not top or i // 2 % 2):
                        j, pair = i % ITEMS, bb + i // ITEMS
                        k = ITEMS * bb + i if not top else ITEMS // 2 * pair + j // 4 * 2 + i % 2
                        pe.wait_ge(o_s[n].sem, o_s[n].past(ITEMS * bb + i + 1))
                        pe.wait_ge(ot_s[n].sem, ot_s[n].past(k))
                        if j < 4:
                            pe.wait_ge(done[n].sem, done[n].past(4 * pair))
                        for t in range(TB):
                            ins = nc.tensor.transpose(bank(7)[:, t * P:(t + 1) * P], osb[i % 2][:, t, :], ident[:, :])
                        ins.then_inc(ot_p[n].sem, 1)
                    if s == ITEMS + 2 + lag:
                        pe.wait_ge(ot_s[n].sem, ot_s[n].past(2 * nch * (bb + 1)))
                        for p in range(2):
                            if p == 1:
                                pe.wait_ge(o_s[n].sem, o_s[n].past(ITEMS * (bb + 1) + (1 if ahead else 0)))
                            for t in range(TB):
                                for g in range(nch):
                                    ins = nc.tensor.matmul(bank(7 - p)[:, t * D:(t + 1) * D],
                                                           oT[p][:, g, t * P:(t + 1) * P], wo[:, g, :],
                                                           start=g == 0, stop=g == nch - 1)
                                ins.then_inc(f_p[n].sem, 1)

                head_steps(pe, n, step)

            pe.wait_ge(s_w[0], 3 * 16)
            turn_ahead(0, 0)
            queries(0, 0)
            heads(0)

            def plain(n, w):
                def step(q, own, ahead):
                    if own:
                        pe.wait_ge(done[n].sem, done[n].past(4 * q))
                        for p in range(2):
                            pe.wait_ge(xts[n].sem, xts[n].past(2 * q + p + 1))
                            for t in range(TB):
                                for c in range(CH):
                                    ins = nc.tensor.matmul(bank(4 + 2 * p + t)[:, 0:D], xnT[p][:, c, t * P:(t + 1) * P],
                                                           w[:, c, :], start=c == 0, stop=c == CH - 1)
                                ins.then_inc(f_p[n].sem, 1)
                    if ahead:
                        turn(n, q + 1)
                return step

            if phases >= 1:
                pe.wait_ge(done[0].sem, done[0].past(TT))
                pe.wait_ge(prep_v[1].sem, prep_v[1].past(2))
                ahead_steps(pe, plain(1, sgw))

            def keys(n, wkey):
                for j in range(4):
                    m, h = j // 2, j % 2
                    for c in range(CH):
                        ins = nc.tensor.matmul(bank(j)[:, 0:HALF], wkey[:, c, m * P:(m + 1) * P],
                                               ctxT[:, c, h * HALF:(h + 1) * HALF], start=c == 0, stop=c == CH - 1)
                    ins.then_inc(prep_p[n].sem, 1)

            def values(n, wval):
                for b in range(B):
                    dst = bank(4 + b // 2)[0:KEYS, (b % 2) * D:(b % 2 + 1) * D]
                    for c in range(CH):
                        ins = nc.tensor.matmul(dst, ctxT[:, c, b * KEYS:(b + 1) * KEYS], wval[:, c, :], start=c == 0,
                                               stop=c == CH - 1)
                    if b % 2:
                        ins.then_inc(prep_p[n].sem, 1)

            if phases >= 2:
                pe.wait_ge(done[1].sem, done[1].past(TT))
                pe.wait_ge(s_w[2], 3 * 16)
                keys(2, w1k)
                if phases >= 3:
                    pe.wait_ge(prep_v[3].sem, prep_v[3].past(2))
                    for k in range(2):
                        nc.tensor.matmul(bank(6 + k)[:, 0:1], ones[:, :], wstat[:, k:k + 1], start=True,
                                         stop=True).then_inc(prep_p[3].sem, 1)
                    pe.wait_ge(prep_v[3].sem, prep_v[3].past(4))
                values(2, w1v)
                pe.wait_ge(prep_a[2].sem, prep_a[2].past(4))
                pe.wait_ge(prep_v[2].sem, prep_v[2].past(4))

                def step2(q, own, ahead):
                    if own:
                        for p in range(2):
                            pe.wait_ge(q_s[2].sem, q_s[2].past(4 * q + 2 * p + 2))
                            pe.wait_ge(done[2].sem, done[2].past(4 * q))
                            for t in range(TB):
                                for m in range(CH):
                                    ins = nc.tensor.matmul(bank(4 + p)[:, t * KEYS:(t + 1) * KEYS],
                                                           wk[p][:, m, t * P:(t + 1) * P],
                                                           kall[:, m, bass.ds((2 * q + p) * KEYS, KEYS)],
                                                           start=m == 0, stop=m == CH - 1)
                            ins.then_inc(sc_p[2].sem, 1)
                        for p in range(2):
                            pe.wait_ge(ex_s[2].sem, ex_s[2].past(2 * q + p + 1))
                            pe.wait_ge(pt_s[2].sem, pt_s[2].past(2 * q))
                            for t in range(TB):
                                ins = nc.tensor.transpose(bank(6 + p)[0:KEYS, t * P:(t + 1) * P],
                                                          pr[p][:, t, 0:KEYS], ident[:, :])
                            ins.then_inc(pt_p[2].sem, 1)
                        for p in range(2):
                            pe.wait_ge(pt_s[2].sem, pt_s[2].past(2 * q + p + 1))
                            for t in range(TB):
                                ins = nc.tensor.matmul(bank(4 + p)[:, t * D:(t + 1) * D], pt[p][:, t * P:(t + 1) * P],
                                                       vall[:, bass.ds((2 * q + p) * D, D)], start=True, stop=True)
                            ins.then_inc(pv_p[2].sem, 1)
                    if ahead:
                        turn(2, q + 1)
                        for p in range(2):
                            pe.wait_ge(xts[2].sem, xts[2].past(2 * q + 2 + p + 1))
                            pe.wait_ge(q_s[2].sem, q_s[2].past(4 * q + 4))
                            for m in range(CH):
                                for c in range(CH):
                                    ins = nc.tensor.matmul(bank(2 + p)[:, m * S:(m + 1) * S], w1q[:, c, m * P:(m + 1) * P],
                                                           xnT[p][:, c, :], start=c == 0, stop=c == CH - 1)
                            ins.then_inc(q_p[2].sem, 1)

                ahead_steps(pe, step2)
            if phases >= 3:
                pe.wait_ge(done[2].sem, done[2].past(TT))
                pe.wait_ge(prep_v[3].sem, prep_v[3].past(16))

                def bit_step(r, k):
                    t = 4 * r + k
                    if k >= 3:
                        u = (k - 3) % 4
                        pe.wait_ge(ht_s.sem, ht_s.past(t - 2))
                        pe.wait_ge(done[3].sem, done[3].past(least(t - 4)))
                        hT = pr[u % 2].rearrange("p t n -> p (t n)")[:, 0:512].bitcast(bf16)
                        for j in range(FF // P):
                            ins = nc.tensor.matmul(bank(6 + u % 2)[:, 0:D], hT[:, j * P:(j + 1) * P],
                                                   tern2[:, j, :], start=j == 0, stop=j == FF // P - 1)
                        ins.then_inc(f_p[3].sem, 1)
                    if 2 <= k < TT + 2:
                        pe.wait_ge(h_z.sem, h_z.past(t - 1))
                        pe.wait_ge(ht_s.sem, ht_s.past(t - 2))
                        tb = bank(5).bitcast(bf16)
                        for j in range(FF // P):
                            ins = nc.tensor.transpose(tb[:, j * P:(j + 1) * P], hq[k % 2][:, j * P:(j + 1) * P],
                                                      identb[:, :])
                        ins.then_inc(ht_p.sem, 1)
                    if -1 <= k < TT - 1:
                        u = (k + 1) % 4
                        pe.wait_ge(xts[3].sem, xts[3].past(2 * r + (k + 1) // 2 + 1))
                        pe.wait_ge(h_b.sem, h_b.past(least(t)))
                        xT = xnT[u // 2][:, 0, :].bitcast(bf16).rearrange("p (c s) -> p c s", c=CH)
                        for v in range(2):
                            for c in range(CH):
                                ins = nc.tensor.matmul(ps[u % 2][:, v, :], xT[:, c, (u % 2) * P:(u % 2 + 1) * P],
                                                       tern1[:, c, v * 512:(v + 1) * 512], start=c == 0,
                                                       stop=c == CH - 1)
                        ins.then_inc(h_p.sem, 1)
                    if k % 2 == 0 and -2 <= k and (k + 2) // 2 < B:
                        b, p = 2 * r + (k + 2) // 2, (k + 2) // 2 % 2
                        pe.wait_ge(q_s[3].sem, q_s[3].past(b + 1))
                        pe.wait_ge(xts[3].sem, xts[3].past(b))
                        tb = bank(4).bitcast(bf16)
                        for c in range(CH):
                            for q in range(TB):
                                ins = nc.tensor.transpose(tb[:, c * S + q * P:c * S + (q + 1) * P],
                                                          xq[p][:, q, c * P:(c + 1) * P], identb[:, :])
                        ins.then_inc(xtp[3].sem, 1)

                bit_steps(pe, bit_step)
            if phases >= 4:
                pe.wait_ge(done[3].sem, done[3].past(TT))
                pe.wait_ge(s_w[4], 5 * 16)
                keys(4, w2k)
                values(4, w2v)
                pe.wait_ge(prep_a[4].sem, prep_a[4].past(4))
                turn_ahead(4, 0)
                queries(4, 0)
                pe.wait_ge(prep_v[4].sem, prep_v[4].past(10))
                heads(4)

            if phases >= 5:
                pe.wait_ge(done[4].sem, done[4].past(TT))
                pe.wait_ge(s_w[5], 16)

                def step5(q, own, ahead):
                    if own:
                        for p in range(2):
                            pe.wait_ge(xts[5].sem, xts[5].past(2 * q + p + 1))
                            pe.wait_ge(rt_l.sem, rt_l.past(2 * q))
                            for t in range(TB):
                                for c in range(CH):
                                    ins = nc.tensor.matmul(bank(2 + p)[:, t * E:(t + 1) * E],
                                                           xnT[p][:, c, t * P:(t + 1) * P], rwT[:, c, :], start=c == 0,
                                                           stop=c == CH - 1)
                            ins.then_inc(lg_p.sem, 1)
                    if ahead:
                        turn(5, q + 1)

                ahead_steps(pe, step5)
                pe.wait_ge(rt_v.sem, rt_v.past(2))
                nc.tensor.matmul(bank(0)[:, 0:256], lower[:, :], rt[:, 0:256], start=True, stop=True).then_inc(rt_p.sem, 1)
                nc.tensor.matmul(bank(1)[:, 0:256], ones[:, :], rt[:, 0:256], start=True, stop=True).then_inc(rt_p.sem, 1)
                tile1 = rt[:, 2048:2048 + 2 * TT * MT].rearrange("p (q j) -> p q j", j=MT)
                for k in range(4):
                    pe.wait_ge(inv_v.sem, inv_v.past(k + 1))
                    for v in range(8):
                        ins = nc.tensor.matmul(bank(2)[:, 0:MT],
                                               wk[k % 2][:, v // 2, v % 2 * P:(v % 2 + 1) * P], tile1[:, 8 * k + v, :],
                                               start=k == 0 and v == 0, stop=k == 3 and v == 7)
                    ins.then_inc(inv_p.sem, 1)
            if phases >= 6:
                pe.wait_ge(routed.sem, routed.past(1))
                pe.wait_ge(s_we, 2 * E * 16)

                def rows_t(j, u, k):
                    pe.wait_ge(s_ld[u], 16 * k + 16)
                    pe.wait_ge(m_xs.sem, m_xs.past(j))
                    for c in range(CH):
                        ins = nc.tensor.transpose(bank(5)[:, c * P:(c + 1) * P], xsb[u][:, c * P:(c + 1) * P],
                                                  ident[:, :])
                    ins.then_inc(m_xp.sem, 1)

                def first(j, u):
                    pe.wait_ge(m_xs.sem, m_xs.past(j + 1))
                    pe.wait_ge(m_g.sem, m_g.past(j))
                    apart(pe)
                    e = pe.value_load(eid[0:1, bass.ds(j, 1)], min_val=0, max_val=E - 1)
                    for v in range(2):
                        for c in range(CH):
                            ins = nc.tensor.matmul(ps[0][:, v, :], xTb[u][:, c, :],
                                                   experts[:, bass.ds(e * EW + (c * FF + v * 512), 512)],
                                                   start=c == 0, stop=c == CH - 1)
                    ins.then_inc(m_h.sem, 1)

                def hidden_t(j):
                    pe.wait_ge(m_g.sem, m_g.past(j + 1))
                    pe.wait_ge(m_ts.sem, m_ts.past(j))
                    hv = hid[:, :, :].rearrange("p c s -> p (c s)")
                    for k in range(FF // P):
                        ins = nc.tensor.transpose(ps[1][:, k // 4, (k % 4) * P:(k % 4 + 1) * P],
                                                  hv[:, k * P:(k + 1) * P], ident[:, :])
                    ins.then_inc(m_tp.sem, 1)

                def second(j):
                    pe.wait_ge(m_ts.sem, m_ts.past(j + 1))
                    pe.wait_ge(m_ys.sem, m_ys.past(j))
                    apart(pe)
                    e = pe.value_load(eid[0:1, bass.ds(j, 1)], min_val=0, max_val=E - 1)
                    for k in range(FF // P):
                        ins = nc.tensor.matmul(bank(4)[:, 0:D], hidT[:, k * P:(k + 1) * P],
                                               experts[:, bass.ds(e * EW + (E * EW + k * D), D)], start=k == 0,
                                               stop=k == FF // P - 1)
                    ins.then_inc(m_y.sem, 1)

                rows_t(0, 0, 0)
                rows_t(1, 1, 0)
                first(0, 0)
                with pe.Fori(0, (MT - 3) // 3) as r:
                    for u in range(3):
                        j = r * 3 + u + 1
                        rows_t(j + 1, (u + 2) % 3, r if u == 0 else r + 1)
                        hidden_t(j - 1)
                        first(j, (u + 1) % 3)
                        second(j - 1)
                for j in range(MT - 2, MT):
                    if j + 1 < MT:
                        rows_t(j + 1, (j + 1) % 3, (j + 1) // 3)
                    hidden_t(j - 1)
                    first(j, j % 3)
                    second(j - 1)
                hidden_t(MT - 1)
                second(MT - 1)
            if phases >= 7:
                pe.wait_ge(s_w[7], 5 * 16)

                def flip(dst, src):
                    for c in range(CH):
                        for t in range(TB):
                            ins = nc.tensor.transpose(dst[:, c * S + t * P:c * S + (t + 1) * P],
                                                      src[:, t, c * P:(c + 1) * P], ident[:, :])
                    return ins

                def step7(q):
                    attn, ff, norms = has(q)
                    if attn:
                        for p in range(2):
                            b = 2 * q + p
                            pe.wait_ge(xts[7].sem, xts[7].past(b + 1))
                            pe.wait_ge(pt_s[7].sem, pt_s[7].past(b - p))
                            for t in range(TB):
                                for m in range(CH):
                                    ins = nc.tensor.matmul(bank(6 + p)[:, S + t * KEYS:S + (t + 1) * KEYS],
                                                           xnT[p][:, m, t * P:(t + 1) * P],
                                                           ctxT[:, m, bass.ds(b * KEYS, KEYS)], start=m == 0,
                                                           stop=m == CH - 1)
                            ins.then_inc(sc_p[7].sem, 1)
                    if ff:
                        for p in range(2):
                            b = 2 * q - 2 + p
                            pe.wait_ge(x7_s.sem, x7_s.past(b + 1))
                            pe.wait_ge(yb_s.sem, yb_s.past(b - p))
                            flip(bank(2 + p), xb[p]).then_inc(x7_p.sem, 1)
                    if attn:
                        for p in range(2):
                            pe.wait_ge(ex_s[7].sem, ex_s[7].past(2 * q + p + 1))
                            for t in range(TB):
                                ins = nc.tensor.transpose(bank(6 + p)[0:KEYS, t * P:(t + 1) * P],
                                                          pr[p][:, t, 0:KEYS], ident[:, :])
                            ins.then_inc(pt_p[7].sem, 1)
                    if ff:
                        for p in range(2):
                            b = 2 * q - 2 + p
                            pe.wait_ge(x7_t.sem, x7_t.past(b + 1))
                            pe.wait_ge(h7_s.sem, h7_s.past(b - p))
                            for m in range(CH):
                                for c in range(CH):
                                    ins = nc.tensor.matmul(bank(4 + p)[:, m * S:(m + 1) * S],
                                                           w3a[:, c, m * P:(m + 1) * P], xbT[p][:, c, :],
                                                           start=c == 0, stop=c == CH - 1)
                            ins.then_inc(h7_p.sem, 1)
                    if attn:
                        for p in range(2):
                            b = 2 * q + p
                            pe.wait_ge(pt_s[7].sem, pt_s[7].past(b + 1))
                            for t in range(TB):
                                ins = nc.tensor.matmul(bank(p)[:, t * D:(t + 1) * D], pt[p][:, t * P:(t + 1) * P],
                                                       ctxn[:, b, :], start=True, stop=True)
                            ins.then_inc(pv_p[7].sem, 1)
                    if ff:
                        for p in range(2):
                            b = 2 * q - 2 + p
                            pe.wait_ge(h7_s.sem, h7_s.past(b + 1))
                            for t in range(TB):
                                dst = bank(2 + p)[:, t * D:(t + 1) * D]
                                for c in range(CH):
                                    nc.tensor.matmul(dst, wk[p][:, c, t * P:(t + 1) * P], w3b[:, c, :], start=c == 0,
                                                     stop=False)
                                ins = nc.tensor.matmul(dst, row0[:, :], b2row, start=False, stop=True)
                            ins.then_inc(f7_p.sem, 1)
                    if norms:
                        for p in range(2):
                            b = 2 * q + 2 + p
                            pe.wait_ge(nrm[7].sem, nrm[7].past(b + 1))
                            pe.wait_ge(xa_s.sem, xa_s.past(b - p))
                            flip(bank(p), xl[p]).then_inc(xtp[7].sem, 1)

                last_steps(pe, step7)
            if phases >= 8:
                pe.wait_ge(done[7].sem, done[7].past(TT))
                pe.wait_ge(prep_8.sem, prep_8.past(2))
                ahead_steps(pe, plain(8, w3f))


def kernel(**inputs):
    import numpy as np
    import concourse.bacc as bacc
    from concourse import mybir
    from concourse.bass_utils import run_bass_kernel_spmd

    i = {k: np.asarray(v) for k, v in inputs.items()}
    p = np.arange(128)
    fm = i["L0_xattn_fm_w"].T
    fmw = np.zeros((128, 2, 4, 2, 16), fm.dtype)
    for g in range(2):
        for h in range(4):
            for s in range(2):
                fmw[g * 64 + h * 16:g * 64 + h * 16 + 16, g, h, s, :] = fm
    cols = np.zeros((128, 16), np.float32)
    cols[:, 0] = np.tile(i["L0_xattn_fm_b"], 8)
    cols[:, 15] = np.where(p // 16 % 2 == 0, 1.0, -1.0)
    for n, key in ((1, "L1_xattn_bq"), (3, "L1_xattn_bk"), (5, "L2_xattn_wq_b"), (7, "L2_xattn_wk_b"), (9, "L3_xattn_b1")):
        cols[:, n:n + 2] = i[key].reshape(2, 128).T
    hsel = np.zeros((128, 12), np.float32)
    hsel[p, p // 32] = 1.0
    hsel[p, 4 + p // 16] = 1.0
    iota = np.concatenate([np.tile(np.arange(128, dtype=np.float32), (128, 1)),
                           (np.arange(32) // 2 * 128 + np.arange(128)[:, None]).astype(np.float32)], 1)
    given = {
        "x": i["x"],
        "ctx": i["ctx_1024"][:, ::-1],
        "mask": i["mask_BxS2_bf1"][:, ::-1].reshape(-1).view(np.uint8),
        "g": np.concatenate([i["g_xattn"], i["g_ffn"]]),
        "ident": np.eye(128, dtype=np.float32),
        "lower": np.triu(np.ones((128, 128), np.float32)),
        "iota": iota, "hsel": hsel, "cols": cols,
        "rows": np.stack([i["L1_xattn_bv"], i["L2_xattn_wv_b"]]),
        "b2": np.stack([i["L3_xattn_b2"]]),
        "outb": np.stack([i["L0_xattn_fc_b"], i["L2_xattn_wo_b"]]),
        "row0": (p == 0)[:, None] * np.ones((128, 128), np.float32),
        "fmw": fmw.reshape(128, 2, 128),
        "fcw": i["L0_xattn_fc_w"].T, "sgw": i["L0_ffn_weight"].T,
        "w1q": i["L1_xattn_Wq"], "w1k": i["L1_xattn_Wk"], "w1v": i["L1_xattn_Wv"],
        "bw1": i["L1_ffn_W1"].T, "bw2": i["L1_ffn_W2"].T, "bb1": i["L1_ffn_b1"], "bb2": i["L1_ffn_b2"],
        "w2q": i["L2_xattn_wq_w"].T, "w2k": i["L2_xattn_wk_w"].T, "w2v": i["L2_xattn_wv_w"].T,
        "w2o": i["L2_xattn_wo_w"].T, "rw": i["L2_ffn_router_w"].T,
        "ew1": i["L2_ffn_w1"], "ew2": i["L2_ffn_w2"],
        "w3a": i["L3_xattn_W1"], "w3b": i["L3_xattn_W2"],
        "bc3": np.stack([i["L3_xattn_gamma"], i["L3_xattn_beta"], i["L3_ffn_scale"], i["L3_ffn_bias"]]),
        "w3f": i["L3_ffn_weights"].T,
    }
    nc = bacc.Bacc("TRN2", target_bir_lowering=False, num_devices=1)
    arrays, aps = {}, {}
    for key, v in given.items():
        v = np.ascontiguousarray(v)
        arrays["in_" + key] = v
        aps[key] = nc.dram_tensor("in_" + key, v.shape, mybir.dt.from_np(v.dtype), kind="ExternalInput").ap()
    res = nc.dram_tensor("out_0", (B, S, D), mybir.dt.float32, kind="ExternalOutput").ap()
    build(nc, aps, res, PHASES)
    r = run_bass_kernel_spmd(nc, [arrays], core_ids=[0])
    return r.results[0]["out_0"]


PHASES = 8
```
